# Optimizing a Trainium2 kernel written in Bass

```python
import numpy as np
import jax
import jax.numpy as jnp

def _softmax(x, axis=-1):
    return jax.nn.softmax(x, axis=axis)

def _gelu(x):
    return jax.nn.gelu(x, approximate=True)

def _silu(x):
    return jax.nn.silu(x)

def _sigmoid(x):
    return jax.nn.sigmoid(x)

def _layernorm(x, axis=-1, eps=1e-05):
    m = jnp.mean(x, axis=axis, keepdims=True)
    v = jnp.var(x, axis=axis, keepdims=True)
    return (x - m) / jnp.sqrt(v + eps)

def _scatter_add(tgt, idx, src, axis=0):
    return tgt.at[idx].add(src)

def _segment_sum(src, seg, n):
    return jax.ops.segment_sum(src, seg, n)
kernel_name = 'mk_gnn_resnorm_d2_gnn_r8_7746ac'

def setup_inputs(seed: int=0):
    np.random.seed(seed)
    _w = jnp.asarray

    def _rec_inputs():
        import jax
        import jax.numpy as jnp
        _gk = jax.random.key(seed)
        x = -0.0002117 + 1 * jax.random.normal(jax.random.fold_in(_gk, 1), (12500, 256), jnp.float32)
        src = jax.random.randint(jax.random.fold_in(_gk, 2), (200000,), 0, 12500, jnp.int32)
        dst = jax.random.randint(jax.random.fold_in(_gk, 3), (200000,), 0, 12500, jnp.int32)
        _o = jnp.argsort(dst, stable=True)
        src = src[_o]
        dst = dst[_o]
        return (x, src, dst)
    x, src, dst = _rec_inputs()

    def _L0_gnn_setup():
        import jax, jax.numpy as jnp
        import numpy as np
        N, D_DIM, K, R = (12500, 256, 4, 16)
        E_RAND = 200000
        ETA, LAM, C = (0.5, 0.1, 0.5)
        key = jax.random.key(seed)
        k1, k2, k3, k4 = jax.random.split(key, 4)
        Z = jax.random.normal(k1, (N, D_DIM), jnp.float32)
        U = jax.random.normal(k2, (K, D_DIM, R), jnp.float32) / np.float32(np.sqrt(D_DIM))
        Dmat = jax.random.normal(k3, (D_DIM, D_DIM), jnp.float32) / np.float32(np.sqrt(D_DIM))
        head_w = jnp.ones((K,), jnp.float32) / K
        rnd = jax.random.randint(k4, (2, E_RAND), 0, N)
        loops = jnp.stack([jnp.arange(N), jnp.arange(N)])
        edge_index = jnp.concatenate([rnd, loops], axis=1)
        return {'Z': Z, 'U': U, 'Dmat': Dmat, 'head_w': head_w, 'edge_index': edge_index}
    _L0_gnn_all = _L0_gnn_setup()
    _L0_gnn_in = {k: v for k, v in _L0_gnn_all.items() if k in ('U', 'Dmat', 'head_w')}
    del _L0_gnn_all

    def _L1_gnn_setup():
        import jax, jax.numpy as jnp
        import numpy as np
        N, IN_CH, HEADS, OUT_CH, E = (6250, 256, 4, 64, 100000)
        key = jax.random.key(seed)
        k1, k2, k3, k4, k5 = jax.random.split(key, 5)
        x = jax.random.normal(k1, (N, IN_CH), dtype=jnp.float32)
        edge_index = jax.random.randint(k2, (2, E), 0, N, dtype=jnp.int64)
        bw = float(np.sqrt(6.0 / (IN_CH + HEADS * OUT_CH)))
        ba = float(np.sqrt(6.0 / (HEADS + OUT_CH)))
        weight = jax.random.uniform(k3, (IN_CH, HEADS * OUT_CH), jnp.float32, -bw, bw)
        attn_l = jax.random.uniform(k4, (HEADS, OUT_CH), jnp.float32, -ba, ba)
        attn_r = jax.random.uniform(k5, (HEADS, OUT_CH), jnp.float32, -ba, ba)
        return {'x': x, 'edge_index': edge_index, 'weight': weight, 'attn_l': attn_l, 'attn_r': attn_r}
    _L1_gnn_all = _L1_gnn_setup()
    _L1_gnn_in = {k: v for k, v in _L1_gnn_all.items() if k in ('weight', 'attn_l', 'attn_r')}
    del _L1_gnn_all
    return {'x': x, 'src': src, 'dst': dst, 'L0_gnn_U': _L0_gnn_in['U'], 'L0_gnn_Dmat': _L0_gnn_in['Dmat'], 'L0_gnn_head_w': _L0_gnn_in['head_w'], 'L1_gnn_weight': _L1_gnn_in['weight'], 'L1_gnn_attn_l': _L1_gnn_in['attn_l'], 'L1_gnn_attn_r': _L1_gnn_in['attn_r']}

def reference(x, src, dst, L0_gnn_U, L0_gnn_Dmat, L0_gnn_head_w, L1_gnn_weight, L1_gnn_attn_l, L1_gnn_attn_r):
    import jax
    import jax.numpy as jnp

    def _L0_gnn_ref(Z, U, Dmat, head_w, edge_index):
        import jax, jax.numpy as jnp
        import numpy as np
        N, D_DIM, K, R = (12500, 256, 4, 16)
        E_RAND = 200000
        ETA, LAM, C = (0.5, 0.1, 0.5)
        src, dst = (edge_index[0], edge_index[1])
        scale = np.float32(np.sqrt(R))
        ZU = jnp.einsum('nd,kdr->knr', Z, U)
        zs = ZU[:, src, :]
        zd = ZU[:, dst, :]
        logits = (zs * zd).sum(-1) / scale
        seg_max = jax.vmap(lambda l: jax.ops.segment_max(l, dst, num_segments=N))(logits)
        exp_l = jnp.exp(logits - seg_max[:, dst])
        seg_sum = jax.vmap(lambda e: jax.ops.segment_sum(e, dst, num_segments=N))(exp_l)
        alpha = exp_l / (seg_sum[:, dst] + 1e-16)
        weighted = alpha[..., None] * zs
        agg = jax.vmap(lambda w_: jax.ops.segment_sum(w_, dst, num_segments=N))(weighted)
        w = jax.nn.softmax(head_w)
        ssa = jnp.einsum('k,knr,kdr->nd', w, agg, U)
        Z_half = (1.0 - C) * Z + C * ssa
        DZ = Z_half @ Dmat.T
        residual = Z_half - DZ @ Dmat
        grad_step = Z_half + ETA * (residual @ Dmat)
        return jax.nn.relu(grad_step - ETA * LAM)

    def _L1_gnn_ref(x, edge_index, weight, attn_l, attn_r):
        import jax, jax.numpy as jnp
        import numpy as np
        N, IN_CH, HEADS, OUT_CH, E = (6250, 256, 4, 64, 100000)
        heads, out_ch = attn_l.shape
        n = x.shape[0]
        xt = jnp.matmul(x, weight).reshape(-1, heads, out_ch)
        row, col = (edge_index[0], edge_index[1])
        alpha_l = jnp.einsum('ehd,hd->eh', xt[row], attn_l)
        alpha_r = jnp.einsum('ehd,hd->eh', xt[col], attn_r)
        alpha = jax.nn.softmax(jax.nn.leaky_relu(alpha_l + alpha_r, 0.01), axis=1)
        tmp = jnp.einsum('nh,nhd->nd', alpha[:n], xt[col[:n]])
        out = jnp.broadcast_to(tmp[:, None, :], (n, heads, out_ch))
        return out.reshape(n, heads * out_ch)
    edge_index = jnp.stack([src, dst])
    x = _layernorm(x + _L0_gnn_ref(x, L0_gnn_U, L0_gnn_Dmat, L0_gnn_head_w, edge_index), axis=-1)
    x = _layernorm(x + _L1_gnn_ref(x, edge_index, L1_gnn_weight, L1_gnn_attn_l, L1_gnn_attn_r), axis=-1)
    return x

_drawn_inputs = setup_inputs


def setup_inputs(seed=0):
    import zlib

    import numpy as np

    out = dict(_drawn_inputs(seed))
    spreads = {'L0_gnn_head_w': (0.25, 0.6)}
    factors = {'L0_gnn_U': 2.913}
    for name, (base, spread) in spreads.items():
        noise = np.random.default_rng([zlib.crc32(name.encode()), seed]).standard_normal(out[name].shape)
        drawn = base * np.exp(spread * noise) if base else spread * noise
        out[name] = jnp.asarray(drawn.astype(out[name].dtype))
    for name, factor in factors.items():
        out[name] = (out[name] * factor).astype(out[name].dtype)
    return out
```

```python
from contextlib import ExitStack

import numpy as np
import concourse.bass as bass
from concourse import mybir
from concourse.alu_op_type import AluOpType as ALU

F32 = mybir.dt.float32
I32 = mybir.dt.int32
ACT = mybir.ActivationFunctionType
AX_X = mybir.AxisListType.X

P = 128
N = 12500
E = 200000
D = 256
DC = D // P
K, R = 4, 16
KR = K * R
H, O = 4, 64
HO = H * O
NT = -(-N // P)
ET = -(-E // P)
LASTN = N - (NT - 1) * P
B = 32
S = -(-(ET + NT) // P) * P
SG = S // P
NB = S // B
G = 8
NG = B // G
TR = 4
AW = KR + K
XW = HO + H
WW = XW + H
NEG = -1e30
PAD = P * (NT + 2)
ETA, LAM, EPS = 0.5, 0.1, 1e-5
T7 = 7
NG7 = NT // T7
DENSE_FIRST = 3
assert NT % (2 * T7) == 0 and S % (2 * B) == 0 and ET + NT <= S and E % P in (0, 64)


def spread(ap, axis, n):
    shape = list(ap.shape)
    shape[axis] = n
    return ap.broadcast_to(shape)


class Count:

    def __init__(self):
        self.base, self.n, self.i, self.per = 0, 0, None, 0

    def loop(self, i, per):
        self.base, self.n, self.i, self.per = self.base + self.n, 0, i, per

    def end(self, trips):
        assert self.n == self.per, (self.n, self.per)
        self.base, self.n, self.i, self.per = self.base + self.per * trips, 0, None, 0

    def next(self):
        self.n += 1
        return self.base + self.n + (self.i * self.per if self.i is not None else 0)


def program(nc, x, src, dst, u, dmat, head_w, weight, attn_l, attn_r, out):
    ctx = ExitStack()
    with ctx:
        def sb(name, shape, dt=F32):
            return ctx.enter_context(nc.sbuf_tensor(name, shape, dt))

        def sem(name):
            return ctx.enter_context(nc.semaphore(name))

        dst_rows = nc.dram_tensor("dst_rows", (S, P), I32).ap()
        src_rows = nc.dram_tensor("src_rows", (S, P), I32).ap()
        reset_rows = nc.dram_tensor("reset_rows", (S, P), F32).ap()
        z_table = nc.dram_tensor("z_table", (NT * P, KR), F32).ap()
        xT_store = nc.dram_tensor("xT_store", (NT, P, D), F32).ap()
        xt_table = nc.dram_tensor("xt_table", (NT * P, XW), F32).ap()
        al_table = nc.dram_tensor("al_table", (NT * P, H), F32).ap()

        arena = sb("arena", [P, NT * D])
        at = [0]

        def part(width):
            a = arena[:, at[0]:at[0] + width]
            at[0] += width
            assert at[0] <= NT * D
            return a

        z_sb = part((NT + 1) * KR).rearrange("p (t c) -> p t c", c=KR)
        onehot = part(2 * B * P).rearrange("p (h j n) -> p h j n", h=2, j=B)
        onehotT = part(2 * G * P).rearrange("p (j e) -> p j e", j=2 * G)
        zs = part(2 * B * AW).rearrange("p (h j c) -> p h j c", h=2, j=B)
        prod = part(G * KR).rearrange("p (j c) -> p j c", j=G)
        fwd0 = part(P)
        fwd = part(P)
        rev0 = part(P)
        rev = part(P)
        xexp = part(P)
        eexp = part(P)
        resets = part(2 * (P + 1)).rearrange("p (h e) -> p h e", h=2)
        logits = part(2 * P).rearrange("p (h q) -> p h q", h=2)
        dslot = part(S)
        shift = part(P)
        corner = part(P)
        x1 = arena[:, :].rearrange("p (t d) -> p t d", d=D)
        oflat = onehot.rearrange("p h j n -> p (h j n)")
        diag = oflat[:, 0:S]
        ulast = oflat[:, S:2 * S]
        junk = oflat[:, 2 * S:3 * S]
        dloc = oflat[:, 3 * S:4 * S].rearrange("p (g e) -> p g e", e=P)
        cont = diag.rearrange("p (g e) -> p g e", e=P)
        okrow = ulast.rearrange("p (g e) -> p g e", e=P)
        srcf = junk.rearrange("p (g e) -> p g e", e=P)

        acc = sb("acc", [P, NT + 1, AW])
        xto = sb("xto", [P, 2, T7, WW])
        xto_flat = xto[:, :, :, :].rearrange("p h t c -> p (h t c)")
        dst_sb = xto_flat[:, 0:S].bitcast(I32).rearrange("p (g e) -> p g e", e=P)
        src_sb = xto_flat[:, S:2 * S].bitcast(I32).rearrange("p (g e) -> p g e", e=P)
        zs_flat = zs.rearrange("p h j c -> p (h j c)")
        dst_step = zs_flat[:, 0:S].bitcast(I32).rearrange("p (g e) -> p g e", e=P)
        src_step = zs_flat[:, S:2 * S].bitcast(I32).rearrange("p (g e) -> p g e", e=P)
        sslot = sb("sslot", [P, S], I32)
        trow = sb("trow", [1, S], I32)
        src1 = sb("src1", [P, P], I32)
        dst1 = sb("dst1", [P, P], I32)
        didx = sb("didx", [P, 2, B])
        sidx = sb("sidx", [P, 2, B], I32)
        ident = sb("ident", [P, P])
        ones = sb("ones", [P, P])
        iota_row = sb("iota_row", [P, P])
        iota_i = sb("iota_i", [P, P], I32)
        stepno_i = sb("stepno_i", [P, SG], I32)
        stepno = sb("stepno", [P, SG])
        pno = sb("pno", [P, 3])
        lastt_i = sb("lastt_i", [P, SG], I32)
        lastt = sb("lastt", [P, SG])
        istep = sb("istep", [P, SG])
        istep_i = sb("istep_i", [P, SG], I32)
        tstep = sb("tstep", [P, SG])
        tneg = sb("tneg", [P, SG])
        plast = sb("plast", [P, SG])
        rows = sb("rows", [1, 3, P])
        rmin = sb("rmin", [1, P])
        rnext = sb("rnext", [1, P])
        carry = sb("carry", [1, P + K])
        back = sb("back", [1, P])
        backx = sb("backx", [1, P])
        ratio = sb("ratio", [1, 2, K])
        corr = sb("corr", [1, AW])
        inmin = sb("inmin", [P, 1])
        ccol = sb("ccol", [P, 1])
        dcol = sb("dcol", [P, 1])
        first_col = sb("first_col", [P, 2])
        xin = sb("xin", [P, 2, T7, D])
        xTb = sb("xTb", [P, 2, T7, D])
        dm = sb("dm", [P, DC, D])
        ur = sb("ur", [P, DC, K, R])
        wx = sb("wx", [P, DC, WW])
        attn = sb("attn", [1, 2 * HO])
        hw = sb("hw", [1, 3, K])
        hsum = sb("hsum", [1, 3])
        gs = sb("gs", [P, DC, D])
        mz = sb("mz", [P, DC, D])
        w3 = sb("w3", [KR, D])
        wtmp = gs
        rec = sb("rec", [P, 2, T7, K])
        agn = sb("agn", [P, 2, T7, KR])
        lastcol = sb("lastcol", [P, SG + 1])
        aT = sb("aT", [KR, 2, P])
        stats = sb("stats", [P, T7, 6])
        mv = sb("mv", [P, 2, T7, 2])
        rstd = sb("rstd", [P, 2, T7, 3])
        x1T = sb("x1T", [P, 2, D])
        algat = sb("algat", [P, 2, T7, H])
        lg = sb("lg", [P, 2, T7, H])
        lmax = sb("lmax", [P, T7, 2])
        tmp = agn[:, 0, :, :]
        eps_t = sb("eps_t", [P, 2])

        psum = [ctx.enter_context(nc.psum_tensor(f"bank{i}", [P, 512], F32)) for i in range(8)]
        acc_ps = psum[0:2]
        tr_ps = psum[2:4]
        zd_ps = psum[4:6]
        mid_ps, row_ps = psum[6], psum[7]

        edges_in, u_in, weights_in = sem("edges_in"), sem("u_in"), sem("weights_in")
        rows_out, resets_out = sem("rows_out"), sem("resets_out")
        x_in = [sem(f"x_in{i}") for i in range(2)]
        xT_out = [sem(f"xT_out{i}") for i in range(2)]
        z_out = sem("z_out")
        iotas, consts = sem("iotas"), sem("consts")
        v_step = sem("v_step")
        pads_set, diag_ready, bcast_ready, walk_ready = sem("pads_set"), sem("diag_ready"), sem("bcast_ready"), sem("walk_ready")
        tiles_gathered = sem("tiles_gathered")
        dloc_ready, plast_ready, reset_ready = sem("dloc_ready"), sem("plast_ready"), sem("reset_ready")
        tab_ps, tab_read = sem("tab_ps"), sem("tab_read")
        xt_ps, xt_copied, zu_ps, zu_copied = sem("xt_ps"), sem("xt_copied"), sem("zu_ps"), sem("zu_copied")
        prep_ps, prep_read, prep_exp = sem("prep_ps"), sem("prep_read"), sem("prep_exp")
        idx_ready = sem("idx_ready")
        gathered = [[sem(f"gathered{h}{g}") for g in range(NG)] for h in range(2)]
        onehot_ready, oneT_ps, oneT_ready = sem("onehot_ready"), sem("oneT_ps"), sem("oneT_ready")
        zd_ready, zd_used = sem("zd_ready"), sem("zd_used")
        logits_ready, lt_ready = sem("logits_ready"), sem("lt_ready")
        ends_ready, ends_row = sem("ends_ready"), sem("ends_row")
        carry_ready, carry_col = sem("carry_ready"), sem("carry_col")
        heads_ready, heads_row = sem("heads_ready"), sem("heads_row")
        back_ready, back_col = sem("back_ready"), sem("back_col")
        x_ready, e_ready, ratio_ready, et_ready = sem("x_ready"), sem("e_ready"), sem("ratio_ready"), sem("et_ready")
        accrow_ready, corr_ready = sem("accrow_ready"), sem("corr_ready")
        weights_ready, agg_done, acc_ready = sem("weights_ready"), sem("agg_done"), sem("acc_ready")
        resets_in = [sem(f"resets_in{h}") for h in range(2)]
        xT_in = [sem(f"xT_in{i}") for i in range(2)]
        x2_in = [sem(f"x2_in{i}") for i in range(2)]
        rec_ready, agn_ready, aT_ps, aT_ready, y_ps, relu_done, y_added = (
            sem("rec_ready"), sem("agn_ready"), sem("aT_ps"), sem("aT_ready"), sem("y_ps"), sem("relu_done"), sem("y_added"))
        var_ready, ln_done, rstd_ready, nb_ready, x1_ready, x1_kept = (
            sem("var_ready"), sem("ln_done"), sem("rstd_ready"), sem("nb_ready"), sem("x1_ready"), sem("x1_kept"))
        x1T_ps, x1T_ready, xt1_ps, xt1_copied = sem("x1T_ps"), sem("x1T_ready"), sem("xt1_ps"), sem("xt1_copied")
        table_out = [sem(f"table_out{i}") for i in range(2)]
        al_in = [sem(f"al_in{i}") for i in range(2)]
        xg_in = [sem(f"xg_in{i}") for i in range(2)]
        lg_ready, lg_exp, xg_used = sem("lg_ready"), sem("lg_exp"), sem("xg_used")
        var2_ready, ln2_done, rstd2_ready, nb2_ready, out_ready = (
            sem("var2_ready"), sem("ln2_done"), sem("rstd2_ready"), sem("nb2_ready"), sem("out_ready"))
        out_sent = [sem(f"out_sent{i}") for i in range(2)]

        FULL = E // P
        HALF = E - FULL * P
        G12 = (SG - 1) * P

        def rows_of(table, t, n):
            return table[bass.ds(t * P, n * P), :].rearrange("(t p) c -> p t c", p=P)

        block = ctx.enter_context(nc.Block())

        @block.sync
        def _(sp):
            sp.wait_ge(pads_set, 1)
            for e, tile in ((dst, dst_sb), (src, src_sb)):
                sp.dma_start(tile[:, 0:SG - 1, :], e[0:G12 * P].rearrange("(g p e) -> p g e", p=P, e=P)).then_inc(edges_in, 16)
                sp.dma_start(tile[0:FULL - G12, SG - 1, :], e[G12 * P:FULL * P].rearrange("(p e) -> p e", e=P)).then_inc(edges_in, 16)
                sp.dma_start(tile[FULL - G12:FULL - G12 + 1, SG - 1, 0:HALF], e[FULL * P:E].rearrange("(p e) -> p e", p=1)).then_inc(edges_in, 16)
            for c in range(DC):
                sp.dma_start(ur[:, c, :, :], u[:, c * P:(c + 1) * P, :].rearrange("k p r -> p k r")).then_inc(u_in, 16)
            def load_x(buf, g, signal):
                if type(g) is int and g == NG7 - 1:
                    sp.dma_start(xin[:, buf, 0:T7 - 1, :], rows_of(x, g * T7, T7 - 1)).then_inc(signal[buf], 16)
                    sp.dma_start(xin[0:LASTN, buf, T7 - 1, :], x[N - LASTN:N, :]).then_inc(signal[buf], 16)
                else:
                    sp.dma_start(xin[:, buf, :, :], rows_of(x, g * T7, T7)).then_inc(signal[buf], 16)
            load_x(0, 0, x_in)
            load_x(1, 1, x_in)
            sp.wait_ge(edges_in, 96)
            sp.dma_start(dst_rows.rearrange("(g p) e -> p g e", p=P), dst_sb[:, :, :]).then_inc(rows_out, 16)
            sp.dma_start(src_rows.rearrange("(g p) e -> p g e", p=P), src_sb[:, :, :]).then_inc(rows_out, 16)
            sp.dma_start(dm[:, :, :], dmat.rearrange("(c p) d -> p c d", p=P)).then_inc(weights_in, 16)
            sp.dma_start(wx[:, :, 0:HO], weight.rearrange("(c p) d -> p c d", p=P)).then_inc(weights_in, 16)
            sp.dma_start(attn[0:1, 0:HO], attn_r.rearrange("(a h) o -> a (h o)", a=1)).then_inc(weights_in, 16)
            sp.dma_start(attn[0:1, HO:2 * HO], attn_l.rearrange("(a h) o -> a (h o)", a=1)).then_inc(weights_in, 16)
            sp.dma_start(hw[0:1, 0, :], head_w.rearrange("(a h) -> a h", a=1)).then_inc(weights_in, 16)

            def dense_out(i, h):
                g = 2 * i + h
                sp.wait_ge(zu_copied, g + 1)
                sp.dma_start(rows_of(z_table, g * T7, T7), z_sb[:, bass.ds(g * T7, T7), :]).then_inc(z_out, 16)
                sp.dma_start(xT_store[bass.ds(g * T7, T7), :, :].rearrange("t p d -> p t d"), xTb[:, h, :, :]).then_inc(xT_out[h], 16)
            with nc.sync.Fori(0, NG7 // 2 - 2) as i:
                for h in range(2):
                    dense_out(i, h)
                    load_x(h, 2 * i + h + 2, x_in)
            for h in range(2):
                dense_out(NG7 // 2 - 2, h)
                load_x(h, NG7 - 2 + h, x_in)
            for h in range(2):
                dense_out(NG7 // 2 - 1, h)
            sp.wait_ge(reset_ready, 1)
            sp.dma_start(reset_rows.rearrange("(g p) e -> p g e", p=P), cont[:, :, :]).then_inc(resets_out, 16)
            sp.wait_ge(resets_out, 16)

            def load_resets(b, h):
                sp.dma_start(resets[:, h, 0:P], spread(reset_rows[bass.ds(b * B, B), :].rearrange("j (a e) -> j a e", a=1), 1, K)
                             ).then_inc(resets_in[h], 16)
            for b in range(2):
                load_resets(b, b)
            with nc.sync.Fori(1, NB // 2) as i:
                for h in range(2):
                    sp.wait_ge(x_ready, 2 * i + h - 1)
                    load_resets(2 * i + h, h)
            def load_xT(g, h):
                sp.dma_start(xTb[:, h, :, :], xT_store[bass.ds(g * T7, T7), :, :].rearrange("t p d -> p t d")).then_inc(xT_in[h], 16)

            def stage_loads(j, h, more_xT, more_x):
                if more_xT:
                    sp.wait_ge(x1T_ps, j * T7)
                    sp.wait_ge(x1_kept, j)
                    load_xT(j + 1, 1 - h)
                sp.wait_ge(xt1_copied, j * T7)
                sp.dma_start(rows_of(xt_table, (j - 1) * T7, T7), xto[:, 1 - h, :, 0:XW]).then_inc(table_out[1 - h], 16)
                sp.dma_start(rows_of(al_table, (j - 1) * T7, T7), xto[:, 1 - h, :, XW:WW]).then_inc(table_out[1 - h], 16)
                if more_x:
                    sp.wait_ge(y_added, (j + 1) * T7)
                    load_x(h, j + 2, x2_in)
            for h in range(2):
                sp.wait_ge(xT_out[h], 16 * (NG7 // 2))
            for h in range(2):
                load_xT(h, h)
                load_x(h, h, x2_in)
            sp.wait_ge(y_added, T7)
            load_x(0, 2, x2_in)
            stage_loads(1, 1, True, True)
            with nc.sync.Fori(1, NG7 // 2 - 2) as i:
                stage_loads(2 * i, 0, True, True)
                stage_loads(2 * i + 1, 1, True, True)
            stage_loads(NG7 - 4, 0, True, True)
            stage_loads(NG7 - 3, 1, True, True)
            stage_loads(NG7 - 2, 0, True, False)
            stage_loads(NG7 - 1, 1, False, False)
            stage_loads(NG7, 0, False, False)
            with nc.sync.Fori(0, NG7 // 2 - 1) as i:
                for h in range(2):
                    g = 2 * i + h
                    sp.wait_ge(out_ready, g + 1)
                    sp.dma_start(rows_of(out, g * T7, T7), x1[:, bass.ds(g * T7, T7), :]).then_inc(out_sent[h], 16)
            sp.wait_ge(out_ready, NG7 - 1)
            g = NG7 - 2
            sp.dma_start(rows_of(out, g * T7, T7), x1[:, bass.ds(g * T7, T7), :]).then_inc(out_sent[0], 16)
            sp.wait_ge(out_ready, NG7)
            g = NG7 - 1
            sp.dma_start(rows_of(out, g * T7, T7 - 1), x1[:, g * T7:NT - 1, :]).then_inc(out_sent[1], 16)
            sp.dma_start(out[N - LASTN:N, :], x1[0:LASTN, NT - 1, :]).then_inc(out_sent[1], 16)
            sp.wait_ge(out_sent[0], 16 * (NG7 // 2))
            sp.wait_ge(out_sent[1], 16 * (NG7 // 2 + 1))
            sp.wait_ge(z_out, 16 * NG7)

        @block.gpsimd
        def _(pool):
            nc.gpsimd.iota(iota_i[:, :], [[1, P]], base=0, channel_multiplier=0).then_inc(iotas, 1)
            nc.gpsimd.iota(stepno_i[:, :], [[P, SG]], base=0, channel_multiplier=1).then_inc(iotas, 1)
            pool.wait_ge(walk_ready, 1)
            pool.wait_ge(rows_out, 32)
            for table, tile in ((dst_rows, dst_step), (src_rows, src_step)):
                for g in range(SG):
                    pool.indirect_dma_start(tile[:, g, :], None, table,
                                            bass.IndirectOffsetOnAxis(ap=istep_i[:, g:g + 1], axis=0)).then_inc(tiles_gathered, 16)
            pool.wait_ge(z_out, 16 * NG7)

            def gather_block(h, free):
                for g in range(NG):
                    if free is not None:
                        pool.wait_ge(agg_done, free + G * (g + 1))
                        nc.gpsimd.nop(nofuse=True)
                    for j in range(g * G, (g + 1) * G):
                        pool.indirect_dma_start(zs[:, h, j, 0:KR], None, z_table,
                                                bass.IndirectOffsetOnAxis(ap=sidx[:, h, j:j + 1], axis=0)).then_inc(gathered[h][g], 16)
            for b in range(2):
                pool.wait_ge(idx_ready, b + 1)
                gather_block(b, None)
            with nc.gpsimd.Fori(1, NB // 2) as i:
                for h in range(2):
                    pool.wait_ge(idx_ready, 2 * i + h + 1)
                    nc.gpsimd.nop(nofuse=True)
                    gather_block(h, (2 * i + h - 2) * B)
            def normalise_sums(g, h):
                nc.gpsimd.tensor_tensor(agn[:, h, :, :].rearrange("p t (k r) -> p t k r", r=R),
                                        acc[:, bass.ds(g * T7, T7), 0:KR].rearrange("p t (k r) -> p t k r", r=R),
                                        spread(rec[:, h, :, :].rearrange("p t (k a) -> p t k a", a=1), 3, R), ALU.mult).then_inc(agn_ready, 1)

            def keep_rows(g, h):
                pool.wait_ge(x1_ready, (g + 1) * T7)
                nc.gpsimd.tensor_copy(x1[:, bass.ds(g * T7, T7), :], xTb[:, h, :, :]).then_inc(x1_kept, 1)

            for g in range(2):
                pool.wait_ge(rec_ready, g + 1)
                normalise_sums(g, g)
            with nc.gpsimd.Fori(0, NG7 // 2 - 1) as i:
                for h in range(2):
                    g = 2 * i + h
                    keep_rows(g, h)
                    pool.wait_ge(aT_ps, (g + 1) * T7)
                    pool.wait_ge(rec_ready, g + 3)
                    normalise_sums(g + 2, h)
            for h in range(2):
                keep_rows(NG7 - 2 + h, h)
            for h in range(2):
                pool.wait_ge(table_out[h], 32 * (NG7 // 2))
            for g in range(NG7):
                h = g % 2
                if g >= 2:
                    pool.wait_ge(xg_used, g - 1)
                for t in range(T7):
                    n = g * T7 + t
                    pool.indirect_dma_start(algat[:, h, t, :], None, al_table,
                                            bass.IndirectOffsetOnAxis(ap=src1[:, n:n + 1], axis=0)).then_inc(al_in[h], 16)
                    pool.indirect_dma_start(xto[:, h, t, 0:XW], None, xt_table,
                                            bass.IndirectOffsetOnAxis(ap=dst1[:, n:n + 1], axis=0)).then_inc(xg_in[h], 16)

        @block.vector
        def _(dve):
            vn = Count()
            V = nc.vector
            V.memset(dst_sb[:, SG - 1, :], PAD)
            V.memset(src_sb[:, SG - 1, :], 0).then_inc(pads_set, 1)
            V.memset(ones[:, :], 1.0).then_inc(v_step, 1)
            vn.next()
            V.memset(eps_t[:, 0:1], EPS)
            V.memset(eps_t[:, 1:2], -ETA * LAM)
            V.memset(resets[:, :, P:P + 1], 0.0)
            V.memset(rnext[0:1, P - K:P], 0.0)
            V.memset(backx[0:1, P - K:P], NEG)
            V.memset(z_sb[:, NT, :], 0.0)
            V.memset(carry[0:1, P:P + K], NEG).then_inc(v_step, 1)
            vn.next()
            V.memset(acc[:, :, :], 0.0).then_inc(acc_ready, 1)
            dve.wait_ge(iotas, 2)
            V.tensor_copy(iota_row[:, :], iota_i[:, :]).then_inc(v_step, 1)
            dve.wait_ge(v_step, vn.next())
            V.tensor_copy(stepno[:, :], stepno_i[:, :]).then_inc(v_step, 1)
            dve.wait_ge(v_step, vn.next())
            V.tensor_copy(pno[:, 0:1], stepno[:, 0:1])
            V.tensor_scalar(pno[:, 1:2], stepno[:, 0:1], 1.0, None, ALU.add)
            V.tensor_scalar(pno[:, 2:3], stepno[:, 0:1], float(P - 1), None, ALU.subtract).then_inc(v_step, 1)
            dve.wait_ge(v_step, vn.next())
            V.tensor_scalar(ident[:, :], iota_row[:, :], pno[:, 0:1], None, ALU.is_equal)
            V.tensor_scalar(shift[:, :], iota_row[:, :], pno[:, 1:2], None, ALU.is_equal)
            V.tensor_scalar(corner[:, :], iota_row[:, :], pno[:, 2:3], None, ALU.is_equal).then_inc(consts, 1)
            dve.wait_ge(consts, 1)

            dve.wait_ge(edges_in, 96)
            V.tensor_scalar(lastt_i[:, :], dst_sb[:, :, P - 1], 7, None, ALU.arith_shift_right).then_inc(v_step, 1)
            dve.wait_ge(v_step, vn.next())
            V.tensor_tensor(lastt[:, :], lastt_i[:, :], stepno[:, :], ALU.add).then_inc(v_step, 1)
            dve.wait_ge(v_step, vn.next())
            for g in range(SG):
                last = V.tensor_scalar(diag[:, g * P:(g + 1) * P], ident[:, :], lastt[:, g:g + 1], None, ALU.mult)
            last.then_inc(diag_ready, 1)
            for g in range(0, SG, 4):
                n = min(4, SG - g) * P
                dve.wait_ge(bcast_ready, g // 4 + 1)
                last = V.tensor_copy(ulast[:, g * P:g * P + n], psum[4 + g // 4][:, 0:n])
            last.then_inc(v_step, 1)
            dve.wait_ge(v_step, vn.next())
            for g in range(SG):
                V.tensor_scalar(junk[:, :], ulast[:, :], stepno[:, g:g + 1], 0.0, ALU.is_lt, ALU.add,
                                accum_out=istep[:, g:g + 1]).then_inc(v_step, 1)
                dve.wait_ge(v_step, vn.next())
            V.tensor_copy(istep_i[:, :], istep[:, :]).then_inc(walk_ready, 1)
            V.tensor_tensor(tstep[:, :], stepno[:, :], istep[:, :], ALU.subtract).then_inc(v_step, 1)
            dve.wait_ge(v_step, vn.next())
            V.tensor_scalar(tstep[:, :], tstep[:, :], float(NT), None, ALU.min).then_inc(v_step, 1)
            dve.wait_ge(v_step, vn.next())
            V.tensor_scalar(tneg[:, :], tstep[:, :], -float(P), None, ALU.mult).then_inc(v_step, 1)
            dve.wait_ge(v_step, vn.next())
            dve.wait_ge(tiles_gathered, 32 * SG)
            for g in range(SG):
                last = V.tensor_scalar(dloc[:, g, :], dst_step[:, g, :], tneg[:, g:g + 1], None, ALU.add)
            last.then_inc(v_step, 1)
            dve.wait_ge(v_step, vn.next())
            V.memset(lastcol[:, 0:1], 0.0)
            V.tensor_copy(lastcol[:, 1:SG + 1], dloc[:, :, P - 1]).then_inc(dloc_ready, 1)
            V.tensor_copy(srcf[:, :, :], src_step[:, :, :]).then_inc(dloc_ready, 1)
            dve.wait_ge(dloc_ready, 2)
            V.tensor_scalar(okrow[:, :, :], dloc[:, :, :], 0.0, None, ALU.is_ge).then_inc(v_step, 1)
            dve.wait_ge(v_step, vn.next())
            V.scalar_tensor_tensor(okrow[:, :, :], dloc[:, :, :], float(P - 1), okrow[:, :, :], ALU.is_le, ALU.mult).then_inc(v_step, 1)
            dve.wait_ge(v_step, vn.next())
            dve.wait_ge(plast_ready, 1)
            V.tensor_copy(plast[:, :], psum[7][:, 0:SG]).then_inc(tab_read, 1)
            dve.wait_ge(tab_read, 1)
            V.tensor_tensor(cont[:, :, 1:P], dloc[:, :, 1:P], dloc[:, :, 0:P - 1], ALU.is_equal)
            V.tensor_tensor(cont[:, :, 0], dloc[:, :, 0], plast[:, :], ALU.is_equal).then_inc(v_step, 1)
            dve.wait_ge(v_step, vn.next())
            V.tensor_tensor(cont[:, :, :], cont[:, :, :], okrow[:, :, :], ALU.mult).then_inc(v_step, 1)
            dve.wait_ge(v_step, vn.next())
            V.tensor_scalar(cont[:, :, :], cont[:, :, :], 1.0, -NEG, ALU.subtract, ALU.mult).then_inc(reset_ready, 1)
            for n, table in enumerate((dslot, sslot, trow)):
                dve.wait_ge(tab_ps, n + 1)
                w = 1 if table is trow else P
                for g in range(0, SG, 4):
                    m = min(4, SG - g) * P
                    last = V.tensor_copy(table[0:w, g * P:g * P + m], psum[4 + g // 4][0:w, 0:m])
                last.then_inc(tab_read, 1)
            dve.wait_ge(tab_read, 4)
            for b in range(2):
                V.tensor_copy(sidx[:, b, :], sslot[:, b * B:(b + 1) * B]).then_inc(idx_ready, 1)
            V.tensor_copy(okrow[:, 0, :], dst_sb[:, 0, :])
            V.tensor_copy(okrow[:, 1, :], src_sb[:, 0, :]).then_inc(tab_read, 1)
            dve.wait_ge(tab_ps, 4)
            V.tensor_copy(dst1[:, :], psum[4][:, 0:P])
            V.tensor_copy(src1[:, :], psum[4][:, P:2 * P]).then_inc(tab_read, 1)

            dve.wait_ge(weights_in, 16 * 5)
            V.tensor_reduce(hsum[0:1, 0:1], hw[0:1, 0, :], AX_X, ALU.max).then_inc(v_step, 1)
            dve.wait_ge(v_step, vn.next())
            V.tensor_scalar(hw[0:1, 1, :], hw[0:1, 0, :], hsum[0:1, 0:1], None, ALU.subtract).then_inc(prep_read, 1)
            dve.wait_ge(prep_exp, 1)
            V.tensor_reduce(hsum[0:1, 1:2], hw[0:1, 2, :], AX_X, ALU.add).then_inc(v_step, 1)
            dve.wait_ge(v_step, vn.next())
            V.reciprocal(hsum[0:1, 2:3], hsum[0:1, 1:2]).then_inc(v_step, 1)
            dve.wait_ge(v_step, vn.next())
            V.tensor_scalar(hw[0:1, 1, :], hw[0:1, 2, :], hsum[0:1, 2:3], None, ALU.mult).then_inc(prep_read, 1)
            dve.wait_ge(prep_ps, 1)
            dve.wait_ge(zu_copied, NG7)
            V.tensor_copy(gs[:, :, :].rearrange("p c d -> p (c d)"), psum[4][:, :]).then_inc(prep_read, 1)
            V.tensor_tensor(ur[:, :, :, :].rearrange("p c k r -> p k c r"), ur[:, :, :, :].rearrange("p c k r -> p k c r"),
                            spread(spread(psum[5][:, 0:K].rearrange("p (k a b) -> p k a b", a=1, b=1), 2, DC), 3, R), ALU.mult).then_inc(prep_read, 1)
            dve.wait_ge(prep_ps, 2)
            V.tensor_tensor(mz[:, :, :].rearrange("p c d -> p (c d)"), dm[:, :, :].rearrange("p c d -> p (c d)"), psum[6][:, :], ALU.subtract).then_inc(v_step, 1)
            dve.wait_ge(v_step, vn.next())
            V.tensor_scalar(mz[:, :, :], mz[:, :, :], 0.5 * ETA, None, ALU.mult).then_inc(v_step, 1)
            dve.wait_ge(v_step, vn.next())
            for c in range(DC):
                blk = mz[:, c, c * P:(c + 1) * P]
                last = V.scalar_tensor_tensor(blk, ident[:, :], 0.5, blk, ALU.mult, ALU.add)
            last.then_inc(prep_read, 1)
            wv = wx[:, :, 0:HO].rearrange("p c (h o) -> p c h o", h=H)
            for n in range(2):
                V.tensor_tensor(wtmp[:, :, :].rearrange("p c (h o) -> p c h o", h=H), wv,
                                spread(psum[7][:, n * HO:(n + 1) * HO].rearrange("p (a h o) -> p a h o", a=1, h=H), 1, DC),
                                ALU.mult).then_inc(v_step, 1)
                dve.wait_ge(v_step, vn.next())
                V.tensor_reduce(wx[:, :, HO + n * H:HO + (n + 1) * H], wtmp[:, :, :].rearrange("p c (h o) -> p c h o", h=H),
                                AX_X, ALU.add).then_inc(v_step, 1)
                dve.wait_ge(v_step, vn.next())
            dve.wait_ge(prep_ps, 3)
            V.tensor_copy(w3[:, :], psum[4][0:KR, 0:D]).then_inc(prep_read, 1)
            dve.wait_ge(tab_read, 6)
            dve.wait_ge(resets_out, 16)
            dve.wait_ge(prep_read, 6)

            def copy_indices(b, h):
                V.tensor_copy(didx[:, h, :], dslot[:, bass.ds(b * B, B)]).then_inc(v_step, 1)
                dve.wait_ge(v_step, vn.next())

            def make_onehot(b, h, g, free):
                if free is not None:
                    dve.wait_ge(agg_done, free + G * (g + 1))
                for j in range(g * G, (g + 1) * G):
                    last = V.tensor_scalar(onehot[:, h, j, :], iota_row[:, :], didx[:, h, j:j + 1], None, ALU.is_equal)
                last.then_inc(onehot_ready, 1)

            def copy_transposed(b, h, m, first):
                if m >= 4 or not first:
                    dve.wait_ge(zd_ready, NG * b + (m - 4) // 2 + 1)
                dve.wait_ge(oneT_ps, 8 * b + m + 1)
                j = (TR * m) % (2 * G)
                if m == 0:
                    V.tensor_copy(first_col[:, h:h + 1], tr_ps[m % 2][:, 0:1])
                V.tensor_copy(onehotT[:, j:j + TR, :].rearrange("p j e -> p (j e)"), tr_ps[m % 2][:, :]).then_inc(oneT_ready, 1)

            def head_products(b, h, g, uses):
                dve.wait_ge(zd_ready, NG * b + g + 1)
                dve.wait_ge(gathered[h][g], 16 * G * uses)
                V.tensor_tensor(prod[:, :, :], zs[:, h, g * G:(g + 1) * G, 0:KR],
                                zd_ps[g % 2][:, :].rearrange("p (j c) -> p j c", j=G), ALU.mult).then_inc(zd_used, 1)
                dve.wait_ge(zd_used, NG * b + g + 1)
                last = V.tensor_reduce(logits[:, h, g * G * K:(g + 1) * G * K], prod[:, :, :].rearrange("p j (k r) -> p (j k) r", r=R),
                                       AX_X, ALU.add)
                if g == NG - 1:
                    last.then_inc(logits_ready, 1)
                else:
                    last.then_inc(v_step, 1)
                    dve.wait_ge(v_step, vn.next())

            def copy_next_indices(b, h):
                V.tensor_copy(sidx[:, h, :], sslot[:, bass.ds(b * B, B)]).then_inc(idx_ready, 1)

            def front(b, h, free, uses, first, more):
                copy_indices(b, h)
                make_onehot(b, h, 0, free)
                make_onehot(b, h, 1, free)
                for g in range(NG):
                    copy_transposed(b, h, 2 * g, first)
                    copy_transposed(b, h, 2 * g + 1, first)
                    if g >= 1:
                        head_products(b, h, g - 1, uses)
                    if g + 2 < NG:
                        make_onehot(b, h, g + 2, free)
                head_products(b, h, NG - 1, uses)
                if more:
                    copy_next_indices(b + 2, h)

            def by_head(row, k):
                return row.rearrange("a (j k) -> a j k", k=K)[:, :, k]

            def middle(b, h, uses):
                rs = resets[:, h, :]
                rs_rev = rs[:, P:0:-1]
                dve.wait_ge(resets_in[h], 16 * uses)
                V.tensor_reduce(inmin[:, :], rs[:, 1:P], AX_X, ALU.min)
                dve.wait_ge(lt_ready, b + 1)
                V.tensor_tensor_scan(fwd0, rs[:, 0:P], mid_ps[:, 0:P], NEG, ALU.add, ALU.max).then_inc(ends_ready, 1)
                dve.wait_ge(ends_row, b + 1)
                V.tensor_copy(rows[0:1, :, :].rearrange("a n q -> a (n q)"), row_ps[0:1, 0:3 * P]).then_inc(v_step, 1)
                V.tensor_copy(carry[0:1, 0:K], carry[0:1, P:P + K]).then_inc(v_step, 1)
                vn.next()
                dve.wait_ge(v_step, vn.next())
                V.tensor_tensor(rmin[0:1, :], rows[0:1, 1, :], rows[0:1, 2, :], ALU.min)
                V.tensor_tensor(rnext[0:1, 0:P - K], rows[0:1, 1, 0:P - K], rows[0:1, 2, K:P], ALU.add).then_inc(v_step, 1)
                dve.wait_ge(v_step, vn.next())
                for k in range(K):
                    last = V.tensor_tensor_scan(by_head(carry[0:1, K:P + K], k), by_head(rmin[0:1, :], k), by_head(rows[0:1, 0, :], k),
                                                carry[0:1, k:k + 1], ALU.add, ALU.max)
                last.then_inc(carry_ready, 1)
                dve.wait_ge(carry_col, b + 1)
                V.tensor_copy(ccol[:, :], row_ps[:, 384:385]).then_inc(v_step, 1)
                dve.wait_ge(v_step, vn.next())
                V.tensor_tensor_scan(fwd, rs[:, 0:P], mid_ps[:, 0:P], ccol[:, :], ALU.add, ALU.max).then_inc(v_step, 1)
                dve.wait_ge(v_step, vn.next())
                V.tensor_tensor_scan(rev0[:, ::-1], rs_rev, fwd[:, ::-1], NEG, ALU.add, ALU.max).then_inc(heads_ready, 1)
                dve.wait_ge(heads_row, b + 1)
                for k in range(K):
                    last = V.tensor_tensor_scan(by_head(back[0:1, :], k)[:, ::-1], by_head(rnext[0:1, :], k)[:, ::-1],
                                                by_head(row_ps[0:1, 0:P], k)[:, ::-1], NEG, ALU.add, ALU.max)
                last.then_inc(v_step, 1)
                dve.wait_ge(v_step, vn.next())
                V.tensor_tensor(backx[0:1, 0:P - K], back[0:1, K:P], rows[0:1, 2, K:P], ALU.add).then_inc(back_ready, 1)
                V.tensor_tensor(ratio[0:1, 0, :], carry[0:1, 0:K], rows[0:1, 2, 0:K], ALU.add).then_inc(v_step, 1)
                dve.wait_ge(v_step, vn.next())
                V.tensor_tensor(ratio[0:1, 0, :], ratio[0:1, 0, :], back[0:1, 0:K], ALU.subtract).then_inc(v_step, 1)
                dve.wait_ge(v_step, vn.next())
                dve.wait_ge(back_col, b + 1)
                V.tensor_copy(dcol[:, :], row_ps[:, 385:386]).then_inc(v_step, 1)
                dve.wait_ge(v_step, vn.next())
                V.tensor_tensor_scan(rev[:, ::-1], rs_rev, fwd[:, ::-1], dcol[:, :], ALU.add, ALU.max).then_inc(v_step, 1)
                dve.wait_ge(v_step, vn.next())
                V.tensor_tensor(xexp, mid_ps[:, 0:P], rev, ALU.subtract).then_inc(x_ready, 1)
                dve.wait_ge(et_ready, b + 1)
                V.tensor_copy(zs[:, h, :, KR:AW], mid_ps[:, 0:P].rearrange("p (j k) -> p j k", k=K)).then_inc(v_step, 1)
                dve.wait_ge(v_step, vn.next())
                for g in range(NG):
                    z = zs[:, h, g * G:(g + 1) * G, 0:KR].rearrange("p j (k r) -> p j k r", r=R)
                    w = spread(zs[:, h, g * G:(g + 1) * G, KR:AW].rearrange("p j (k a) -> p j k a", a=1), 3, R)
                    V.tensor_tensor(z, z, w, ALU.mult).then_inc(weights_ready, 1)
                dve.wait_ge(ratio_ready, b + 1)
                V.tensor_scalar(ratio[0:1, 1, :], ratio[0:1, 1, :], 1.0, None, ALU.subtract).then_inc(v_step, 1)
                dve.wait_ge(v_step, vn.next())
                dve.wait_ge(accrow_ready, b + 1)
                V.tensor_tensor(corr[0:1, 0:KR].rearrange("a (k r) -> a k r", r=R), row_ps[0:1, 0:KR].rearrange("a (k r) -> a k r", r=R),
                                spread(ratio[0:1, 1, :].rearrange("a (k b) -> a k b", b=1), 2, R), ALU.mult)
                V.tensor_tensor(corr[0:1, KR:AW], row_ps[0:1, KR:AW], ratio[0:1, 1, :], ALU.mult).then_inc(corr_ready, 1)

            FRONT_STEPS = 1 + NG - 1
            MID_STEPS = 12
            front(0, 0, None, 1, True, True)
            middle(0, 0, 1)
            front(1, 1, None, 1, False, True)
            middle(1, 1, 1)
            with nc.vector.Fori(1, NB // 2 - 1) as i:
                vn.loop(i - 1, 2 * (FRONT_STEPS + MID_STEPS))
                for h in range(2):
                    b = 2 * i + h
                    front(b, h, (b - 2) * B, i + 1, False, True)
                    middle(b, h, i + 1)
                vn.end(NB // 2 - 2)
            for h in range(2):
                b = NB - 2 + h
                front(b, h, (b - 2) * B, NB // 2, False, False)
                middle(b, h, NB // 2)


            dve.wait_ge(acc_ready, S + 1)

            def sums_reciprocal(g, h):
                V.tensor_scalar(rec[:, h, :, :], acc[:, bass.ds(g * T7, T7), KR:AW], 1e-16, None, ALU.add).then_inc(v_step, 1)
                dve.wait_ge(v_step, vn.next())
                V.reciprocal(rec[:, h, :, :], rec[:, h, :, :]).then_inc(rec_ready, 1)

            def dense_tile(g, h, t):
                n = g * T7 + t
                dve.wait_ge(aT_ps, n + 1)
                V.tensor_copy(aT[:, (h + t) % 2, :], psum[(h + t) % 2][0:KR, 0:P]).then_inc(aT_ready, 1)
                dve.wait_ge(relu_done, n + 1)
                V.tensor_tensor(xTb[:, h, t, :], xin[:, h, t, :], xTb[:, h, t, :], ALU.add).then_inc(y_added, 1)
                dve.wait_ge(y_added, n + 1)
                V.nop(nofuse=True)
                V.bn_stats(stats[:, t, :], xTb[:, h, t, :]).then_inc(v_step, 1)
                dve.wait_ge(v_step, vn.next())
                V.nop(nofuse=True)
                last = V.bn_aggr(mv[:, h, t, :], stats[:, t, :])
                if t == T7 - 1:
                    last.then_inc(var_ready, 1)

            def stage(j, h, dense, tables, more, two_parts=False):
                if tables:
                    dve.wait_ge(rstd_ready, j)
                    V.scalar_tensor_tensor(rstd[:, 1 - h, :, 1], mv[:, 1 - h, :, 0], -1.0, rstd[:, 1 - h, :, 0], ALU.mult, ALU.mult).then_inc(nb_ready, 1)
                if dense:
                    dve.wait_ge(x2_in[h], 16 * ((j - h) // 2 + 1) + (16 if two_parts else 0) if type(j) is int else X2_IN(j, h))
                    for t in range(DENSE_FIRST):
                        dense_tile(j, h, t)
                if tables:
                    for t in range(T7):
                        n = (j - 1) * T7 + t
                        dve.wait_ge(x1T_ps, n + 1)
                        V.tensor_copy(x1T[:, (1 - h + t) % 2, :], psum[4 + (1 - h + t) % 2][:, 0:D]).then_inc(x1T_ready, 1)
                if dense:
                    for t in range(DENSE_FIRST, T7):
                        dense_tile(j, h, t)
                if more:
                    dve.wait_ge(agn_ready, j + 1)
                    sums_reciprocal(j + 2, h)

            for g in range(2):
                sums_reciprocal(g, g)
            stage(0, 0, True, False, True)
            stage(1, 1, True, True, True)
            with nc.vector.Fori(1, NG7 // 2 - 1) as i:
                X2_IN = lambda j, h: 16 * (i + 1)
                vn.loop(i - 1, 2 * (T7 + 1))
                for h in range(2):
                    stage(2 * i + h, h, True, True, True)
                vn.end(NG7 // 2 - 2)
            stage(NG7 - 2, 0, True, True, False)
            stage(NG7 - 1, 1, True, True, False, two_parts=True)
            stage(NG7, 0, False, True, False)

            def attend_group(i, h):
                g = 2 * i + h
                z = lg[:, h, :, :]
                rowsg = xto[:, h, :, 0:HO].rearrange("p t (h o) -> p t h o", h=H)
                dve.wait_ge(al_in[h], 16 * T7 * (i + 1))
                dve.wait_ge(xg_in[h], 16 * T7 * (i + 1))
                V.tensor_tensor(z, algat[:, h, :, :], xto[:, h, :, HO:XW], ALU.add).then_inc(v_step, 1)
                dve.wait_ge(v_step, vn.next())
                V.scalar_tensor_tensor(z, z, 0.01, z, ALU.mult, ALU.max).then_inc(v_step, 1)
                dve.wait_ge(v_step, vn.next())
                V.tensor_reduce(lmax[:, :, 0:1], z, AX_X, ALU.max).then_inc(v_step, 1)
                dve.wait_ge(v_step, vn.next())
                V.tensor_tensor(z, z, spread(lmax[:, :, 0:1], 2, H), ALU.subtract).then_inc(lg_ready, 1)
                dve.wait_ge(lg_exp, g + 1)
                V.tensor_reduce(lmax[:, :, 0:1], z, AX_X, ALU.add).then_inc(v_step, 1)
                dve.wait_ge(v_step, vn.next())
                V.reciprocal(lmax[:, :, 1:2], lmax[:, :, 0:1]).then_inc(v_step, 1)
                dve.wait_ge(v_step, vn.next())
                V.tensor_tensor(z, z, spread(lmax[:, :, 1:2], 2, H), ALU.mult).then_inc(v_step, 1)
                dve.wait_ge(v_step, vn.next())
                for t in range(T7):
                    last = V.tensor_tensor(rowsg[:, t], rowsg[:, t], spread(z[:, t, :].rearrange("p (h a) -> p h a", a=1), 2, O), ALU.mult)
                last.then_inc(v_step, 1)
                dve.wait_ge(v_step, vn.next())
                V.tensor_reduce(tmp[:, :, :], rowsg.rearrange("p t h o -> p t o h"), AX_X, ALU.add).then_inc(xg_used, 1)
                dve.wait_ge(xg_used, g + 1)
                for t in range(T7):
                    y = x1[:, bass.ds(g * T7 + t, 1), :].rearrange("p a (h o) -> p (a h) o", h=H)
                    V.tensor_tensor(y, y, spread(tmp[:, t:t + 1, :], 1, H), ALU.add).then_inc(v_step, 1)
                    dve.wait_ge(v_step, vn.next())
                    V.nop(nofuse=True)
                    V.bn_stats(stats[:, t, :], x1[:, bass.ds(g * T7 + t, 1), :].rearrange("p a d -> p (a d)")).then_inc(v_step, 1)
                    dve.wait_ge(v_step, vn.next())
                    V.nop(nofuse=True)
                    last = V.bn_aggr(mv[:, h, t, :], stats[:, t, :])
                last.then_inc(var2_ready, 1)
                dve.wait_ge(rstd2_ready, g + 1)
                V.scalar_tensor_tensor(rstd[:, h, :, 1], mv[:, h, :, 0], -1.0, rstd[:, h, :, 0], ALU.mult, ALU.mult).then_inc(nb2_ready, 1)

            dve.wait_ge(x1_kept, NG7)
            with nc.vector.Fori(0, NG7 // 2) as i:
                vn.loop(i, 2 * (7 + 2 * T7))
                for h in range(2):
                    attend_group(i, h)
                vn.end(NG7 // 2)

        @block.tensor
        def _(pe):
            T = nc.tensor

            def steps_of(b, g):
                _, tiles = nc.values_load_multi_w_load_instructions(
                    trow[0:1, bass.ds(b * B + g * G, G)], engines=[mybir.EngineType.PE], min_val=0, max_val=NT,
                    skip_runtime_bounds_check_because="the vector engine has clamped the node tile")
                return tiles

            pe.wait_ge(diag_ready, 1)
            for g in range(SG):
                last = T.matmul(psum[4 + g // 4][:, (g % 4) * P:(g % 4 + 1) * P], ones[:, :], diag[:, g * P:(g + 1) * P], start=True, stop=True)
                if g % 4 == 3 or g == SG - 1:
                    last.then_inc(bcast_ready, 1)

            def transpose_x(h, t, r):
                for c in range(DC):
                    last = T.transpose(psum[r][:, c * P:(c + 1) * P], xin[:, h, t, c * P:(c + 1) * P], ident[:, :])
                last.then_inc(xt_ps, 1)

            def project(i, first, last_one):
                for m in range(2 * T7):
                    h, t, r = m // T7, m % T7, m % 2
                    n = 2 * T7 * i + m
                    if m + 1 < 2 * T7:
                        if m + 1 == T7:
                            pe.wait_ge(x_in[1], 16 * (i + 1) + (16 if last_one else 0))
                        transpose_x((m + 1) // T7, (m + 1) % T7, (m + 1) % 2)
                    elif not last_one:
                        pe.wait_ge(x_in[0], 16 * (i + 2))
                        transpose_x(0, 0, 0)
                    if t == 0 and not first:
                        pe.wait_ge(zu_copied, 2 * i + h - 1)
                    pe.wait_ge(xt_copied, n + 1)
                    for c in range(DC):
                        last = T.matmul(psum[2 + h][:, t * KR:(t + 1) * KR], xTb[:, h, t, c * P:(c + 1) * P],
                                        ur[:, c, :, :].rearrange("p k r -> p (k r)"), start=(c == 0), stop=(c == DC - 1))
                    if t == T7 - 1:
                        last.then_inc(zu_ps, 1)

            pe.wait_ge(consts, 1)
            pe.wait_ge(u_in, 16 * DC)
            pe.wait_ge(x_in[0], 16)
            transpose_x(0, 0, 0)
            project(0, True, False)
            with nc.tensor.Fori(1, NG7 // 2 - 1) as i:
                project(i, False, False)
            project(NG7 // 2 - 1, False, True)

            pe.wait_ge(dloc_ready, 2)
            T.matmul(psum[7][:, 0:SG], shift[:, :], lastcol[:, 1:SG + 1], start=True, stop=False)
            T.matmul(psum[7][:, 0:SG], corner[:, :], lastcol[:, 0:SG], start=False, stop=True).then_inc(plast_ready, 1)
            for n, table in enumerate((dloc, srcf)):
                pe.wait_ge(tab_read, n + 1)
                for g in range(SG):
                    last = T.transpose(psum[4 + g // 4][:, (g % 4) * P:(g % 4 + 1) * P], table[:, g, :], ident[:, :])
                last.then_inc(tab_ps, 1)
            pe.wait_ge(tab_read, 3)
            for g in range(SG):
                last = T.matmul(psum[4 + g // 4][0:1, (g % 4) * P:(g % 4 + 1) * P], tstep[:, g:g + 1], ident[:, :], start=True, stop=True)
            last.then_inc(tab_ps, 1)
            pe.wait_ge(tab_read, 5)
            T.transpose(psum[4][:, 0:P], okrow[:, 0, :], ident[:, :])
            T.transpose(psum[4][:, P:2 * P], okrow[:, 1, :], ident[:, :]).then_inc(tab_ps, 1)

            pe.wait_ge(weights_in, 16 * 5)
            pe.wait_ge(tab_read, 6)
            T.matmul(psum[7][:, :], ones[0:1, :], attn[0:1, :], start=True, stop=True)
            for a in range(DC):
                for c in range(DC):
                    T.matmul(psum[4][:, a * D:(a + 1) * D], dm[:, c, a * P:(a + 1) * P], dm[:, c, :], start=(c == 0), stop=(c == DC - 1))
            pe.wait_ge(prep_read, 2)
            T.matmul(psum[5][:, 0:K], ones[0:1, :], hw[0:1, 1, :], start=True, stop=True).then_inc(prep_ps, 1)
            pe.wait_ge(prep_read, 3)
            for a in range(DC):
                for c in range(DC):
                    last = T.matmul(psum[6][:, a * D:(a + 1) * D], gs[:, c, a * P:(a + 1) * P], dm[:, c, :], start=(c == 0), stop=(c == DC - 1))
            last.then_inc(prep_ps, 1)
            pe.wait_ge(prep_read, 5)
            for c in range(DC):
                last = T.matmul(psum[4][0:KR, 0:D], ur[:, c, :, :].rearrange("p k r -> p (k r)"), mz[:, c, :], start=(c == 0), stop=(c == DC - 1))
            last.then_inc(prep_ps, 1)
            pe.wait_ge(prep_read, 6)

            def transpose_onehot(b, h, u, first):
                m = u // TR
                if u % TR == 0 and (m >= 2 or not first):
                    pe.wait_ge(oneT_ready, 8 * b + m - 1)
                last = T.transpose(tr_ps[m % 2][:, (u % TR) * P:(u % TR + 1) * P], onehot[:, h, u, :], ident[:, :])
                if u % TR == TR - 1:
                    last.then_inc(oneT_ps, 1)

            def expand(b, u, tiles, first):
                g = u // G
                if u % G == 0 and (g >= 2 or not first):
                    pe.wait_ge(zd_used, NG * b + g - 1)
                if u % TR == 0:
                    pe.wait_ge(oneT_ready, 8 * b + u // TR + 1)
                last = T.matmul(zd_ps[g % 2][:, (u % G) * KR:(u % G + 1) * KR], onehotT[:, u % (2 * G), :],
                                z_sb[:, bass.ds(tiles[u % G], 1), :].rearrange("p a c -> p (a c)"), start=True, stop=True)
                if u % G == G - 1:
                    last.then_inc(zd_ready, 1)

            def front(b, h, first):
                for u in range(B):
                    if u % G == 0:
                        pe.wait_ge(onehot_ready, NG * b + u // G + 1)
                    transpose_onehot(b, h, u, first)
                    if u >= G:
                        if u % G == 0:
                            tiles = steps_of(b, u // G - 1)
                        expand(b, u - G, tiles, first)
                tiles = steps_of(b, NG - 1)
                for u in range(B - G, B):
                    expand(b, u, tiles, first)

            def add_up(b, h, u, tiles, between=None):
                if u % G == 0:
                    pe.wait_ge(weights_ready, NG * b + u // G + 1)
                ps = acc_ps[u % 2][:, 0:AW]
                T.matmul(ps, onehot[:, h, u, :], zs[:, h, u, :], start=True, stop=False)
                if u == 0:
                    pe.wait_ge(corr_ready, b + 1)
                    T.matmul(ps, onehot[0:1, h, 0, :], corr[0:1, :], start=False, stop=False)
                if between is not None:
                    between()
                pe.wait_ge(acc_ready, B * b + u + 1)
                T.matmul(ps, ident[:, :], acc[:, bass.ds(tiles[u % G], 1), :].rearrange("p a c -> p (a c)"),
                         start=False, stop=True).then_inc(agg_done, 1)

            def back_and_front(b, h, first):
                for u in range(B):
                    if u % G == 0:
                        tiles_a = steps_of(b - 1, u // G)
                        pe.wait_ge(onehot_ready, NG * b + u // G + 1)
                        if u >= G:
                            tiles_z = steps_of(b, u // G - 1)

                    def between():
                        transpose_onehot(b, h, u, first)
                        if u >= G:
                            expand(b, u - G, tiles_z, first)
                    add_up(b - 1, 1 - h, u, tiles_a, between)
                tiles_z = steps_of(b, NG - 1)
                for u in range(B - G, B):
                    expand(b, u, tiles_z, first)

            def middle(b, h):
                pe.wait_ge(logits_ready, b + 1)
                T.transpose(mid_ps[:, 0:P], logits[:, h, :], ident[:, :]).then_inc(lt_ready, 1)
                pe.wait_ge(ends_ready, b + 1)
                T.matmul(row_ps[0:1, 0:P], fwd0[:, P - 1:P], ident[:, :], start=True, stop=True)
                T.matmul(row_ps[0:1, P:2 * P], inmin[:, :], ident[:, :], start=True, stop=True)
                T.matmul(row_ps[0:1, 2 * P:3 * P], resets[:, h, 0:1], ident[:, :], start=True, stop=True).then_inc(ends_row, 1)
                pe.wait_ge(carry_ready, b + 1)
                T.matmul(row_ps[:, 384:385], carry[0:1, 0:P], ones[0:1, 0:1], start=True, stop=True).then_inc(carry_col, 1)
                pe.wait_ge(heads_ready, b + 1)
                T.matmul(row_ps[0:1, 0:P], rev0[:, 0:1], ident[:, :], start=True, stop=True).then_inc(heads_row, 1)
                pe.wait_ge(back_ready, b + 1)
                T.matmul(row_ps[:, 385:386], backx[0:1, :], ones[0:1, 0:1], start=True, stop=True).then_inc(back_col, 1)
                pe.wait_ge(e_ready, b + 1)
                T.transpose(mid_ps[:, 0:P], eexp, ident[:, :]).then_inc(et_ready, 1)
                _, (t0,) = nc.values_load_multi_w_load_instructions(
                    trow[0:1, bass.ds(b * B, 1)], engines=[mybir.EngineType.PE], min_val=0, max_val=NT,
                    skip_runtime_bounds_check_because="the vector engine has clamped the node tile")
                pe.wait_ge(acc_ready, B * b + 1)
                T.matmul(row_ps[0:1, 0:AW], first_col[:, h:h + 1], acc[:, bass.ds(t0, 1), :].rearrange("p a c -> p (a c)"),
                         start=True, stop=True).then_inc(accrow_ready, 1)

            front(0, 0, True)
            middle(0, 0)
            back_and_front(1, 1, False)
            middle(1, 1)
            with nc.tensor.Fori(1, NB // 2 - 1) as i:
                for h in range(2):
                    back_and_front(2 * i + h, h, False)
                    middle(2 * i + h, h)
            for h in range(2):
                back_and_front(NB - 2 + h, h, False)
                middle(NB - 2 + h, h)
            for u in range(B):
                if u % G == 0:
                    tiles = steps_of(NB - 1, u // G)
                add_up(NB - 1, 1, u, tiles)

            def dense_tile(g, h, t, first):
                n = g * T7 + t
                r = (h + t) % 2
                T.nop(nofuse=True)
                T.transpose(psum[r][0:KR, 0:P], agn[:, h, t, :], ident[:, :]).then_inc(aT_ps, 1)
                if t >= 2 or not first:
                    pe.wait_ge(relu_done, n - 1)
                ps = psum[2 + r][:, 0:D]
                for c in range(DC):
                    T.matmul(ps, xTb[:, h, t, c * P:(c + 1) * P], mz[:, c, :], start=(c == 0), stop=False)
                pe.wait_ge(aT_ready, n + 1)
                T.matmul(ps, aT[:, r, :], w3[:, :], start=False, stop=True).then_inc(y_ps, 1)

            def transpose_x1(h, t, r):
                for c in range(DC):
                    last = T.transpose(psum[4 + r][:, c * P:(c + 1) * P], xTb[:, h, t, c * P:(c + 1) * P], ident[:, :])
                last.then_inc(x1T_ps, 1)

            def table_tiles(g, h, first):
                for t in range(T7):
                    n = g * T7 + t
                    r = (h + t) % 2
                    if t == 0:
                        pe.wait_ge(x1_ready, n + 1)
                        transpose_x1(h, 0, r)
                    if t + 1 < T7:
                        pe.wait_ge(x1_ready, n + 2)
                        transpose_x1(h, t + 1, 1 - r)
                    if t >= 2 or not first:
                        pe.wait_ge(xt1_copied, n - 1)
                    pe.wait_ge(x1T_ready, n + 1)
                    for c in range(DC):
                        last = T.matmul(psum[6 + r][:, 0:WW], x1T[:, r, c * P:(c + 1) * P], wx[:, c, :], start=(c == 0), stop=(c == DC - 1))
                    last.then_inc(xt1_ps, 1)

            def stage(j, h, xT_loads, dense, tables):
                if dense:
                    pe.wait_ge(xT_in[h], 16 * xT_loads)
                    pe.wait_ge(agn_ready, j + 1)
                    for t in range(DENSE_FIRST):
                        dense_tile(j, h, t, not tables)
                if tables:
                    table_tiles(j - 1, 1 - h, type(j) is int and j == 1)
                if dense:
                    for t in range(DENSE_FIRST, T7):
                        dense_tile(j, h, t, not tables)

            stage(0, 0, 1, True, False)
            stage(1, 1, 1, True, True)
            with nc.tensor.Fori(1, NG7 // 2) as i:
                for h in range(2):
                    stage(2 * i + h, h, i + 1, True, True)
            stage(NG7, 0, 0, False, True)

        @block.scalar
        def _(act):
            A = nc.scalar

            def project(i, first):
                for m in range(2 * T7):
                    h, t, r = m // T7, m % T7, m % 2
                    g = 2 * i + h
                    if t == 0 and not first:
                        act.wait_ge(xT_out[h], 16 * i)
                    act.wait_ge(xt_ps, 2 * T7 * i + m + 1)
                    A.activation(xTb[:, h, t, :], psum[r][:, 0:D], ACT.Copy).then_inc(xt_copied, 1)
                    if t == T7 - 1:
                        act.wait_ge(zu_ps, g + 1)
                        A.activation(z_sb[:, bass.ds(g * T7, T7), :].rearrange("p t c -> p (t c)"), psum[2 + h][:, 0:T7 * KR],
                                     ACT.Copy).then_inc(zu_copied, 1)
            project(0, True)
            with nc.scalar.Fori(1, NG7 // 2) as i:
                project(i, False)
            act.wait_ge(prep_read, 1)
            A.activation(hw[0:1, 2, :], hw[0:1, 1, :], ACT.Exp).then_inc(prep_exp, 1)

            def store_sums(b):
                for u in range(B):
                    if u % G == 0:
                        _, tiles = nc.values_load_multi_w_load_instructions(
                            trow[0:1, bass.ds(b * B + u, G)], engines=[mybir.EngineType.Activation], min_val=0, max_val=NT,
                            skip_runtime_bounds_check_because="the vector engine has clamped the node tile")
                    act.wait_ge(agg_done, B * b + u + 1)
                    A.activation(acc[:, bass.ds(tiles[u % G], 1), :].rearrange("p a c -> p (a c)"), acc_ps[u % 2][:, 0:AW],
                                 ACT.Copy).then_inc(acc_ready, 1)

            def weights(b):
                act.wait_ge(x_ready, b + 1)
                A.activation(eexp, xexp, ACT.Exp, scale=float(R) ** -0.5).then_inc(e_ready, 1)
                A.activation(ratio[0:1, 1, :], ratio[0:1, 0, :], ACT.Exp, scale=float(R) ** -0.5).then_inc(ratio_ready, 1)

            act.wait_ge(tab_read, 4)
            weights(0)
            store_sums(0)
            weights(1)
            with nc.scalar.Fori(1, NB // 2 - 1) as i:
                for h in range(2):
                    store_sums(2 * i + h - 1)
                    weights(2 * i + h)
            for h in range(2):
                store_sums(NB - 3 + h)
                weights(NB - 2 + h)
            store_sums(NB - 1)

            def rstd_of(h, g, variance, ln, ready):
                act.wait_ge(variance, g + 1)
                A.activation(rstd[:, h, :, 2], mv[:, h, :, 1], ACT.Ln, bias=eps_t[:, 0:1]).then_inc(ln, 1)
                act.wait_ge(ln, g + 1)
                A.activation(rstd[:, h, :, 0], rstd[:, h, :, 2], ACT.Exp, scale=-0.5).then_inc(ready, 1)

            def normalise(h, g, t, done):
                y = x1[:, bass.ds(g * T7 + t, 1), :].rearrange("p a d -> p (a d)")
                A.activation(y, y, ACT.Identity, bias=rstd[:, h, t, 1:2], scale=rstd[:, h, t, 0:1]).then_inc(done, 1)

            def relu_tile(g, h, t):
                act.wait_ge(y_ps, g * T7 + t + 1)
                A.activation(xTb[:, h, t, :], psum[2 + (h + t) % 2][:, 0:D], ACT.Relu, bias=eps_t[:, 1:2]).then_inc(relu_done, 1)

            def norm_tile(h, t):
                y = xTb[:, h, t, :]
                A.activation(y, y, ACT.Identity, bias=rstd[:, h, t, 1:2], scale=rstd[:, h, t, 0:1]).then_inc(x1_ready, 1)

            def stage(j, h, dense, tables, reuse):
                if tables:
                    rstd_of(1 - h, j - 1, var_ready, ln_done, rstd_ready)
                    act.wait_ge(nb_ready, j)
                for t in range(DENSE_FIRST):
                    if dense:
                        relu_tile(j, h, t)
                    if tables:
                        for n in range(T7 * t // DENSE_FIRST, T7 * (t + 1) // DENSE_FIRST):
                            norm_tile(1 - h, n)
                if tables:
                    if reuse is not None:
                        act.wait_ge(table_out[1 - h], 32 * reuse)
                    for t in range(T7):
                        act.wait_ge(xt1_ps, (j - 1) * T7 + t + 1)
                        A.activation(xto[:, 1 - h, t, :], psum[6 + (1 - h + t) % 2][:, 0:WW], ACT.Copy).then_inc(xt1_copied, 1)
                if dense:
                    for t in range(DENSE_FIRST, T7):
                        relu_tile(j, h, t)

            stage(0, 0, True, False, None)
            stage(1, 1, True, True, None)
            stage(2, 0, True, True, None)
            stage(3, 1, True, True, 1)
            with nc.scalar.Fori(2, NG7 // 2) as i:
                stage(2 * i, 0, True, True, i - 1)
                stage(2 * i + 1, 1, True, True, i)
            stage(NG7, 0, False, True, NG7 // 2 - 1)

            with nc.scalar.Fori(0, NG7 // 2) as i:
                for h in range(2):
                    g = 2 * i + h
                    act.wait_ge(lg_ready, g + 1)
                    A.activation(lg[:, h, :, :], lg[:, h, :, :], ACT.Exp).then_inc(lg_exp, 1)
                    rstd_of(h, g, var2_ready, ln2_done, rstd2_ready)
                    act.wait_ge(nb2_ready, g + 1)
                    for t in range(T7 - 1):
                        y = x1[:, bass.ds(g * T7 + t, 1), :].rearrange("p a d -> p (a d)")
                        A.activation(y, y, ACT.Identity, bias=rstd[:, h, t, 1:2], scale=rstd[:, h, t, 0:1])
                    normalise(h, g, T7 - 1, out_ready)


_INS = ["x", "src", "dst", "L0_gnn_U", "L0_gnn_Dmat", "L0_gnn_head_w", "L1_gnn_weight", "L1_gnn_attn_l", "L1_gnn_attn_r"]


def kernel(**inputs):
    import concourse.bacc as bacc
    from concourse.bass_utils import run_bass_kernel_spmd

    nc = bacc.Bacc("TRN2", target_bir_lowering=False, num_devices=1)
    arrays, args = {}, []
    for name in _INS:
        a = np.ascontiguousarray(inputs[name])
        arrays[f"in_{name}"] = a
        args.append(nc.dram_tensor(f"in_{name}", a.shape, mybir.dt.from_np(a.dtype), kind="ExternalInput").ap())
    out = nc.dram_tensor("out_0", (N, D), F32, kind="ExternalOutput").ap()
    program(nc, *args, out)
    r = run_bass_kernel_spmd(nc, [arrays], core_ids=[0])
    return r.results[0]["out_0"]
```

```python
from contextlib import ExitStack

import numpy as np
import concourse.bass as bass
from concourse import mybir
from concourse.alu_op_type import AluOpType as ALU

F32 = mybir.dt.float32
I32 = mybir.dt.int32
BF16 = mybir.dt.bfloat16
ACT = mybir.ActivationFunctionType
AX_X = mybir.AxisListType.X

P = 128
N = 12500
E = 200000
D = 256
DC = D // P
K, R = 4, 16
KR = K * R
H, O = 4, 64
HO = H * O
NT = -(-N // P)
ET = -(-E // P)
LASTN = N - (NT - 1) * P
B = 32
S = -(-(ET + NT) // P) * P
SG = S // P
NB = S // B
G = 8
NG = B // G
Q = 4
NSPARE = 4
ZP = 3
AW = KR + K
XW = HO + H
WW = XW + H
NEG = -1e30
PAD = P * (NT + 2)
ETA, LAM, EPS = 0.5, 0.1, 1e-5
T7 = 7
NG7 = NT // T7
DENSE_FIRST = 3
assert NT % (2 * T7) == 0 and S % (2 * B) == 0 and ET + NT <= S and E % P in (0, 64)


def spread(ap, axis, n):
    shape = list(ap.shape)
    shape[axis] = n
    return ap.broadcast_to(shape)


class Count:

    def __init__(self):
        self.base, self.n, self.i, self.per = 0, 0, None, 0

    def loop(self, i, per):
        self.base, self.n, self.i, self.per = self.base + self.n, 0, i, per

    def end(self, trips):
        assert self.n == self.per, (self.n, self.per)
        self.base, self.n, self.i, self.per = self.base + self.per * trips, 0, None, 0

    def next(self):
        self.n += 1
        return self.base + self.n + (self.i * self.per if self.i is not None else 0)


def program(nc, x, src, dst, u, dmat, head_w, weight, attn_l, attn_r, out):
    ctx = ExitStack()
    with ctx:
        def sb(name, shape, dt=F32):
            return ctx.enter_context(nc.sbuf_tensor(name, shape, dt))

        def sem(name):
            return ctx.enter_context(nc.semaphore(name))

        dst_rows = nc.dram_tensor("dst_rows", (S, P), I32).ap()
        src_rows = nc.dram_tensor("src_rows", (S, P), I32).ap()
        reset_rows = nc.dram_tensor("reset_rows", (S, P), F32).ap()
        z_table = nc.dram_tensor("z_table", (NT * P, KR), F32).ap()
        xT_store = nc.dram_tensor("xT_store", (NT, P, D), F32).ap()
        xt_table = nc.dram_tensor("xt_table", (NT * P, XW), F32).ap()
        al_table = nc.dram_tensor("al_table", (NT * P, H), F32).ap()

        arena = sb("arena", [P, NT * D])
        at = [0]

        def part(width):
            a = arena[:, at[0]:at[0] + width]
            at[0] += width
            assert at[0] <= NT * D
            return a

        z3 = part((NT + 1) * ZP * KR // 2).bitcast(BF16).rearrange("p (t s c) -> p t s c", s=ZP, c=KR)
        zs = part(2 * B * AW).rearrange("p (h j c) -> p h j c", h=2, j=B)
        dslot = part(S)
        keep = part(S // 2).bitcast(BF16)
        shift = part(P)
        corner = part(P)
        oflat = arena[:, at[0]:at[0] + 4 * S]
        onehot = part(B * P).bitcast(BF16).rearrange("p (h j n) -> p h j n", h=2, j=B)
        onehotT = part(B * P // 2).bitcast(BF16).rearrange("p (j e) -> p j e", j=B)
        sums = part(AW * (B + 1)).rearrange("p (c j) -> p c j", c=AW)
        x1 = arena[:, :].rearrange("p (t d) -> p t d", d=D)
        diag = oflat[:, 0:S]
        ulast = oflat[:, S:2 * S]
        keeprow = ulast[0:1, :]
        spare = oflat[0:1, 2 * S:3 * S]
        arowf = oflat[0:1, 3 * S:4 * S]
        junk = oflat[:, 2 * S:3 * S]
        dloc = oflat[:, 3 * S:4 * S].rearrange("p (g e) -> p g e", e=P)
        cont = diag.rearrange("p (g e) -> p g e", e=P)
        okrow = ulast.rearrange("p (g e) -> p g e", e=P)
        srcf = junk.rearrange("p (g e) -> p g e", e=P)

        acc = sb("acc", [P, NT + 1 + NSPARE, AW])
        zf = acc[:, :, :].rearrange("p t c -> p (t c)")[:, 0:NT * KR].rearrange("p (t c) -> p t c", c=KR)
        xto = sb("xto", [P, 2, T7, WW])
        xto_flat = xto[:, :, :, :].rearrange("p h t c -> p (h t c)")
        dst_sb = xto_flat[:, 0:S].bitcast(I32).rearrange("p (g e) -> p g e", e=P)
        src_sb = xto_flat[:, S:2 * S].bitcast(I32).rearrange("p (g e) -> p g e", e=P)
        zs_flat = zs.rearrange("p h j c -> p (h j c)")
        dst_step = zs_flat[:, 0:S].bitcast(I32).rearrange("p (g e) -> p g e", e=P)
        src_step = zs_flat[:, S:2 * S].bitcast(I32).rearrange("p (g e) -> p g e", e=P)
        wparts = xto_flat[:, 0:B * ZP * AW // 2].bitcast(BF16).rearrange("p (j s c) -> p j s c", s=ZP, c=AW)
        sslot = sb("sslot", [P, S], I32)
        tspace = sb("tspace", [P, S], I32)
        trow = tspace[0:1, :]
        arow = tspace[32:33, :]
        src1 = sb("src1", [P, P], I32)
        dst1 = sb("dst1", [P, P], I32)
        didx = sb("didx", [P, 2, B])
        sidx = sb("sidx", [P, 2, B], I32)
        ident = sb("ident", [P, P])
        ones = sb("ones", [P, P])
        iota_row = sb("iota_row", [P, P])
        iota_i = sb("iota_i", [P, P], I32)
        stepno_i = sb("stepno_i", [P, SG], I32)
        stepno = sb("stepno", [P, SG])
        pno = sb("pno", [P, 3])
        lastt_i = sb("lastt_i", [P, SG], I32)
        lastt = sb("lastt", [P, SG])
        istep = sb("istep", [P, SG])
        istep_i = sb("istep_i", [P, SG], I32)
        tstep = sb("tstep", [P, SG])
        tneg = sb("tneg", [P, SG])
        plast = sb("plast", [P, SG])
        x1T = sb("x1T", [P, 2, D])
        x1T_row = x1T[0:1, :, :].rearrange("a r d -> a (r d)")
        rows = x1T_row[:, 0:3 * P].rearrange("a (n q) -> a n q", q=P)
        rmin = x1T_row[:, 3 * P:4 * P]
        rnext = sb("rnext", [1, P])
        carry = sb("carry", [1, P + K])
        back = sb("back", [1, P])
        backx = sb("backx", [1, P])
        ratio = sb("ratio", [1, 2, K])
        inmin = sb("inmin", [P, 1])
        ccol = sb("ccol", [P, 1])
        dcol = sb("dcol", [P, 1])
        first_col = sb("first_col", [P, 2])
        fac = sb("fac", [P, K])
        ident_b = sb("ident_b", [P, P], BF16)
        iota_b = sb("iota_b", [P, P], BF16)
        xin = sb("xin", [P, 2, T7, D])
        xTb = sb("xTb", [P, 2, T7, D])
        xin_flat = xin[:, :, :, :].rearrange("p h t d -> p (h t d)")
        keepf = xin_flat[:, 0:AW * (B + 1)].rearrange("p (c j) -> p c j", c=AW)
        xat = [AW * (B + 1)]

        def xpart(width):
            a = xin_flat[:, xat[0]:xat[0] + width]
            xat[0] += width
            assert xat[0] <= 2 * T7 * D
            return a

        prod = xpart(G * KR).rearrange("p (j c) -> p j c", j=G)
        fwd0, fwd, rev0, rev, xexp, eexp = [xpart(P) for _ in range(6)]
        xTb_flat = xTb[:, :, :, :].rearrange("p h t d -> p (h t d)")
        state = xTb_flat[:, 0:AW * (B + 1)].rearrange("p (c j) -> p c j", c=AW)
        yat = AW * (B + 1)
        resets = xTb_flat[:, yat:yat + 2 * (P + 1)].rearrange("p (h e) -> p h e", h=2)
        yat += 2 * (P + 1)
        logits = xTb_flat[:, yat:yat + 2 * P].rearrange("p (h q) -> p h q", h=2)
        dm = sb("dm", [P, DC, D])
        ur = sb("ur", [P, DC, K, R])
        wx = sb("wx", [P, DC, WW])
        attn = sb("attn", [1, 2 * HO])
        hw = sb("hw", [1, 3, K])
        hsum = sb("hsum", [1, 3])
        gs = sb("gs", [P, DC, D])
        mz = sb("mz", [P, DC, D])
        w3 = sb("w3", [KR, D])
        wtmp = gs
        rec = sb("rec", [P, 2, T7, K])
        agn = sb("agn", [P, 2, T7, KR])
        lastcol = sb("lastcol", [P, SG + 1])
        aT = [sslot[0:KR, 0:T7 * P].bitcast(F32), tspace[0:KR, 0:T7 * P].bitcast(F32)]
        stats = sb("stats", [P, T7, 6])
        mv = sb("mv", [P, 2, T7, 2])
        rstd = sb("rstd", [P, 2, T7, 3])
        algat = sb("algat", [P, 2, T7, H])
        lg = sb("lg", [P, 2, T7, H])
        lmax = sb("lmax", [P, T7, 2])
        tmp = agn[:, 0, :, :]
        relu_bias = sb("relu_bias", [P, 1])

        psum = [ctx.enter_context(nc.psum_tensor(f"bank{i}", [P, 512], F32)) for i in range(8)]
        sum_ps = psum[0:2]
        tr_ps = [p[:, :].bitcast(BF16) for p in psum[2:4]]
        zd_ps = psum[4:6]
        mid_ps, row_ps = psum[6], psum[7]

        edges_in, u_in, weights_in = sem("edges_in"), sem("u_in"), sem("weights_in")
        rows_out, resets_out = sem("rows_out"), sem("resets_out")
        x_in = [sem(f"x_in{i}") for i in range(2)]
        z_rest = sem("z_rest")
        xT_out = [sem(f"xT_out{i}") for i in range(2)]
        z_out = sem("z_out")
        iotas, consts = sem("iotas"), sem("consts")
        v_step = sem("v_step")
        pads_set, diag_ready, bcast_ready, walk_ready = sem("pads_set"), sem("diag_ready"), sem("bcast_ready"), sem("walk_ready")
        tiles_gathered = sem("tiles_gathered")
        dloc_ready, plast_ready, reset_ready = sem("dloc_ready"), sem("plast_ready"), sem("reset_ready")
        tab_ps, tab_read = sem("tab_ps"), sem("tab_read")
        xt_ps, xt_copied, zu_ps, zu_copied = sem("xt_ps"), sem("xt_copied"), sem("zu_ps"), sem("zu_copied")
        prep_ps, prep_read, prep_exp = sem("prep_ps"), sem("prep_read"), sem("prep_exp")
        idx_ready = sem("idx_ready")
        gathered = [[sem(f"gathered{h}{g}") for g in range(NG)] for h in range(2)]
        onehot_ready, oneT_ps, oneT_ready = sem("onehot_ready"), sem("oneT_ps"), sem("oneT_ready")
        zd_ready, zd_used = sem("zd_ready"), sem("zd_used")
        logits_ready, lt_ready = sem("logits_ready"), sem("lt_ready")
        ends_ready, ends_row = sem("ends_ready"), sem("ends_row")
        carry_ready, carry_col = sem("carry_ready"), sem("carry_col")
        heads_ready, heads_row = sem("heads_ready"), sem("heads_row")
        back_ready, back_col = sem("back_ready"), sem("back_col")
        x_ready, e_ready, ratio_ready, et_ready = sem("x_ready"), sem("e_ready"), sem("ratio_ready"), sem("et_ready")
        z_parts, scale_ready = sem("z_parts"), sem("scale_ready")
        weighted, hi_ready, rest_ready, mid_ready, parts_ready = (
            sem("weighted"), sem("hi_ready"), sem("rest_ready"), sem("mid_ready"), sem("parts_ready"))
        sums_ps, sums_copied, keep_ready, scan_done, state_stored = (
            sem("sums_ps"), sem("sums_copied"), sem("keep_ready"), sem("scan_done"), sem("state_stored"))
        keeprow_ready = sem("keeprow_ready")
        resets_in = [sem(f"resets_in{h}") for h in range(2)]
        xT_in = [sem(f"xT_in{i}") for i in range(2)]
        x2_in = [sem(f"x2_in{i}") for i in range(2)]
        rec_ready, agn_ready, aT_ps, aT_ready, y_ps, relu_done, y_added = (
            sem("rec_ready"), sem("agn_ready"), sem("aT_ps"), sem("aT_ready"), sem("y_ps"), sem("relu_done"), sem("y_added"))
        var_ready, rstd_ready, nb_ready, x1_ready, x1_kept = (
            sem("var_ready"), sem("rstd_ready"), sem("nb_ready"), sem("x1_ready"), sem("x1_kept"))
        x1T_ps, x1T_ready, xt1_ps, xt1_copied = sem("x1T_ps"), sem("x1T_ready"), sem("xt1_ps"), sem("xt1_copied")
        table_out = [sem(f"table_out{i}") for i in range(2)]
        al_in = [sem(f"al_in{i}") for i in range(2)]
        xg_in = [sem(f"xg_in{i}") for i in range(2)]
        lg_ready, lg_exp, xg_used = sem("lg_ready"), sem("lg_exp"), sem("xg_used")
        var2_ready, rstd2_ready, nb2_ready, out_ready = (
            sem("var2_ready"), sem("rstd2_ready"), sem("nb2_ready"), sem("out_ready"))
        out_sent = [sem(f"out_sent{i}") for i in range(2)]

        FULL = E // P
        HALF = E - FULL * P
        G12 = (SG - 1) * P

        def rows_of(table, t, n):
            return table[bass.ds(t * P, n * P), :].rearrange("(t p) c -> p t c", p=P)

        block = ctx.enter_context(nc.Block())

        @block.sync
        def _(sp):
            sp.wait_ge(pads_set, 1)
            for e, tile in ((dst, dst_sb), (src, src_sb)):
                sp.dma_start(tile[:, 0:SG - 1, :], e[0:G12 * P].rearrange("(g p e) -> p g e", p=P, e=P)).then_inc(edges_in, 16)
                sp.dma_start(tile[0:FULL - G12, SG - 1, :], e[G12 * P:FULL * P].rearrange("(p e) -> p e", e=P)).then_inc(edges_in, 16)
                sp.dma_start(tile[FULL - G12:FULL - G12 + 1, SG - 1, 0:HALF], e[FULL * P:E].rearrange("(p e) -> p e", p=1)).then_inc(edges_in, 16)
            for c in range(DC):
                sp.dma_start(ur[:, c, :, :], u[:, c * P:(c + 1) * P, :].rearrange("k p r -> p k r")).then_inc(u_in, 16)
            def load_x(buf, g, signal):
                if type(g) is int and g == NG7 - 1:
                    sp.dma_start(xin[:, buf, 0:T7 - 1, :], rows_of(x, g * T7, T7 - 1)).then_inc(signal[buf], 16)
                    sp.dma_start(xin[0:LASTN, buf, T7 - 1, :], x[N - LASTN:N, :]).then_inc(signal[buf], 16)
                else:
                    sp.dma_start(xin[:, buf, :, :], rows_of(x, g * T7, T7)).then_inc(signal[buf], 16)
            load_x(0, 0, x_in)
            load_x(1, 1, x_in)
            sp.wait_ge(edges_in, 96)
            sp.dma_start(dst_rows.rearrange("(g p) e -> p g e", p=P), dst_sb[:, :, :]).then_inc(rows_out, 16)
            sp.dma_start(src_rows.rearrange("(g p) e -> p g e", p=P), src_sb[:, :, :]).then_inc(rows_out, 16)
            sp.dma_start(dm[:, :, :], dmat.rearrange("(c p) d -> p c d", p=P)).then_inc(weights_in, 16)
            sp.dma_start(wx[:, :, 0:HO], weight.rearrange("(c p) d -> p c d", p=P)).then_inc(weights_in, 16)
            sp.dma_start(attn[0:1, 0:HO], attn_r.rearrange("(a h) o -> a (h o)", a=1)).then_inc(weights_in, 16)
            sp.dma_start(attn[0:1, HO:2 * HO], attn_l.rearrange("(a h) o -> a (h o)", a=1)).then_inc(weights_in, 16)
            sp.dma_start(hw[0:1, 0, :], head_w.rearrange("(a h) -> a h", a=1)).then_inc(weights_in, 16)

            def dense_out(i, h):
                g = 2 * i + h
                sp.wait_ge(zu_copied, g + 1)
                sp.dma_start(rows_of(z_table, g * T7, T7), zf[:, bass.ds(g * T7, T7), :]).then_inc(z_out, 16)
                sp.dma_start(xT_store[bass.ds(g * T7, T7), :, :].rearrange("t p d -> p t d"), xTb[:, h, :, :]).then_inc(xT_out[h], 16)
            with nc.sync.Fori(0, NG7 // 2 - 2) as i:
                for h in range(2):
                    dense_out(i, h)
                    load_x(h, 2 * i + h + 2, x_in)
            for h in range(2):
                dense_out(NG7 // 2 - 2, h)
                load_x(h, NG7 - 2 + h, x_in)
            for h in range(2):
                dense_out(NG7 // 2 - 1, h)
            sp.wait_ge(reset_ready, 1)
            sp.dma_start(reset_rows.rearrange("(g p) e -> p g e", p=P), cont[:, :, :]).then_inc(resets_out, 16)
            sp.wait_ge(resets_out, 16)

            def load_resets(b, h):
                sp.dma_start(resets[:, h, 0:P], spread(reset_rows[bass.ds(b * B, B), :].rearrange("j (a e) -> j a e", a=1), 1, K)
                             ).then_inc(resets_in[h], 16)
            for h in range(2):
                sp.wait_ge(xT_out[h], 16 * (NG7 // 2))
            for b in range(2):
                load_resets(b, b)
            with nc.sync.Fori(1, NB // 2) as i:
                for h in range(2):
                    sp.wait_ge(x_ready, 2 * i + h - 1)
                    load_resets(2 * i + h, h)
            def load_xT(g, h):
                sp.dma_start(xTb[:, h, :, :], xT_store[bass.ds(g * T7, T7), :, :].rearrange("t p d -> p t d")).then_inc(xT_in[h], 16)

            def stage_loads(j, h, more_xT, more_x):
                if more_xT:
                    sp.wait_ge(x1T_ps, j * T7)
                    sp.wait_ge(x1_kept, j)
                    load_xT(j + 1, 1 - h)
                sp.wait_ge(xt1_copied, j * T7)
                sp.dma_start(rows_of(xt_table, (j - 1) * T7, T7), xto[:, 1 - h, :, 0:XW]).then_inc(table_out[1 - h], 16)
                sp.dma_start(rows_of(al_table, (j - 1) * T7, T7), xto[:, 1 - h, :, XW:WW]).then_inc(table_out[1 - h], 16)
                if more_x:
                    sp.wait_ge(y_added, (j + 1) * T7)
                    load_x(h, j + 2, x2_in)
            sp.wait_ge(state_stored, S)
            for h in range(2):
                load_xT(h, h)
                load_x(h, h, x2_in)
            sp.wait_ge(y_added, T7)
            load_x(0, 2, x2_in)
            stage_loads(1, 1, True, True)
            with nc.sync.Fori(1, NG7 // 2 - 2) as i:
                stage_loads(2 * i, 0, True, True)
                stage_loads(2 * i + 1, 1, True, True)
            stage_loads(NG7 - 4, 0, True, True)
            stage_loads(NG7 - 3, 1, True, True)
            stage_loads(NG7 - 2, 0, True, False)
            stage_loads(NG7 - 1, 1, False, False)
            stage_loads(NG7, 0, False, False)
            with nc.sync.Fori(0, NG7 // 2 - 1) as i:
                for h in range(2):
                    g = 2 * i + h
                    sp.wait_ge(out_ready, g + 1)
                    sp.dma_start(rows_of(out, g * T7, T7), x1[:, bass.ds(g * T7, T7), :]).then_inc(out_sent[h], 16)
            sp.wait_ge(out_ready, NG7 - 1)
            g = NG7 - 2
            sp.dma_start(rows_of(out, g * T7, T7), x1[:, bass.ds(g * T7, T7), :]).then_inc(out_sent[0], 16)
            sp.wait_ge(out_ready, NG7)
            g = NG7 - 1
            sp.dma_start(rows_of(out, g * T7, T7 - 1), x1[:, g * T7:NT - 1, :]).then_inc(out_sent[1], 16)
            sp.dma_start(out[N - LASTN:N, :], x1[0:LASTN, NT - 1, :]).then_inc(out_sent[1], 16)
            sp.wait_ge(out_sent[0], 16 * (NG7 // 2))
            sp.wait_ge(out_sent[1], 16 * (NG7 // 2 + 1))
            sp.wait_ge(z_out, 16 * NG7)

        @block.gpsimd
        def _(pool):
            nc.gpsimd.iota(iota_i[:, :], [[1, P]], base=0, channel_multiplier=0).then_inc(iotas, 1)
            nc.gpsimd.iota(stepno_i[:, :], [[P, SG]], base=0, channel_multiplier=1).then_inc(iotas, 1)
            pool.wait_ge(iotas, 2)
            nc.gpsimd.iota(arow, [[0, S // NSPARE], [1, NSPARE]], base=NT + 1, channel_multiplier=0).then_inc(iotas, 1)
            pool.wait_ge(walk_ready, 1)
            pool.wait_ge(rows_out, 32)
            for table, tile in ((dst_rows, dst_step), (src_rows, src_step)):
                for g in range(SG):
                    pool.indirect_dma_start(tile[:, g, :], None, table,
                                            bass.IndirectOffsetOnAxis(ap=istep_i[:, g:g + 1], axis=0)).then_inc(tiles_gathered, 16)
            pool.wait_ge(z_out, 16 * NG7)

            def gather_block(h, free):
                for g in range(NG):
                    if free is not None:
                        pool.wait_ge(parts_ready, free + g + 1)
                        nc.gpsimd.nop(nofuse=True)
                    for j in range(g * G, (g + 1) * G):
                        pool.indirect_dma_start(zs[:, h, j, 0:KR], None, z_table,
                                                bass.IndirectOffsetOnAxis(ap=sidx[:, h, j:j + 1], axis=0)).then_inc(gathered[h][g], 16)
            for b in range(2):
                pool.wait_ge(idx_ready, b + 1)
                gather_block(b, None)
            with nc.gpsimd.Fori(1, NB // 2) as i:
                for h in range(2):
                    pool.wait_ge(idx_ready, 2 * i + h + 1)
                    nc.gpsimd.nop(nofuse=True)
                    gather_block(h, (2 * i + h - 2) * NG)
            def normalise_sums(g, h):
                nc.gpsimd.tensor_tensor(agn[:, h, :, :].rearrange("p t (k r) -> p t k r", r=R),
                                        acc[:, bass.ds(g * T7, T7), 0:KR].rearrange("p t (k r) -> p t k r", r=R),
                                        spread(rec[:, h, :, :].rearrange("p t (k a) -> p t k a", a=1), 3, R), ALU.mult).then_inc(agn_ready, 1)

            def keep_rows(g, h):
                pool.wait_ge(x1_ready, (g + 1) * T7)
                nc.gpsimd.tensor_copy(x1[:, bass.ds(g * T7, T7), :], xTb[:, h, :, :]).then_inc(x1_kept, 1)

            for g in range(2):
                pool.wait_ge(rec_ready, g + 1)
                normalise_sums(g, g)
            with nc.gpsimd.Fori(0, NG7 // 2 - 1) as i:
                for h in range(2):
                    g = 2 * i + h
                    pool.wait_ge(aT_ps, 2 * (g + 1))
                    pool.wait_ge(rec_ready, g + 3)
                    normalise_sums(g + 2, h)
                    keep_rows(g, h)
            for h in range(2):
                keep_rows(NG7 - 2 + h, h)
            for h in range(2):
                pool.wait_ge(table_out[h], 32 * (NG7 // 2))
            for g in range(NG7):
                h = g % 2
                if g >= 2:
                    pool.wait_ge(xg_used, g - 1)
                for t in range(T7):
                    n = g * T7 + t
                    pool.indirect_dma_start(algat[:, h, t, :], None, al_table,
                                            bass.IndirectOffsetOnAxis(ap=src1[:, n:n + 1], axis=0)).then_inc(al_in[h], 16)
                    pool.indirect_dma_start(xto[:, h, t, 0:XW], None, xt_table,
                                            bass.IndirectOffsetOnAxis(ap=dst1[:, n:n + 1], axis=0)).then_inc(xg_in[h], 16)

        @block.vector
        def _(dve):
            vn = Count()
            PERIOD_STEPS = 3 + 10 + 3
            V = nc.vector
            V.memset(dst_sb[:, SG - 1, :], PAD)
            V.memset(src_sb[:, SG - 1, :], 0).then_inc(pads_set, 1)
            V.memset(ones[:, :], 1.0).then_inc(v_step, 1)
            vn.next()
            V.memset(relu_bias[:, :], -ETA * LAM)
            V.memset(rnext[0:1, P - K:P], 0.0)
            V.memset(backx[0:1, P - K:P], NEG)
            V.memset(z3[:, NT, :, :], 0.0)
            V.memset(carry[0:1, P:P + K], NEG).then_inc(v_step, 1)
            vn.next()
            dve.wait_ge(iotas, 2)
            V.tensor_copy(iota_b[:, :], iota_i[:, :])
            V.tensor_copy(iota_row[:, :], iota_i[:, :]).then_inc(v_step, 1)
            dve.wait_ge(v_step, vn.next())
            V.tensor_copy(stepno[:, :], stepno_i[:, :]).then_inc(v_step, 1)
            dve.wait_ge(v_step, vn.next())
            V.tensor_copy(pno[:, 0:1], stepno[:, 0:1])
            V.tensor_scalar(pno[:, 1:2], stepno[:, 0:1], 1.0, None, ALU.add)
            V.tensor_scalar(pno[:, 2:3], stepno[:, 0:1], float(P - 1), None, ALU.subtract).then_inc(v_step, 1)
            dve.wait_ge(v_step, vn.next())
            V.tensor_scalar(ident[:, :], iota_row[:, :], pno[:, 0:1], None, ALU.is_equal)
            V.tensor_scalar(ident_b[:, :], iota_row[:, :], pno[:, 0:1], None, ALU.is_equal)
            V.tensor_scalar(shift[:, :], iota_row[:, :], pno[:, 1:2], None, ALU.is_equal)
            V.tensor_scalar(corner[:, :], iota_row[:, :], pno[:, 2:3], None, ALU.is_equal).then_inc(consts, 1)
            dve.wait_ge(consts, 1)

            dve.wait_ge(edges_in, 96)
            V.tensor_scalar(lastt_i[:, :], dst_sb[:, :, P - 1], 7, None, ALU.arith_shift_right).then_inc(v_step, 1)
            dve.wait_ge(v_step, vn.next())
            V.tensor_tensor(lastt[:, :], lastt_i[:, :], stepno[:, :], ALU.add).then_inc(v_step, 1)
            dve.wait_ge(v_step, vn.next())
            for g in range(SG):
                last = V.tensor_scalar(diag[:, g * P:(g + 1) * P], ident[:, :], lastt[:, g:g + 1], None, ALU.mult)
            last.then_inc(diag_ready, 1)
            for g in range(0, SG, 4):
                n = min(4, SG - g) * P
                dve.wait_ge(bcast_ready, g // 4 + 1)
                last = V.tensor_copy(ulast[:, g * P:g * P + n], psum[4 + g // 4][:, 0:n])
            last.then_inc(v_step, 1)
            dve.wait_ge(v_step, vn.next())
            for g in range(SG):
                V.tensor_scalar(junk[:, :], ulast[:, :], stepno[:, g:g + 1], 0.0, ALU.is_lt, ALU.add,
                                accum_out=istep[:, g:g + 1]).then_inc(v_step, 1)
                dve.wait_ge(v_step, vn.next())
            V.tensor_copy(istep_i[:, :], istep[:, :]).then_inc(walk_ready, 1)
            V.tensor_tensor(tstep[:, :], stepno[:, :], istep[:, :], ALU.subtract).then_inc(v_step, 1)
            dve.wait_ge(v_step, vn.next())
            V.tensor_scalar(tstep[:, :], tstep[:, :], float(NT), None, ALU.min).then_inc(v_step, 1)
            dve.wait_ge(v_step, vn.next())
            V.tensor_scalar(tneg[:, :], tstep[:, :], -float(P), None, ALU.mult).then_inc(v_step, 1)
            dve.wait_ge(v_step, vn.next())
            dve.wait_ge(tiles_gathered, 32 * SG)
            for g in range(SG):
                last = V.tensor_scalar(dloc[:, g, :], dst_step[:, g, :], tneg[:, g:g + 1], None, ALU.add)
            last.then_inc(v_step, 1)
            dve.wait_ge(v_step, vn.next())
            V.memset(lastcol[:, 0:1], 0.0)
            V.tensor_copy(lastcol[:, 1:SG + 1], dloc[:, :, P - 1]).then_inc(dloc_ready, 1)
            V.tensor_copy(srcf[:, :, :], src_step[:, :, :]).then_inc(dloc_ready, 1)
            dve.wait_ge(dloc_ready, 2)
            V.tensor_scalar(okrow[:, :, :], dloc[:, :, :], 0.0, None, ALU.is_ge).then_inc(v_step, 1)
            dve.wait_ge(v_step, vn.next())
            V.scalar_tensor_tensor(okrow[:, :, :], dloc[:, :, :], float(P - 1), okrow[:, :, :], ALU.is_le, ALU.mult).then_inc(v_step, 1)
            dve.wait_ge(v_step, vn.next())
            dve.wait_ge(plast_ready, 1)
            V.tensor_copy(plast[:, :], psum[7][:, 0:SG]).then_inc(tab_read, 1)
            dve.wait_ge(tab_read, 1)
            V.tensor_tensor(cont[:, :, 1:P], dloc[:, :, 1:P], dloc[:, :, 0:P - 1], ALU.is_equal)
            V.tensor_tensor(cont[:, :, 0], dloc[:, :, 0], plast[:, :], ALU.is_equal).then_inc(v_step, 1)
            dve.wait_ge(v_step, vn.next())
            V.tensor_tensor(cont[:, :, :], cont[:, :, :], okrow[:, :, :], ALU.mult).then_inc(v_step, 1)
            dve.wait_ge(v_step, vn.next())
            V.tensor_scalar(cont[:, :, :], cont[:, :, :], 1.0, -NEG, ALU.subtract, ALU.mult).then_inc(reset_ready, 1)
            for n, table in enumerate((dslot, sslot, trow)):
                dve.wait_ge(tab_ps, n + 1)
                w = 1 if table is trow else P
                for g in range(0, SG, 4):
                    m = min(4, SG - g) * P
                    last = V.tensor_copy(table[0:w, g * P:g * P + m], psum[4 + g // 4][0:w, 0:m])
                last.then_inc(tab_read, 1)
            dve.wait_ge(tab_read, 4)
            V.memset(keeprow[0:1, 0:1], 0.0)
            V.tensor_tensor(keeprow[0:1, 1:S], trow[0:1, 1:S], trow[0:1, 0:S - 1], ALU.is_equal).then_inc(keeprow_ready, 1)
            for n in range(0, S, 512):
                m = min(512, S - n)
                dve.wait_ge(bcast_ready, 5 + n // 512)
                last = V.tensor_copy(keep[:, n:n + m], psum[4 + n // 512][:, 0:m])
            last.then_inc(tab_read, 1)
            dve.wait_ge(iotas, 3)
            V.tensor_copy(spare, arow)
            V.tensor_copy(arowf, trow).then_inc(v_step, 1)
            stays = keeprow.rearrange("a (b j) -> a b j", j=B)
            here = arowf.rearrange("a (b j) -> a b j", j=B)[:, :, 0:B - 1]
            other = spare.rearrange("a (b j) -> a b j", j=B)[:, :, 0:B - 1]
            dve.wait_ge(v_step, vn.next())
            V.tensor_tensor(other, other, here, ALU.subtract).then_inc(v_step, 1)
            dve.wait_ge(v_step, vn.next())
            V.tensor_tensor(other, other, stays[:, :, 1:B], ALU.mult).then_inc(v_step, 1)
            dve.wait_ge(v_step, vn.next())
            V.tensor_tensor(here, here, other, ALU.add).then_inc(v_step, 1)
            dve.wait_ge(v_step, vn.next())
            V.tensor_copy(arow, arowf).then_inc(tab_read, 1)
            for b in range(2):
                V.tensor_copy(sidx[:, b, :], sslot[:, b * B:(b + 1) * B]).then_inc(idx_ready, 1)
            V.tensor_copy(okrow[:, 0, :], dst_sb[:, 0, :])
            V.tensor_copy(okrow[:, 1, :], src_sb[:, 0, :]).then_inc(tab_read, 1)
            dve.wait_ge(tab_ps, 4)
            V.tensor_copy(dst1[:, :], psum[4][:, 0:P])
            V.tensor_copy(src1[:, :], psum[4][:, P:2 * P]).then_inc(tab_read, 1)

            dve.wait_ge(weights_in, 16 * 5)
            V.tensor_reduce(hsum[0:1, 0:1], hw[0:1, 0, :], AX_X, ALU.max).then_inc(v_step, 1)
            dve.wait_ge(v_step, vn.next())
            V.tensor_scalar(hw[0:1, 1, :], hw[0:1, 0, :], hsum[0:1, 0:1], None, ALU.subtract).then_inc(prep_read, 1)
            dve.wait_ge(prep_exp, 1)
            V.tensor_reduce(hsum[0:1, 1:2], hw[0:1, 2, :], AX_X, ALU.add).then_inc(v_step, 1)
            dve.wait_ge(v_step, vn.next())
            V.reciprocal(hsum[0:1, 2:3], hsum[0:1, 1:2]).then_inc(v_step, 1)
            dve.wait_ge(v_step, vn.next())
            V.tensor_scalar(hw[0:1, 1, :], hw[0:1, 2, :], hsum[0:1, 2:3], None, ALU.mult).then_inc(prep_read, 1)
            dve.wait_ge(prep_ps, 1)
            dve.wait_ge(zu_copied, NG7)
            V.tensor_copy(gs[:, :, :].rearrange("p c d -> p (c d)"), psum[4][:, :]).then_inc(prep_read, 1)
            V.tensor_tensor(ur[:, :, :, :].rearrange("p c k r -> p k c r"), ur[:, :, :, :].rearrange("p c k r -> p k c r"),
                            spread(spread(psum[5][:, 0:K].rearrange("p (k a b) -> p k a b", a=1, b=1), 2, DC), 3, R), ALU.mult).then_inc(prep_read, 1)
            dve.wait_ge(prep_ps, 2)
            V.tensor_tensor(mz[:, :, :].rearrange("p c d -> p (c d)"), dm[:, :, :].rearrange("p c d -> p (c d)"), psum[6][:, :], ALU.subtract).then_inc(v_step, 1)
            dve.wait_ge(v_step, vn.next())
            V.tensor_scalar(mz[:, :, :], mz[:, :, :], 0.5 * ETA, None, ALU.mult).then_inc(v_step, 1)
            dve.wait_ge(v_step, vn.next())
            for c in range(DC):
                blk = mz[:, c, c * P:(c + 1) * P]
                last = V.scalar_tensor_tensor(blk, ident[:, :], 0.5, blk, ALU.mult, ALU.add)
            last.then_inc(prep_read, 1)
            wv = wx[:, :, 0:HO].rearrange("p c (h o) -> p c h o", h=H)
            for n in range(2):
                V.tensor_tensor(wtmp[:, :, :].rearrange("p c (h o) -> p c h o", h=H), wv,
                                spread(psum[7][:, n * HO:(n + 1) * HO].rearrange("p (a h o) -> p a h o", a=1, h=H), 1, DC),
                                ALU.mult).then_inc(v_step, 1)
                dve.wait_ge(v_step, vn.next())
                V.tensor_reduce(wx[:, :, HO + n * H:HO + (n + 1) * H], wtmp[:, :, :].rearrange("p c (h o) -> p c h o", h=H),
                                AX_X, ALU.add).then_inc(v_step, 1)
                dve.wait_ge(v_step, vn.next())
            dve.wait_ge(prep_ps, 3)
            V.tensor_copy(w3[:, :], psum[4][0:KR, 0:D]).then_inc(prep_read, 1)
            dve.wait_ge(tab_read, 8)
            dve.wait_ge(resets_out, 16)
            dve.wait_ge(prep_read, 6)

            V.memset(sums[:, :, 0], 0.0)
            V.memset(keepf[:, :, 0], 0.0).then_inc(v_step, 1)
            dve.wait_ge(v_step, vn.next())
            dve.wait_ge(z_out, 16 * NG7)
            for h in range(2):
                dve.wait_ge(xT_out[h], 16 * (NG7 // 2))
            V.memset(resets[:, :, P:P + 1], 0.0).then_inc(v_step, 1)
            dve.wait_ge(v_step, vn.next())
            for s in range(2):
                for half in range(2):
                    ts = slice(half * NT // 2, (half + 1) * NT // 2)
                    dve.wait_ge(z_parts, 2 * s + half + 1)
                    to = zf[:, ts, :] if s == 0 else z3[:, ts, ZP - 1, :]
                    V.tensor_tensor(to, zf[:, ts, :], z3[:, ts, s, :], ALU.subtract).then_inc(z_rest, 1)

            def copy_indices(b, h):
                V.tensor_copy(didx[:, h, :], dslot[:, bass.ds(b * B, B)]).then_inc(v_step, 1)
                dve.wait_ge(v_step, vn.next())

            def make_onehot(b, h, g, reused):
                if reused and g == 0:
                    dve.wait_ge(sums_ps, (b - 1) * (B // Q))
                for j in range(g * G, (g + 1) * G):
                    last = V.tensor_scalar(onehot[:, h, j, :], iota_b[:, :], didx[:, h, j:j + 1], None, ALU.is_equal)
                last.then_inc(onehot_ready, 1)

            def head_products(b, h, g, uses):
                dve.wait_ge(zd_ready, NG * b + g + 1)
                dve.wait_ge(gathered[h][g], 16 * G * uses)
                V.tensor_tensor(prod[:, :, :], zs[:, h, g * G:(g + 1) * G, 0:KR],
                                zd_ps[g % 2][:, :].rearrange("p (j c) -> p j c", j=G), ALU.mult).then_inc(zd_used, 1)
                dve.wait_ge(zd_used, NG * b + g + 1)
                last = V.tensor_reduce(logits[:, h, g * G * K:(g + 1) * G * K], prod[:, :, :].rearrange("p j (k r) -> p (j k) r", r=R),
                                       AX_X, ALU.add)
                if g == NG - 1:
                    last.then_inc(logits_ready, 1)
                else:
                    last.then_inc(v_step, 1)
                    dve.wait_ge(v_step, vn.next())

            def copy_next_indices(b, h):
                V.tensor_copy(sidx[:, h, :], sslot[:, bass.ds(b * B, B)]).then_inc(idx_ready, 1)

            def by_head(row, k):
                return row.rearrange("a (j k) -> a j k", k=K)[:, :, k]

            def scan_steps(b, first, last=False):
                dve.wait_ge(keep_ready, b + 1)
                for c0, c1, r in ((0, KR, R), (KR, AW, 1)):
                    k1 = keepf[:, c0:c1, 1].rearrange("p (k r) -> p k r", r=r)
                    f = fac[:, :].rearrange("p (k a) -> p k a", a=1)
                    scaled = V.scalar_tensor_tensor(k1, spread(f, 2, r) if r > 1 else f, 1.0, k1, ALU.add, ALU.mult)
                scaled.then_inc(v_step, 1)
                dve.wait_ge(v_step, vn.next())
                dve.wait_ge(sums_copied, (b + 1) * (B // Q))
                if not first:
                    dve.wait_ge(state_stored, B * b)
                V.tensor_tensor_scan(state.rearrange("p c j -> p (c j)"), keepf.rearrange("p c j -> p (c j)"),
                                     sums.rearrange("p c j -> p (c j)"), 0.0, ALU.mult, ALU.add).then_inc(scan_done, 1)
                if not last:
                    dve.wait_ge(scan_done, b + 1)
                    V.tensor_copy(sums[:, :, 0], state[:, :, B]).then_inc(v_step, 1)
                    dve.wait_ge(v_step, vn.next())

            def period(b, h, uses, reused=True, more_idx=True, more=True):
                first = type(b) is int and b == 0
                rs = resets[:, h, :]
                rs_rev = rs[:, P:0:-1]

                def next_onehot(g):
                    if more:
                        make_onehot(b + 1, 1 - h, g, reused)
                for g in range(NG):
                    head_products(b, h, g, uses)
                if more_idx:
                    copy_next_indices(b + 2, h)
                dve.wait_ge(resets_in[h], 16 * uses)
                V.tensor_reduce(inmin[:, :], rs[:, 1:P], AX_X, ALU.min)
                dve.wait_ge(lt_ready, b + 1)
                V.tensor_tensor_scan(fwd0, rs[:, 0:P], mid_ps[:, 0:P], NEG, ALU.add, ALU.max).then_inc(ends_ready, 1)
                if more:
                    copy_indices(b + 1, 1 - h)
                next_onehot(0)
                dve.wait_ge(ends_row, b + 1)
                V.tensor_copy(rows[0:1, :, :].rearrange("a n q -> a (n q)"), row_ps[0:1, 0:3 * P])
                V.tensor_copy(carry[0:1, 0:K], carry[0:1, P:P + K]).then_inc(v_step, 1)
                dve.wait_ge(v_step, vn.next())
                V.tensor_tensor(rmin[0:1, :], rows[0:1, 1, :], rows[0:1, 2, :], ALU.min)
                V.tensor_tensor(rnext[0:1, 0:P - K], rows[0:1, 1, 0:P - K], rows[0:1, 2, K:P], ALU.add).then_inc(v_step, 1)
                dve.wait_ge(v_step, vn.next())
                for k in range(K):
                    last = V.tensor_tensor_scan(by_head(carry[0:1, K:P + K], k), by_head(rmin[0:1, :], k), by_head(rows[0:1, 0, :], k),
                                                carry[0:1, k:k + 1], ALU.add, ALU.max)
                last.then_inc(carry_ready, 1)
                next_onehot(1)
                dve.wait_ge(carry_col, b + 1)
                V.tensor_copy(ccol[:, :], row_ps[:, 384:385]).then_inc(v_step, 1)
                dve.wait_ge(v_step, vn.next())
                V.tensor_tensor_scan(fwd, rs[:, 0:P], mid_ps[:, 0:P], ccol[:, :], ALU.add, ALU.max).then_inc(v_step, 1)
                dve.wait_ge(v_step, vn.next())
                V.tensor_tensor_scan(rev0[:, ::-1], rs_rev, fwd[:, ::-1], NEG, ALU.add, ALU.max).then_inc(heads_ready, 1)
                next_onehot(2)
                dve.wait_ge(heads_row, b + 1)
                for k in range(K):
                    last = V.tensor_tensor_scan(by_head(back[0:1, :], k)[:, ::-1], by_head(rnext[0:1, :], k)[:, ::-1],
                                                by_head(row_ps[0:1, 0:P], k)[:, ::-1], NEG, ALU.add, ALU.max)
                last.then_inc(v_step, 1)
                dve.wait_ge(v_step, vn.next())
                V.tensor_tensor(backx[0:1, 0:P - K], back[0:1, K:P], rows[0:1, 2, K:P], ALU.add).then_inc(back_ready, 1)
                V.tensor_tensor(ratio[0:1, 0, :], carry[0:1, 0:K], rows[0:1, 2, 0:K], ALU.add).then_inc(v_step, 1)
                next_onehot(3)
                dve.wait_ge(v_step, vn.next())
                V.tensor_tensor(ratio[0:1, 0, :], ratio[0:1, 0, :], back[0:1, 0:K], ALU.subtract)
                dve.wait_ge(back_col, b + 1)
                V.tensor_copy(dcol[:, :], row_ps[:, 385:386]).then_inc(v_step, 1)
                dve.wait_ge(v_step, vn.next())
                V.tensor_tensor_scan(rev[:, ::-1], rs_rev, fwd[:, ::-1], dcol[:, :], ALU.add, ALU.max).then_inc(v_step, 1)
                dve.wait_ge(v_step, vn.next())
                V.tensor_tensor(xexp, mid_ps[:, 0:P], rev, ALU.subtract).then_inc(x_ready, 1)
                if not first:
                    scan_steps(b - 1, type(b) is int and b == 1)
                dve.wait_ge(et_ready, b + 1)
                V.tensor_copy(zs[:, h, :, KR:AW], mid_ps[:, 0:P].rearrange("p (j k) -> p j k", k=K)).then_inc(v_step, 1)
                dve.wait_ge(v_step, vn.next())
                for g in range(NG):
                    z = zs[:, h, g * G:(g + 1) * G, 0:KR].rearrange("p j (k r) -> p j k r", r=R)
                    w = spread(zs[:, h, g * G:(g + 1) * G, KR:AW].rearrange("p j (k a) -> p j k a", a=1), 3, R)
                    V.tensor_tensor(z, z, w, ALU.mult).then_inc(weighted, 1)
                dve.wait_ge(scale_ready, b + 1)
                V.tensor_scalar(fac[:, :], row_ps[:, 386:386 + K], 1.0, first_col[:, h:h + 1], ALU.subtract, ALU.mult).then_inc(v_step, 1)
                dve.wait_ge(v_step, vn.next())
                for s, rounded, left in ((0, hi_ready, rest_ready), (1, mid_ready, parts_ready)):
                    for g in range(NG):
                        js = slice(g * G, (g + 1) * G)
                        dve.wait_ge(rounded, NG * b + g + 1)
                        V.tensor_tensor(zs[:, h, js, :] if s == 0 else wparts[:, js, ZP - 1, :], zs[:, h, js, :], wparts[:, js, s, :],
                                        ALU.subtract).then_inc(left, 1)

            copy_indices(0, 0)
            for g in range(NG):
                make_onehot(0, 0, g, False)
            period(0, 0, 1, reused=False)
            period(1, 1, 1)
            with nc.vector.Fori(1, NB // 2 - 1) as i:
                vn.loop(i - 1, 2 * PERIOD_STEPS)
                for h in range(2):
                    period(2 * i + h, h, i + 1)
                vn.end(NB // 2 - 2)
            period(NB - 2, 0, NB // 2, more_idx=False)
            period(NB - 1, 1, NB // 2, more_idx=False, more=False)
            scan_steps(NB - 1, False, last=True)

            dve.wait_ge(state_stored, S)

            def sums_reciprocal(g, h):
                V.tensor_scalar(rec[:, h, :, :], acc[:, bass.ds(g * T7, T7), KR:AW], 1e-16, None, ALU.add).then_inc(v_step, 1)
                dve.wait_ge(v_step, vn.next())
                V.reciprocal(rec[:, h, :, :], rec[:, h, :, :]).then_inc(rec_ready, 1)

            def inverse_variance(h, ready):
                V.tensor_scalar(rstd[:, h, :, 2], mv[:, h, :, 1], EPS, None, ALU.add).then_inc(v_step, 1)
                dve.wait_ge(v_step, vn.next())
                V.reciprocal(rstd[:, h, :, 2], rstd[:, h, :, 2]).then_inc(ready, 1)

            def norm_bias(h, g, rooted, ready):
                dve.wait_ge(rooted, g + 1)
                V.scalar_tensor_tensor(rstd[:, h, :, 1], mv[:, h, :, 0], -1.0, rstd[:, h, :, 0], ALU.mult, ALU.mult).then_inc(ready, 1)

            def dense_tile(g, h, t):
                n = g * T7 + t
                dve.wait_ge(relu_done, n + 1)
                V.tensor_tensor(xTb[:, h, t, :], xin[:, h, t, :], xTb[:, h, t, :], ALU.add).then_inc(y_added, 1)
                dve.wait_ge(y_added, n + 1)
                V.nop(nofuse=True)
                V.bn_stats(stats[:, t, :], xTb[:, h, t, :]).then_inc(v_step, 1)
                dve.wait_ge(v_step, vn.next())
                V.nop(nofuse=True)
                last = V.bn_aggr(mv[:, h, t, :], stats[:, t, :])
                if t == T7 - 1:
                    last.then_inc(v_step, 1)
                    dve.wait_ge(v_step, vn.next())
                    inverse_variance(h, var_ready)

            def copy_sums(j, h):
                for q in range(2):
                    dve.wait_ge(aT_ps, 2 * j + q + 1)
                    n = 4 if q == 0 else T7 - 4
                    V.tensor_copy(aT[h][:, q * 4 * P:(q * 4 + n) * P], psum[q][0:KR, 0:n * P]).then_inc(aT_ready, 1)

            def stage(j, h, dense, tables, more, two_parts=False, next_sums=True):
                if tables:
                    norm_bias(1 - h, j - 1, rstd_ready, nb_ready)
                if dense:
                    dve.wait_ge(x2_in[h], 16 * ((j - h) // 2 + 1) + (16 if two_parts else 0) if type(j) is int else X2_IN(j, h))
                    for t in range(DENSE_FIRST):
                        dense_tile(j, h, t)
                if tables:
                    for t in range(T7):
                        n = (j - 1) * T7 + t
                        dve.wait_ge(x1T_ps, n + 1)
                        V.tensor_copy(x1T[:, (1 - h + t) % 2, :], psum[4 + (1 - h + t) % 2][:, 0:D]).then_inc(x1T_ready, 1)
                if dense and next_sums:
                    copy_sums(j + 1, 1 - h)
                if dense:
                    for t in range(DENSE_FIRST, T7):
                        dense_tile(j, h, t)
                if more:
                    dve.wait_ge(agn_ready, j + 1)
                    sums_reciprocal(j + 2, h)

            for g in range(2):
                sums_reciprocal(g, g)
            copy_sums(0, 0)
            stage(0, 0, True, False, True)
            stage(1, 1, True, True, True)
            with nc.vector.Fori(1, NG7 // 2 - 1) as i:
                X2_IN = lambda j, h: 16 * (i + 1)
                vn.loop(i - 1, 2 * (T7 + 3))
                for h in range(2):
                    stage(2 * i + h, h, True, True, True)
                vn.end(NG7 // 2 - 2)
            stage(NG7 - 2, 0, True, True, False)
            stage(NG7 - 1, 1, True, True, False, two_parts=True, next_sums=False)
            stage(NG7, 0, False, True, False)

            def attend_group(i, h, first=False):
                g = 2 * i + h
                z = lg[:, h, :, :]
                rowsg = xto[:, h, :, 0:HO].rearrange("p t (h o) -> p t h o", h=H)
                dve.wait_ge(al_in[h], 16 * T7 * (i + 1))
                dve.wait_ge(xg_in[h], 16 * T7 * (i + 1))
                V.tensor_tensor(z, algat[:, h, :, :], xto[:, h, :, HO:XW], ALU.add).then_inc(v_step, 1)
                dve.wait_ge(v_step, vn.next())
                V.scalar_tensor_tensor(z, z, 0.01, z, ALU.mult, ALU.max).then_inc(v_step, 1)
                dve.wait_ge(v_step, vn.next())
                V.tensor_reduce(lmax[:, :, 0:1], z, AX_X, ALU.max).then_inc(v_step, 1)
                dve.wait_ge(v_step, vn.next())
                V.tensor_tensor(z, z, spread(lmax[:, :, 0:1], 2, H), ALU.subtract).then_inc(lg_ready, 1)
                if not first:
                    norm_bias(1 - h, g - 1, rstd2_ready, nb2_ready)
                dve.wait_ge(lg_exp, g + 1)
                V.tensor_reduce(lmax[:, :, 0:1], z, AX_X, ALU.add).then_inc(v_step, 1)
                dve.wait_ge(v_step, vn.next())
                V.reciprocal(lmax[:, :, 1:2], lmax[:, :, 0:1]).then_inc(v_step, 1)
                dve.wait_ge(v_step, vn.next())
                V.tensor_tensor(z, z, spread(lmax[:, :, 1:2], 2, H), ALU.mult).then_inc(v_step, 1)
                dve.wait_ge(v_step, vn.next())
                V.tensor_tensor(rowsg, rowsg, spread(z.rearrange("p t (h a) -> p t h a", a=1), 3, O), ALU.mult).then_inc(v_step, 1)
                dve.wait_ge(v_step, vn.next())
                V.tensor_reduce(tmp[:, :, :], rowsg.rearrange("p t h o -> p t o h"), AX_X, ALU.add).then_inc(xg_used, 1)
                dve.wait_ge(xg_used, g + 1)
                y = x1[:, bass.ds(g * T7, T7), :]
                V.tensor_tensor(y.rearrange("p t (h o) -> p t h o", h=H), y.rearrange("p t (h o) -> p t h o", h=H),
                                spread(tmp[:, :, :].rearrange("p t (a o) -> p t a o", a=1), 2, H), ALU.add).then_inc(v_step, 1)
                dve.wait_ge(v_step, vn.next())
                V.nop(nofuse=True)
                for t in range(T7):
                    last = V.bn_stats(stats[:, t, :], x1[:, bass.ds(g * T7 + t, 1), :].rearrange("p a d -> p (a d)"))
                last.then_inc(v_step, 1)
                dve.wait_ge(v_step, vn.next())
                V.nop(nofuse=True)
                for t in range(T7):
                    last = V.bn_aggr(mv[:, h, t, :], stats[:, t, :])
                last.then_inc(v_step, 1)
                dve.wait_ge(v_step, vn.next())
                inverse_variance(h, var2_ready)

            dve.wait_ge(x1_kept, NG7)
            for g in range(2):
                attend_group(0, g, g == 0)
            with nc.vector.Fori(1, NG7 // 2) as i:
                vn.loop(i - 1, 2 * 11)
                for h in range(2):
                    attend_group(i, h)
                vn.end(NG7 // 2 - 1)
            norm_bias(1, NG7 - 1, rstd2_ready, nb2_ready)

        @block.tensor
        def _(pe):
            T = nc.tensor

            def steps_of(b, g):
                _, tiles = nc.values_load_multi_w_load_instructions(
                    trow[0:1, bass.ds(b * B + g * G, G)], engines=[mybir.EngineType.PE], min_val=0, max_val=NT,
                    skip_runtime_bounds_check_because="the vector engine has clamped the node tile")
                return tiles

            pe.wait_ge(diag_ready, 1)
            for g in range(SG):
                last = T.matmul(psum[4 + g // 4][:, (g % 4) * P:(g % 4 + 1) * P], ones[:, :], diag[:, g * P:(g + 1) * P], start=True, stop=True)
                if g % 4 == 3 or g == SG - 1:
                    last.then_inc(bcast_ready, 1)

            def transpose_x(h, t, r):
                for c in range(DC):
                    last = T.transpose(psum[r][:, c * P:(c + 1) * P], xin[:, h, t, c * P:(c + 1) * P], ident[:, :])
                last.then_inc(xt_ps, 1)

            def project(i, first, last_one):
                for m in range(2 * T7):
                    h, t, r = m // T7, m % T7, m % 2
                    n = 2 * T7 * i + m
                    if m + 1 < 2 * T7:
                        if m + 1 == T7:
                            pe.wait_ge(x_in[1], 16 * (i + 1) + (16 if last_one else 0))
                        transpose_x((m + 1) // T7, (m + 1) % T7, (m + 1) % 2)
                    elif not last_one:
                        pe.wait_ge(x_in[0], 16 * (i + 2))
                        transpose_x(0, 0, 0)
                    if t == 0 and not first:
                        pe.wait_ge(zu_copied, 2 * i + h - 1)
                    pe.wait_ge(xt_copied, n + 1)
                    for c in range(DC):
                        last = T.matmul(psum[2 + h][:, t * KR:(t + 1) * KR], xTb[:, h, t, c * P:(c + 1) * P],
                                        ur[:, c, :, :].rearrange("p k r -> p (k r)"), start=(c == 0), stop=(c == DC - 1))
                    if t == T7 - 1:
                        last.then_inc(zu_ps, 1)

            pe.wait_ge(consts, 1)
            pe.wait_ge(u_in, 16 * DC)
            pe.wait_ge(x_in[0], 16)
            transpose_x(0, 0, 0)
            project(0, True, False)
            with nc.tensor.Fori(1, NG7 // 2 - 1) as i:
                project(i, False, False)
            project(NG7 // 2 - 1, False, True)

            pe.wait_ge(dloc_ready, 2)
            T.matmul(psum[7][:, 0:SG], shift[:, :], lastcol[:, 1:SG + 1], start=True, stop=False)
            T.matmul(psum[7][:, 0:SG], corner[:, :], lastcol[:, 0:SG], start=False, stop=True).then_inc(plast_ready, 1)
            for n, table in enumerate((dloc, srcf)):
                pe.wait_ge(tab_read, n + 1)
                for g in range(SG):
                    last = T.transpose(psum[4 + g // 4][:, (g % 4) * P:(g % 4 + 1) * P], table[:, g, :], ident[:, :])
                last.then_inc(tab_ps, 1)
            pe.wait_ge(tab_read, 3)
            for g in range(SG):
                last = T.matmul(psum[4 + g // 4][0:1, (g % 4) * P:(g % 4 + 1) * P], tstep[:, g:g + 1], ident[:, :], start=True, stop=True)
            last.then_inc(tab_ps, 1)
            pe.wait_ge(keeprow_ready, 1)
            for n in range(0, S, 512):
                m = min(512, S - n)
                T.matmul(psum[4 + n // 512][:, 0:m], ones[0:1, :], keeprow[0:1, n:n + m], start=True, stop=True).then_inc(bcast_ready, 1)
            pe.wait_ge(tab_read, 7)
            T.transpose(psum[4][:, 0:P], okrow[:, 0, :], ident[:, :])
            T.transpose(psum[4][:, P:2 * P], okrow[:, 1, :], ident[:, :]).then_inc(tab_ps, 1)

            pe.wait_ge(weights_in, 16 * 5)
            pe.wait_ge(tab_read, 8)
            T.matmul(psum[7][:, :], ones[0:1, :], attn[0:1, :], start=True, stop=True)
            for a in range(DC):
                for c in range(DC):
                    T.matmul(psum[4][:, a * D:(a + 1) * D], dm[:, c, a * P:(a + 1) * P], dm[:, c, :], start=(c == 0), stop=(c == DC - 1))
            pe.wait_ge(prep_read, 2)
            T.matmul(psum[5][:, 0:K], ones[0:1, :], hw[0:1, 1, :], start=True, stop=True).then_inc(prep_ps, 1)
            pe.wait_ge(prep_read, 3)
            for a in range(DC):
                for c in range(DC):
                    last = T.matmul(psum[6][:, a * D:(a + 1) * D], gs[:, c, a * P:(a + 1) * P], dm[:, c, :], start=(c == 0), stop=(c == DC - 1))
            last.then_inc(prep_ps, 1)
            pe.wait_ge(prep_read, 5)
            for c in range(DC):
                last = T.matmul(psum[4][0:KR, 0:D], ur[:, c, :, :].rearrange("p k r -> p (k r)"), mz[:, c, :], start=(c == 0), stop=(c == DC - 1))
            last.then_inc(prep_ps, 1)
            pe.wait_ge(prep_read, 6)

            def transpose_onehots(b, h, g):
                if g >= 2 or not (type(b) is int and b == 0):
                    pe.wait_ge(oneT_ready, NG * b + g - 1)
                pe.wait_ge(onehot_ready, NG * b + g + 1)
                for u in range(G):
                    last = T.transpose(tr_ps[g % 2][:, u * P:(u + 1) * P], onehot[:, h, g * G + u, :], ident_b[:, :])
                last.then_inc(oneT_ps, 1)

            def expand(b, g):
                tiles = steps_of(b, g)
                if g >= 2 or not (type(b) is int and b == 0):
                    pe.wait_ge(zd_used, NG * b + g - 1)
                pe.wait_ge(oneT_ready, NG * b + g + 1)
                for u in range(G):
                    for s in range(ZP):
                        last = T.matmul(zd_ps[g % 2][:, u * KR:(u + 1) * KR], onehotT[:, g * G + u, :],
                                        z3[:, bass.ds(tiles[u], 1), s, :].rearrange("p a c -> p (a c)"), start=(s == 0), stop=(s == ZP - 1))
                last.then_inc(zd_ready, 1)

            def add_up(b, h, q0, q1):
                for q in range(q0, q1):
                    if q >= 2 or not (type(b) is int and b == 0):
                        pe.wait_ge(sums_copied, (B // Q) * b + q - 1)
                    if q % 2 == 0:
                        pe.wait_ge(parts_ready, NG * b + q // 2 + 1)
                    for u in range(q * Q, (q + 1) * Q):
                        for s in range(ZP):
                            last = T.matmul(sum_ps[q % 2][:, (u % Q) * AW:(u % Q + 1) * AW], onehot[:, h, u, :], wparts[:, u, s, :],
                                            start=(s == 0), stop=(s == ZP - 1))
                    last.then_inc(sums_ps, 1)

            def period(b, h, more=True):
                def next_transposes(g):
                    if more:
                        transpose_onehots(b + 1, 1 - h, g)
                pe.wait_ge(logits_ready, b + 1)
                T.transpose(mid_ps[:, 0:P], logits[:, h, :], ident[:, :]).then_inc(lt_ready, 1)
                pe.wait_ge(ends_ready, b + 1)
                T.matmul(row_ps[0:1, 0:P], fwd0[:, P - 1:P], ident[:, :], start=True, stop=True)
                T.matmul(row_ps[0:1, P:2 * P], inmin[:, :], ident[:, :], start=True, stop=True)
                T.matmul(row_ps[0:1, 2 * P:3 * P], resets[:, h, 0:1], ident[:, :], start=True, stop=True).then_inc(ends_row, 1)
                next_transposes(0)
                pe.wait_ge(carry_ready, b + 1)
                T.matmul(row_ps[:, 384:385], carry[0:1, 0:P], ones[0:1, 0:1], start=True, stop=True).then_inc(carry_col, 1)
                next_transposes(1)
                pe.wait_ge(heads_ready, b + 1)
                T.matmul(row_ps[0:1, 0:P], rev0[:, 0:1], ident[:, :], start=True, stop=True).then_inc(heads_row, 1)
                next_transposes(2)
                pe.wait_ge(back_ready, b + 1)
                T.matmul(row_ps[:, 385:386], backx[0:1, :], ones[0:1, 0:1], start=True, stop=True).then_inc(back_col, 1)
                next_transposes(3)
                pe.wait_ge(e_ready, b + 1)
                T.transpose(mid_ps[:, 0:P], eexp, ident[:, :]).then_inc(et_ready, 1)
                pe.wait_ge(ratio_ready, b + 1)
                T.matmul(row_ps[:, 386:386 + K], ones[0:1, :], ratio[0:1, 1, :], start=True, stop=True).then_inc(scale_ready, 1)
                if more:
                    expand(b + 1, 0)
                    expand(b + 1, 1)
                add_up(b, h, 0, 4)
                if more:
                    expand(b + 1, 2)
                add_up(b, h, 4, 6)
                if more:
                    expand(b + 1, 3)
                add_up(b, h, 6, 8)

            for g in range(NG):
                transpose_onehots(0, 0, g)
            pe.wait_ge(z_rest, 4)
            for g in range(NG):
                expand(0, g)
            period(0, 0)
            period(1, 1)
            with nc.tensor.Fori(1, NB // 2 - 1) as i:
                for h in range(2):
                    period(2 * i + h, h)
            period(NB - 2, 0)
            period(NB - 1, 1, more=False)

            def dense_tile(g, h, t, first):
                n = g * T7 + t
                r = (h + t) % 2
                if t >= 2 or not first:
                    pe.wait_ge(relu_done, n - 1)
                ps = psum[2 + r][:, 0:D]
                for c in range(DC):
                    T.matmul(ps, xTb[:, h, t, c * P:(c + 1) * P], mz[:, c, :], start=(c == 0), stop=False)
                if t % 4 == 0:
                    pe.wait_ge(aT_ready, 2 * g + t // 4 + 1)
                T.matmul(ps, aT[h][:, t * P:(t + 1) * P], w3[:, :], start=False, stop=True).then_inc(y_ps, 1)

            def transpose_sums(j, h):
                pe.wait_ge(agn_ready, j + 1)
                if not (type(j) is int and j == 0):
                    pe.wait_ge(aT_ready, 2 * j)
                T.nop(nofuse=True)
                for t in range(T7):
                    last = T.transpose(psum[t // 4][0:KR, (t % 4) * P:(t % 4 + 1) * P], agn[:, h, t, :], ident[:, :])
                    if t in (3, T7 - 1):
                        last.then_inc(aT_ps, 1)

            def transpose_x1(h, t, r):
                for c in range(DC):
                    last = T.transpose(psum[4 + r][:, c * P:(c + 1) * P], xTb[:, h, t, c * P:(c + 1) * P], ident[:, :])
                last.then_inc(x1T_ps, 1)

            def table_tiles(g, h, first):
                for t in range(T7):
                    n = g * T7 + t
                    r = (h + t) % 2
                    if t == 0:
                        pe.wait_ge(x1_ready, n + 1)
                        transpose_x1(h, 0, r)
                    if t + 1 < T7:
                        pe.wait_ge(x1_ready, n + 2)
                        transpose_x1(h, t + 1, 1 - r)
                    if t >= 2 or not first:
                        pe.wait_ge(xt1_copied, n - 1)
                    pe.wait_ge(x1T_ready, n + 1)
                    for c in range(DC):
                        last = T.matmul(psum[6 + r][:, 0:WW], x1T[:, r, c * P:(c + 1) * P], wx[:, c, :], start=(c == 0), stop=(c == DC - 1))
                    last.then_inc(xt1_ps, 1)

            def stage(j, h, xT_loads, dense, tables, next_sums=True):
                if dense:
                    pe.wait_ge(xT_in[h], 16 * xT_loads)
                    for t in range(DENSE_FIRST):
                        dense_tile(j, h, t, not tables)
                    if next_sums:
                        transpose_sums(j + 1, 1 - h)
                if tables:
                    table_tiles(j - 1, 1 - h, type(j) is int and j == 1)
                if dense:
                    for t in range(DENSE_FIRST, T7):
                        dense_tile(j, h, t, not tables)

            transpose_sums(0, 0)
            stage(0, 0, 1, True, False)
            stage(1, 1, 1, True, True)
            with nc.tensor.Fori(1, NG7 // 2 - 1) as i:
                for h in range(2):
                    stage(2 * i + h, h, i + 1, True, True)
            stage(NG7 - 2, 0, NG7 // 2, True, True)
            stage(NG7 - 1, 1, NG7 // 2, True, True, next_sums=False)
            stage(NG7, 0, 0, False, True)

        @block.scalar
        def _(act):
            A = nc.scalar

            def project(i, first):
                for m in range(2 * T7):
                    h, t, r = m // T7, m % T7, m % 2
                    g = 2 * i + h
                    if t == 0 and not first:
                        act.wait_ge(xT_out[h], 16 * i)
                    act.wait_ge(xt_ps, 2 * T7 * i + m + 1)
                    A.activation(xTb[:, h, t, :], psum[r][:, 0:D], ACT.Copy).then_inc(xt_copied, 1)
                    if t == T7 - 1:
                        act.wait_ge(zu_ps, g + 1)
                        A.activation(zf[:, bass.ds(g * T7, T7), :].rearrange("p t c -> p (t c)"), psum[2 + h][:, 0:T7 * KR],
                                     ACT.Copy).then_inc(zu_copied, 1)
            project(0, True)
            with nc.scalar.Fori(1, NG7 // 2) as i:
                project(i, False)
            act.wait_ge(prep_read, 1)
            A.activation(hw[0:1, 2, :], hw[0:1, 1, :], ACT.Exp).then_inc(prep_exp, 1)

            for s in range(2):
                for half in range(2):
                    ts = slice(half * NT // 2, (half + 1) * NT // 2)
                    if s == 1:
                        act.wait_ge(z_rest, half + 1)
                    else:
                        act.wait_ge(zu_copied, NG7)
                    A.activation(z3[:, ts, s, :], zf[:, ts, :], ACT.Copy).then_inc(z_parts, 1)

            def store_states(b, g):
                _, tiles = nc.values_load_multi_w_load_instructions(
                    arow[0:1, bass.ds(b * B + g * G, G)], engines=[mybir.EngineType.Activation], min_val=0, max_val=NT + NSPARE,
                    skip_runtime_bounds_check_because="the vector engine has clamped the node tile")
                if g == 0:
                    act.wait_ge(scan_done, b + 1)
                    if not (type(b) is int and b == 0):
                        act.wait_ge(state_stored, B * b)
                for u in range(g * G, (g + 1) * G):
                    if u >= NSPARE:
                        act.wait_ge(state_stored, B * b + u - NSPARE + 1)
                    A.activation(acc[:, bass.ds(tiles[u % G], 1), :].rearrange("p a c -> p (a c)"), state[:, :, 1 + u], ACT.Copy
                                 ).then_inc(state_stored, 1)

            def copy_onehots(b, h, g):
                if not (type(b) is int and b == 0):
                    act.wait_ge(zd_ready, NG * (b - 1) + g + 1)
                act.wait_ge(oneT_ps, NG * b + g + 1)
                if g == 0:
                    A.activation(first_col[:, h:h + 1], tr_ps[0][:, 0:1], ACT.Copy)
                A.activation(onehotT[:, g * G:(g + 1) * G, :].rearrange("p j e -> p (j e)"), tr_ps[g % 2][:, :], ACT.Copy).then_inc(oneT_ready, 1)

            def copy_sums(b, first):
                if not first:
                    act.wait_ge(scan_done, b)
                A.activation(keepf[:, :, 1:B + 1], spread(keep[:, bass.ds(b * B, B)].rearrange("p (a j) -> p a j", a=1), 1, AW),
                             ACT.Copy).then_inc(keep_ready, 1)
                for q in range(B // Q):
                    act.wait_ge(sums_ps, (B // Q) * b + q + 1)
                    A.activation(sums[:, :, 1 + q * Q:1 + (q + 1) * Q].rearrange("p c j -> p j c"),
                                 sum_ps[q % 2][:, 0:Q * AW].rearrange("p (j c) -> p j c", c=AW), ACT.Copy).then_inc(sums_copied, 1)

            def period(b, h, more=True):
                first = type(b) is int and b == 0
                states = not (type(b) is int and b < 2)
                if more:
                    copy_onehots(b + 1, 1 - h, 0)
                if states:
                    store_states(b - 2, 2)
                if more:
                    copy_onehots(b + 1, 1 - h, 1)
                if states:
                    store_states(b - 2, 3)
                if more:
                    copy_onehots(b + 1, 1 - h, 2)
                act.wait_ge(x_ready, b + 1)
                A.activation(eexp, xexp, ACT.Exp, scale=float(R) ** -0.5).then_inc(e_ready, 1)
                A.activation(ratio[0:1, 1, :], ratio[0:1, 0, :], ACT.Exp, scale=float(R) ** -0.5).then_inc(ratio_ready, 1)
                if more:
                    copy_onehots(b + 1, 1 - h, 3)
                if not first:
                    act.wait_ge(sums_ps, (B // Q) * b)
                for s, made, rounded in ((0, weighted, hi_ready), (1, rest_ready, mid_ready)):
                    for g in range(NG):
                        js = slice(g * G, (g + 1) * G)
                        act.wait_ge(made, NG * b + g + 1)
                        A.activation(wparts[:, js, s, :], zs[:, h, js, :], ACT.Copy).then_inc(rounded, 1)
                copy_sums(b, first)
                if not first:
                    store_states(b - 1, 0)
                    store_states(b - 1, 1)

            act.wait_ge(tab_read, 8)
            for g in range(NG):
                copy_onehots(0, 0, g)
            period(0, 0)
            period(1, 1)
            with nc.scalar.Fori(1, NB // 2 - 1) as i:
                for h in range(2):
                    period(2 * i + h, h)
            period(NB - 2, 0)
            period(NB - 1, 1, more=False)
            for b, g in ((NB - 2, 2), (NB - 2, 3), (NB - 1, 0), (NB - 1, 1), (NB - 1, 2), (NB - 1, 3)):
                store_states(b, g)

            def root(g, h, variance, ready):
                act.wait_ge(variance, g + 1)
                A.activation(rstd[:, h, :, 0], rstd[:, h, :, 2], ACT.Sqrt).then_inc(ready, 1)

            def relu_tile(g, h, t):
                act.wait_ge(y_ps, g * T7 + t + 1)
                A.activation(xTb[:, h, t, :], psum[2 + (h + t) % 2][:, 0:D], ACT.Relu, bias=relu_bias[:, :]).then_inc(relu_done, 1)

            def norm_tile(h, t):
                y = xTb[:, h, t, :]
                A.activation(y, y, ACT.Identity, bias=rstd[:, h, t, 1:2], scale=rstd[:, h, t, 0:1]).then_inc(x1_ready, 1)

            def stage(j, h, dense, tables, reuse):
                if tables:
                    root(j - 1, 1 - h, var_ready, rstd_ready)
                    act.wait_ge(nb_ready, j)
                for t in range(DENSE_FIRST):
                    if dense:
                        relu_tile(j, h, t)
                    if tables:
                        for n in range(T7 * t // DENSE_FIRST, T7 * (t + 1) // DENSE_FIRST):
                            norm_tile(1 - h, n)
                if tables:
                    if reuse is not None:
                        act.wait_ge(table_out[1 - h], 32 * reuse)
                    for t in range(T7):
                        act.wait_ge(xt1_ps, (j - 1) * T7 + t + 1)
                        A.activation(xto[:, 1 - h, t, :], psum[6 + (1 - h + t) % 2][:, 0:WW], ACT.Copy).then_inc(xt1_copied, 1)
                if dense:
                    for t in range(DENSE_FIRST, T7):
                        relu_tile(j, h, t)

            stage(0, 0, True, False, None)
            stage(1, 1, True, True, None)
            stage(2, 0, True, True, None)
            stage(3, 1, True, True, 1)
            with nc.scalar.Fori(2, NG7 // 2) as i:
                stage(2 * i, 0, True, True, i - 1)
                stage(2 * i + 1, 1, True, True, i)
            stage(NG7, 0, False, True, NG7 // 2 - 1)

            def exp_logits(g, h):
                act.wait_ge(lg_ready, g + 1)
                A.activation(lg[:, h, :, :], lg[:, h, :, :], ACT.Exp).then_inc(lg_exp, 1)

            def finish_group(g, h):
                act.wait_ge(nb2_ready, g + 1)
                for t in range(T7):
                    y = x1[:, bass.ds(g * T7 + t, 1), :].rearrange("p a d -> p (a d)")
                    last = A.activation(y, y, ACT.Identity, bias=rstd[:, h, t, 1:2], scale=rstd[:, h, t, 0:1])
                last.then_inc(out_ready, 1)

            def next_group(g, h):
                root(g - 1, 1 - h, var2_ready, rstd2_ready)
                exp_logits(g, h)
                finish_group(g - 1, 1 - h)

            exp_logits(0, 0)
            next_group(1, 1)
            with nc.scalar.Fori(1, NG7 // 2) as i:
                for h in range(2):
                    next_group(2 * i + h, h)
            root(NG7 - 1, 1, var2_ready, rstd2_ready)
            finish_group(NG7 - 1, 1)


_INS = ["x", "src", "dst", "L0_gnn_U", "L0_gnn_Dmat", "L0_gnn_head_w", "L1_gnn_weight", "L1_gnn_attn_l", "L1_gnn_attn_r"]


def kernel(**inputs):
    import concourse.bacc as bacc
    from concourse.bass_utils import run_bass_kernel_spmd

    nc = bacc.Bacc("TRN2", target_bir_lowering=False, num_devices=1)
    arrays, args = {}, []
    for name in _INS:
        a = np.ascontiguousarray(inputs[name])
        arrays[f"in_{name}"] = a
        args.append(nc.dram_tensor(f"in_{name}", a.shape, mybir.dt.from_np(a.dtype), kind="ExternalInput").ap())
    out = nc.dram_tensor("out_0", (N, D), F32, kind="ExternalOutput").ap()
    program(nc, *args, out)
    r = run_bass_kernel_spmd(nc, [arrays], core_ids=[0])
    return r.results[0]["out_0"]
```

```python
from contextlib import ExitStack

import numpy as np
import concourse.bass as bass
from concourse import mybir
from concourse.alu_op_type import AluOpType as ALU

F32 = mybir.dt.float32
I32 = mybir.dt.int32
BF16 = mybir.dt.bfloat16
ACT = mybir.ActivationFunctionType
AX_X = mybir.AxisListType.X

P = 128
N = 12500
E = 200000
D = 256
DC = D // P
K, R = 4, 16
KR = K * R
H, O = 4, 64
HO = H * O
NT = -(-N // P)
ET = -(-E // P)
LASTN = N - (NT - 1) * P
B = 32
S = -(-(ET + NT) // P) * P
SG = S // P
NB = S // B
G = 8
NG = B // G
Q = 4
NSPARE = 4
ZP = 3
AW = KR + K
XW = HO + H
WW = XW + H
NEG = -1e30
PAD = P * (NT + 2)
ETA, LAM, EPS = 0.5, 0.1, 1e-5
T7 = 7
NG7 = NT // T7
HALVES = ((0, 4), (4, T7))
DENSE_FIRST = 2
YT = 2
NY = NT // YT
RING = 4
assert NT % YT == 0 and NY == NB - 3 and G == 2 * Q
assert NG7 // 2 == 7 and NT % (2 * T7) == 0 and S % (2 * B) == 0 and ET + NT <= S and E % P in (0, 64)


def spread(ap, axis, n):
    shape = list(ap.shape)
    shape[axis] = n
    return ap.broadcast_to(shape)


class Count:

    def __init__(self):
        self.base, self.n, self.i, self.per = 0, 0, None, 0

    def loop(self, i, per):
        self.base, self.n, self.i, self.per = self.base + self.n, 0, i, per

    def end(self, trips):
        assert self.n == self.per, (self.n, self.per)
        self.base, self.n, self.i, self.per = self.base + self.per * trips, 0, None, 0

    def next(self):
        self.n += 1
        return self.base + self.n + (self.i * self.per if self.i is not None else 0)


def program(nc, x, src, dst, u, dmat, head_w, weight, attn_l, attn_r, out):
    ctx = ExitStack()
    with ctx:
        def sb(name, shape, dt=F32):
            return ctx.enter_context(nc.sbuf_tensor(name, shape, dt))

        def sem(name):
            return ctx.enter_context(nc.semaphore(name))

        dst_rows = nc.dram_tensor("dst_rows", (S, P), I32).ap()
        src_rows = nc.dram_tensor("src_rows", (S, P), I32).ap()
        reset_rows = nc.dram_tensor("reset_rows", (S, P), F32).ap()
        z_table = nc.dram_tensor("z_table", (NT * P, KR), F32).ap()
        xmz_table = nc.dram_tensor("xmz_table", (NT * P, D), F32).ap()
        xt_table = nc.dram_tensor("xt_table", (NT * P, XW), F32).ap()
        al_table = nc.dram_tensor("al_table", (NT * P, H), F32).ap()

        arena = sb("arena", [P, NT * D])
        at = [0]

        def part(width):
            a = arena[:, at[0]:at[0] + width]
            at[0] += width
            assert at[0] <= NT * D
            return a

        z3 = part((NT + 1) * ZP * KR // 2).bitcast(BF16).rearrange("p (t s c) -> p t s c", s=ZP, c=KR)
        zs = part(2 * B * AW).rearrange("p (h j c) -> p h j c", h=2, j=B)
        dslot = part(S)
        keep = part(S // 2).bitcast(BF16)
        shift = part(P)
        corner = part(P)
        oflat = arena[:, at[0]:at[0] + 4 * S]
        onehot = part(B * P).bitcast(BF16).rearrange("p (h j n) -> p h j n", h=2, j=B)
        onehotT = part(B * P // 2).bitcast(BF16).rearrange("p (j e) -> p j e", j=B)
        sums = part(AW * (B + 1)).rearrange("p (c j) -> p c j", c=AW)
        x1 = arena[:, :].rearrange("p (t d) -> p t d", d=D)
        diag = oflat[:, 0:S]
        ulast = oflat[:, S:2 * S]
        keeprow = ulast[0:1, :]
        spare = oflat[0:1, 2 * S:3 * S]
        arowf = oflat[0:1, 3 * S:4 * S]
        junk = oflat[:, 2 * S:3 * S]
        dloc = oflat[:, 3 * S:4 * S].rearrange("p (g e) -> p g e", e=P)
        cont = diag.rearrange("p (g e) -> p g e", e=P)
        okrow = ulast.rearrange("p (g e) -> p g e", e=P)
        srcf = junk.rearrange("p (g e) -> p g e", e=P)

        acc = sb("acc", [P, NT + 1 + NSPARE, AW])
        zf = acc[:, :, :].rearrange("p t c -> p (t c)")[:, 0:NT * KR].rearrange("p (t c) -> p t c", c=KR)
        xto = sb("xto", [P, 2, T7, WW])
        xto_flat = xto[:, :, :, :].rearrange("p h t c -> p (h t c)")
        dst_sb = xto_flat[:, 0:S].bitcast(I32).rearrange("p (g e) -> p g e", e=P)
        src_sb = xto_flat[:, S:2 * S].bitcast(I32).rearrange("p (g e) -> p g e", e=P)
        zs_flat = zs.rearrange("p h j c -> p (h j c)")
        dst_step = zs_flat[:, 0:S].bitcast(I32).rearrange("p (g e) -> p g e", e=P)
        src_step = zs_flat[:, S:2 * S].bitcast(I32).rearrange("p (g e) -> p g e", e=P)
        wparts = xto_flat[:, 0:B * ZP * AW // 2].bitcast(BF16).rearrange("p (j s c) -> p j s c", s=ZP, c=AW)
        sslot = sb("sslot", [P, S], I32)
        tspace = sb("tspace", [P, S], I32)
        trow = tspace[0:1, :]
        arow = tspace[32:33, :]
        src1 = sb("src1", [P, P], I32)
        dst1 = sb("dst1", [P, P], I32)
        didx = sb("didx", [P, 2, B])
        sidx = sb("sidx", [P, 2, B], I32)
        ident = sb("ident", [P, P])
        ones = sb("ones", [P, P])
        iota_row = sb("iota_row", [P, P])
        iota_i = sb("iota_i", [P, P], I32)
        stepno_i = sb("stepno_i", [P, SG], I32)
        stepno = sb("stepno", [P, SG])
        pno = sb("pno", [P, 3])
        lastt_i = sb("lastt_i", [P, SG], I32)
        lastt = sb("lastt", [P, SG])
        istep = sb("istep", [P, SG])
        istep_i = sb("istep_i", [P, SG], I32)
        tstep = sb("tstep", [P, SG])
        tneg = sb("tneg", [P, SG])
        plast = sb("plast", [P, SG])
        x1T = sb("x1T", [P, 2, D])
        x1T_row = x1T[0:1, :, :].rearrange("a r d -> a (r d)")
        rows = x1T_row[:, 0:3 * P].rearrange("a (n q) -> a n q", q=P)
        rmin = x1T_row[:, 3 * P:4 * P]
        rnext = sb("rnext", [1, P])
        carry = sb("carry", [1, P + K])
        back = sb("back", [1, P])
        backx = sb("backx", [1, P])
        ratio = sb("ratio", [1, 2, K])
        inmin = sb("inmin", [P, 1])
        ccol = sb("ccol", [P, 1])
        dcol = sb("dcol", [P, 1])
        first_col = sb("first_col", [P, 2])
        fac = sb("fac", [P, K])
        ident_b = sb("ident_b", [P, P], BF16)
        iota_b = sb("iota_b", [P, P], BF16)
        xin = sb("xin", [P, 2, T7, D])
        xTb = sb("xTb", [P, 2, T7, D])
        xin_flat = xin[:, :, :, :].rearrange("p h t d -> p (h t d)")
        keepf = xin_flat[:, 0:AW * (B + 1)].rearrange("p (c j) -> p c j", c=AW)
        xat = [AW * (B + 1)]

        def xpart(width):
            a = xin_flat[:, xat[0]:xat[0] + width]
            xat[0] += width
            assert xat[0] <= 2 * T7 * D
            return a

        prod = xpart(G * KR).rearrange("p (j c) -> p j c", j=G)
        fwd0, fwd, rev0, rev, xexp, eexp = [xpart(P) for _ in range(6)]
        xTb_flat = xTb[:, :, :, :].rearrange("p h t d -> p (h t d)")
        state = xTb_flat[:, 0:AW * (B + 1)].rearrange("p (c j) -> p c j", c=AW)
        yat = AW * (B + 1)
        resets = xTb_flat[:, yat:yat + 2 * (P + 1)].rearrange("p (h e) -> p h e", h=2)
        yat += 2 * (P + 1)
        logits = xTb_flat[:, yat:yat + 2 * P].rearrange("p (h q) -> p h q", h=2)
        dspace = sb("dspace", [P, 2, YT, D])
        dm, gs = dspace[:, 0], dspace[:, 1]
        xn = dspace[:, :, :, :].rearrange("p h t d -> p (h t) d")
        ur = sb("ur", [P, DC, K, R])
        wur = sb("wur", [P, DC, K, R])
        wx = sb("wx", [P, DC, WW])
        attn = sb("attn", [1, 2 * HO])
        hw = sb("hw", [1, 3, K])
        hsum = sb("hsum", [1, 3])
        mz = sb("mz", [P, DC, D])
        w3 = sb("w3", [KR, D])
        wtmp = gs
        rec = sb("rec", [P, 2, T7, K])
        agn = sb("agn", [P, 2, T7, KR])
        zT = agn[:, :, :, :].rearrange("p h t c -> p (h t c)")[0:KR, 0:T7 * P]
        xmz = agn[:, :, :, :].rearrange("p h t c -> p (h t c)")[:, 0:YT * D]
        lastcol = sb("lastcol", [P, SG + 1])
        aT = [sslot[0:KR, 0:T7 * P].bitcast(F32), tspace[0:KR, 0:T7 * P].bitcast(F32)]
        stats = sb("stats", [P, T7, 6])
        mv = sb("mv", [P, 2, T7, 2])
        rstd = sb("rstd", [P, 2, T7, 3])
        algat = sb("algat", [P, 2, T7, H])
        lg = sb("lg", [P, 2, T7, H])
        lmax = sb("lmax", [P, T7, 2])
        tmp = agn[:, 0, :, :]

        psum = [ctx.enter_context(nc.psum_tensor(f"bank{i}", [P, 512], F32)) for i in range(8)]
        sum_ps = psum[0:2]
        tr_ps = [p[:, :].bitcast(BF16) for p in psum[2:4]]
        zd_ps = psum[4:6]
        mid_ps, row_ps = psum[6], psum[7]

        edges_in, u_in, weights_in = sem("edges_in"), sem("u_in"), sem("weights_in")
        rows_out, resets_out = sem("rows_out"), sem("resets_out")
        x_in = [sem(f"x_in{i}") for i in range(2)]
        z_rest = sem("z_rest")
        weights_read = sem("weights_read")
        stats_ready = sem("stats_ready")
        z_out = sem("z_out")
        iotas, consts = sem("iotas"), sem("consts")
        v_step = sem("v_step")
        pads_set, diag_ready, bcast_ready, walk_ready = sem("pads_set"), sem("diag_ready"), sem("bcast_ready"), sem("walk_ready")
        tiles_gathered = sem("tiles_gathered")
        dloc_ready, plast_ready, reset_ready = sem("dloc_ready"), sem("plast_ready"), sem("reset_ready")
        tab_ps, tab_read = sem("tab_ps"), sem("tab_read")
        xt_ps, xt_copied = sem("xt_ps"), sem("xt_copied")
        zT_ps, zT_copied, zf_ps, zf_copied = sem("zT_ps"), sem("zT_copied"), sem("zf_ps"), sem("zf_copied")
        prep_ps, prep_read, prep_exp = sem("prep_ps"), sem("prep_read"), sem("prep_exp")
        idx_ready = sem("idx_ready")
        gathered = [[sem(f"gathered{h}{g}") for g in range(NG)] for h in range(2)]
        onehot_ready, oneT_ps, oneT_ready = sem("onehot_ready"), sem("oneT_ps"), sem("oneT_ready")
        zd_ready, zd_used = sem("zd_ready"), sem("zd_used")
        logits_ready, lt_ready = sem("logits_ready"), sem("lt_ready")
        ends_ready, ends_row = sem("ends_ready"), sem("ends_row")
        carry_ready, carry_col = sem("carry_ready"), sem("carry_col")
        heads_ready, heads_row = sem("heads_ready"), sem("heads_row")
        back_ready, back_col = sem("back_ready"), sem("back_col")
        x_ready, e_ready, ratio_ready, et_ready = sem("x_ready"), sem("e_ready"), sem("ratio_ready"), sem("et_ready")
        z_parts, scale_ready = sem("z_parts"), sem("scale_ready")
        weighted, hi_ready, rest_ready, mid_ready, parts_ready = (
            sem("weighted"), sem("hi_ready"), sem("rest_ready"), sem("mid_ready"), sem("parts_ready"))
        sums_ps, sums_copied, keep_ready, scan_done, state_stored = (
            sem("sums_ps"), sem("sums_copied"), sem("keep_ready"), sem("scan_done"), sem("state_stored"))
        keeprow_ready = sem("keeprow_ready")
        resets_in = [sem(f"resets_in{h}") for h in range(2)]
        xe_in, x_last_in, xe_ps, xe_copied = sem("xe_in"), sem("x_last_in"), sem("xe_ps"), sem("xe_copied")
        xmz_ps, xmz_copied, xmz_out = sem("xmz_ps"), sem("xmz_copied"), sem("xmz_out")
        xmz_in = [sem(f"xmz_in{i}") for i in range(2)]
        x2_in = [sem(f"x2_in{i}") for i in range(2)]
        rec_ready, agn_ready, aT_ps, aT_ready, y_ps, y_summed, y_added = (
            sem("rec_ready"), sem("agn_ready"), sem("aT_ps"), sem("aT_ready"), sem("y_ps"), sem("y_summed"), sem("y_added"))
        var_ready, rstd_ready, nb_ready, x1_ready, x1_kept = (
            sem("var_ready"), sem("rstd_ready"), sem("nb_ready"), sem("x1_ready"), sem("x1_kept"))
        x1T_ps, x1T_ready, xt1_ps, xt1_copied = sem("x1T_ps"), sem("x1T_ready"), sem("xt1_ps"), sem("xt1_copied")
        table_out = [sem(f"table_out{i}") for i in range(2)]
        al_in = [sem(f"al_in{i}") for i in range(2)]
        xg_in = [sem(f"xg_in{i}") for i in range(2)]
        lg_ready, lg_exp, xg_used = sem("lg_ready"), sem("lg_exp"), sem("xg_used")
        var2_ready, rstd2_ready, nb2_ready, out_ready = (
            sem("var2_ready"), sem("rstd2_ready"), sem("nb2_ready"), sem("out_ready"))
        out_sent = [sem(f"out_sent{i}") for i in range(2)]

        FULL = E // P
        HALF = E - FULL * P
        G12 = (SG - 1) * P

        def rows_of(table, t, n):
            return table[bass.ds(t * P, n * P), :].rearrange("(t p) c -> p t c", p=P)

        block = ctx.enter_context(nc.Block())

        @block.sync
        def _(sp):
            sp.wait_ge(pads_set, 1)
            for e, tile in ((dst, dst_sb), (src, src_sb)):
                sp.dma_start(tile[:, 0:SG - 1, :], e[0:G12 * P].rearrange("(g p e) -> p g e", p=P, e=P)).then_inc(edges_in, 16)
                sp.dma_start(tile[0:FULL - G12, SG - 1, :], e[G12 * P:FULL * P].rearrange("(p e) -> p e", e=P)).then_inc(edges_in, 16)
                sp.dma_start(tile[FULL - G12:FULL - G12 + 1, SG - 1, 0:HALF], e[FULL * P:E].rearrange("(p e) -> p e", p=1)).then_inc(edges_in, 16)
            for c in range(DC):
                sp.dma_start(ur[:, c, :, :], u[:, c * P:(c + 1) * P, :].rearrange("k p r -> p k r")).then_inc(u_in, 16)
            def load_x(buf, g, signal):
                if type(g) is int and g == NG7 - 1:
                    sp.dma_start(xin[:, buf, 0:T7 - 1, :], rows_of(x, g * T7, T7 - 1)).then_inc(signal[buf], 16)
                    sp.dma_start(xin[0:LASTN, buf, T7 - 1, :], x[N - LASTN:N, :]).then_inc(signal[buf], 16)
                else:
                    sp.dma_start(xin[:, buf, :, :], rows_of(x, g * T7, T7)).then_inc(signal[buf], 16)
            load_x(0, 0, x_in)
            load_x(1, 1, x_in)
            sp.wait_ge(edges_in, 96)
            sp.dma_start(dst_rows.rearrange("(g p) e -> p g e", p=P), dst_sb[:, :, :]).then_inc(rows_out, 16)
            sp.dma_start(src_rows.rearrange("(g p) e -> p g e", p=P), src_sb[:, :, :]).then_inc(rows_out, 16)
            sp.dma_start(dm[:, :, :], dmat.rearrange("(c p) d -> p c d", p=P)).then_inc(weights_in, 16)
            sp.dma_start(wx[:, :, 0:HO], weight.rearrange("(c p) d -> p c d", p=P)).then_inc(weights_in, 16)
            sp.dma_start(attn[0:1, 0:HO], attn_r.rearrange("(a h) o -> a (h o)", a=1)).then_inc(weights_in, 16)
            sp.dma_start(attn[0:1, HO:2 * HO], attn_l.rearrange("(a h) o -> a (h o)", a=1)).then_inc(weights_in, 16)
            sp.dma_start(hw[0:1, 0, :], head_w.rearrange("(a h) -> a h", a=1)).then_inc(weights_in, 16)

            def next_x(g, h):
                sp.wait_ge(xt_ps, T7 * (g + 1))
                load_x(h, g + 2, x_in)

            def z_to_table(g):
                sp.wait_ge(zf_copied, 2 * (g + 1))
                sp.dma_start(rows_of(z_table, g * T7, T7), zf[:, bass.ds(g * T7, T7), :]).then_inc(z_out, 16)

            next_x(0, 0)
            next_x(1, 1)
            z_to_table(0)
            with nc.sync.Fori(1, NG7 // 2 - 2) as i:
                for h in range(2):
                    next_x(2 * i + h, h)
                    z_to_table(2 * i + h - 1)
            for g in range(NG7 - 4, NG7):
                if g + 2 < NG7:
                    next_x(g, g % 2)
                z_to_table(g - 1)
            z_to_table(NG7 - 1)
            sp.wait_ge(reset_ready, 1)
            sp.dma_start(reset_rows.rearrange("(g p) e -> p g e", p=P), cont[:, :, :]).then_inc(resets_out, 16)
            sp.wait_ge(resets_out, 16)

            def load_resets(b, h):
                sp.dma_start(resets[:, h, 0:P], spread(reset_rows[bass.ds(b * B, B), :].rearrange("j (a e) -> j a e", a=1), 1, K)
                             ).then_inc(resets_in[h], 16)
            sp.wait_ge(zT_ps, 2 * NG7)
            for b in range(2):
                load_resets(b, b)

            def load_tiles(n):
                if type(n) is int and n == NY - 1:
                    sp.dma_start(dspace[0:LASTN, 0, YT - 1, :], x[N - LASTN:N, :]).then_inc(x_last_in, 16)
                    sp.wait_ge(x_last_in, 16)
                    sp.dma_start(dspace[:, 0, 0:YT - 1, :], rows_of(x, n * YT, YT - 1)).then_inc(xe_in, 16)
                else:
                    sp.dma_start(dspace[:, 0, :, :], rows_of(x, n * YT, YT)).then_inc(xe_in, 16)

            def turn(b, h, store, load):
                sp.wait_ge(x_ready, b - 1)
                load_resets(b, h)
                if store:
                    sp.wait_ge(xmz_copied, b - 1)
                    sp.dma_start(rows_of(xmz_table, (b - 2) * YT, YT), xmz.rearrange("p (t d) -> p t d", t=YT)).then_inc(xmz_out, 16)
                if load:
                    load_tiles(b - 1)
            sp.wait_ge(prep_read, 6)
            load_tiles(0)
            with nc.sync.Fori(1, NB // 2 - 2) as i:
                for h in range(2):
                    turn(2 * i + h, h, True, True)
            for b in range(NB - 4, NB):
                turn(b, b % 2, b - 2 < NY, b - 1 < NY)
            def load_xmz(g, h):
                sp.dma_start(xTb[:, h, :, :], rows_of(xmz_table, g * T7, T7)).then_inc(xmz_in[h], 16)

            def stage_loads(j, h, more):
                sp.wait_ge(xt1_copied, j * T7)
                sp.dma_start(rows_of(xt_table, (j - 1) * T7, T7), xto[:, 1 - h, :, 0:XW]).then_inc(table_out[1 - h], 16)
                sp.dma_start(rows_of(al_table, (j - 1) * T7, T7), xto[:, 1 - h, :, XW:WW]).then_inc(table_out[1 - h], 16)
                if more:
                    sp.wait_ge(y_added, (j + 1) * T7)
                    load_xmz(j + 2, h)
                    load_x(h, j + 2, x2_in)
            sp.wait_ge(scan_done, NB)
            for h in range(2):
                load_x(h, h, x2_in)
            sp.wait_ge(state_stored, S)
            sp.wait_ge(xmz_out, 16 * NY)
            for h in range(2):
                load_xmz(h, h)
            sp.wait_ge(y_added, T7)
            load_xmz(2, 0)
            load_x(0, 2, x2_in)
            stage_loads(1, 1, True)
            with nc.sync.Fori(1, NG7 // 2 - 2) as i:
                stage_loads(2 * i, 0, True)
                stage_loads(2 * i + 1, 1, True)
            stage_loads(NG7 - 4, 0, True)
            stage_loads(NG7 - 3, 1, True)
            stage_loads(NG7 - 2, 0, False)
            stage_loads(NG7 - 1, 1, False)
            stage_loads(NG7, 0, False)
            with nc.sync.Fori(0, NG7 // 2 - 1) as i:
                for h in range(2):
                    g = 2 * i + h
                    sp.wait_ge(out_ready, g + 1)
                    sp.dma_start(rows_of(out, g * T7, T7), x1[:, bass.ds(g * T7, T7), :]).then_inc(out_sent[h], 16)
            sp.wait_ge(out_ready, NG7 - 1)
            g = NG7 - 2
            sp.dma_start(rows_of(out, g * T7, T7), x1[:, bass.ds(g * T7, T7), :]).then_inc(out_sent[0], 16)
            sp.wait_ge(out_ready, NG7)
            g = NG7 - 1
            sp.dma_start(rows_of(out, g * T7, T7 - 1), x1[:, g * T7:NT - 1, :]).then_inc(out_sent[1], 16)
            sp.dma_start(out[N - LASTN:N, :], x1[0:LASTN, NT - 1, :]).then_inc(out_sent[1], 16)
            sp.wait_ge(out_sent[0], 16 * (NG7 // 2))
            sp.wait_ge(out_sent[1], 16 * (NG7 // 2 + 1))
            sp.wait_ge(z_out, 16 * NG7)

        @block.gpsimd
        def _(pool):
            nc.gpsimd.iota(iota_i[:, :], [[1, P]], base=0, channel_multiplier=0).then_inc(iotas, 1)
            nc.gpsimd.iota(stepno_i[:, :], [[P, SG]], base=0, channel_multiplier=1).then_inc(iotas, 1)
            pool.wait_ge(iotas, 2)
            nc.gpsimd.iota(arow, [[0, S // NSPARE], [1, NSPARE]], base=NT + 1, channel_multiplier=0).then_inc(iotas, 1)
            pool.wait_ge(walk_ready, 1)
            pool.wait_ge(rows_out, 32)
            for table, tile in ((dst_rows, dst_step), (src_rows, src_step)):
                for g in range(SG):
                    pool.indirect_dma_start(tile[:, g, :], None, table,
                                            bass.IndirectOffsetOnAxis(ap=istep_i[:, g:g + 1], axis=0)).then_inc(tiles_gathered, 16)
            pool.wait_ge(z_out, 16 * NG7)

            def gather_block(h, free):
                for g in range(NG):
                    if free is not None:
                        pool.wait_ge(parts_ready, free + g + 1)
                        nc.gpsimd.nop(nofuse=True)
                    for j in range(g * G, (g + 1) * G):
                        pool.indirect_dma_start(zs[:, h, j, 0:KR], None, z_table,
                                                bass.IndirectOffsetOnAxis(ap=sidx[:, h, j:j + 1], axis=0)).then_inc(gathered[h][g], 16)
            for b in range(2):
                pool.wait_ge(idx_ready, b + 1)
                gather_block(b, None)
            with nc.gpsimd.Fori(1, NB // 2) as i:
                for h in range(2):
                    pool.wait_ge(idx_ready, 2 * i + h + 1)
                    nc.gpsimd.nop(nofuse=True)
                    gather_block(h, (2 * i + h - 2) * NG)
            b = NB - 2
            pool.wait_ge(scan_done, b + 1)
            pool.wait_ge(state_stored, B * b)
            for g in range(NG):
                _, tiles = nc.values_load_multi_w_load_instructions(
                    arow[0:1, b * B + g * G:b * B + (g + 1) * G], engines=[mybir.EngineType.Pool], min_val=0, max_val=NT + NSPARE,
                    skip_runtime_bounds_check_because="the vector engine has clamped the node tile")
                for u in range(g * G, (g + 1) * G):
                    if u >= NSPARE:
                        pool.wait_ge(state_stored, B * b + u - NSPARE + 1)
                    nc.gpsimd.tensor_copy(acc[:, bass.ds(tiles[u % G], 1), :].rearrange("p a c -> p (a c)"), state[:, :, 1 + u]
                                          ).then_inc(state_stored, 1)
            def normalise_sums(g, h):
                nc.gpsimd.tensor_tensor(agn[:, h, :, :].rearrange("p t (k r) -> p t k r", r=R),
                                        acc[:, bass.ds(g * T7, T7), 0:KR].rearrange("p t (k r) -> p t k r", r=R),
                                        spread(rec[:, h, :, :].rearrange("p t (k a) -> p t k a", a=1), 3, R), ALU.mult).then_inc(agn_ready, 1)

            def keep_rows(g):
                for t in range(T7):
                    n = g * T7 + t
                    pool.wait_ge(x1_ready, n + 1)
                    nc.gpsimd.tensor_copy(x1[:, bass.ds(n, 1), :].rearrange("p a d -> p (a d)"), xn[:, t % RING, :]).then_inc(x1_kept, 1)

            for g in range(2):
                pool.wait_ge(rec_ready, g + 1)
                normalise_sums(g, g)
            with nc.gpsimd.Fori(0, NG7 // 2 - 1) as i:
                for h in range(2):
                    g = 2 * i + h
                    pool.wait_ge(aT_ps, 2 * (g + 1))
                    pool.wait_ge(rec_ready, g + 3)
                    normalise_sums(g + 2, h)
                    keep_rows(g)
            for h in range(2):
                keep_rows(NG7 - 2 + h)
            for h in range(2):
                pool.wait_ge(table_out[h], 32 * (NG7 // 2))
            for g in range(NG7):
                h = g % 2
                if g >= 2:
                    pool.wait_ge(xg_used, g - 1)
                for t in range(T7):
                    n = g * T7 + t
                    pool.indirect_dma_start(algat[:, h, t, :], None, al_table,
                                            bass.IndirectOffsetOnAxis(ap=src1[:, n:n + 1], axis=0)).then_inc(al_in[h], 16)
                    pool.indirect_dma_start(xto[:, h, t, 0:XW], None, xt_table,
                                            bass.IndirectOffsetOnAxis(ap=dst1[:, n:n + 1], axis=0)).then_inc(xg_in[h], 16)

        @block.vector
        def _(dve):
            vn = Count()
            PERIOD_STEPS = 3 + 9 + 3
            V = nc.vector
            V.memset(dst_sb[:, SG - 1, :], PAD)
            V.memset(src_sb[:, SG - 1, :], 0).then_inc(pads_set, 1)
            V.memset(ones[:, :], 1.0).then_inc(v_step, 1)
            vn.next()
            V.memset(rnext[0:1, P - K:P], 0.0)
            V.memset(backx[0:1, P - K:P], NEG)
            V.memset(z3[:, NT, :, :], 0.0)
            V.memset(carry[0:1, P:P + K], NEG).then_inc(v_step, 1)
            vn.next()
            dve.wait_ge(iotas, 2)
            V.tensor_copy(iota_b[:, :], iota_i[:, :])
            V.tensor_copy(iota_row[:, :], iota_i[:, :]).then_inc(v_step, 1)
            dve.wait_ge(v_step, vn.next())
            V.tensor_copy(stepno[:, :], stepno_i[:, :]).then_inc(v_step, 1)
            dve.wait_ge(v_step, vn.next())
            V.tensor_copy(pno[:, 0:1], stepno[:, 0:1])
            V.tensor_scalar(pno[:, 1:2], stepno[:, 0:1], 1.0, None, ALU.add)
            V.tensor_scalar(pno[:, 2:3], stepno[:, 0:1], float(P - 1), None, ALU.subtract).then_inc(v_step, 1)
            dve.wait_ge(v_step, vn.next())
            V.tensor_scalar(ident[:, :], iota_row[:, :], pno[:, 0:1], None, ALU.is_equal)
            V.tensor_scalar(ident_b[:, :], iota_row[:, :], pno[:, 0:1], None, ALU.is_equal)
            V.tensor_scalar(shift[:, :], iota_row[:, :], pno[:, 1:2], None, ALU.is_equal)
            V.tensor_scalar(corner[:, :], iota_row[:, :], pno[:, 2:3], None, ALU.is_equal).then_inc(consts, 1)
            dve.wait_ge(consts, 1)

            dve.wait_ge(edges_in, 96)
            V.tensor_scalar(lastt_i[:, :], dst_sb[:, :, P - 1], 7, None, ALU.arith_shift_right).then_inc(v_step, 1)
            dve.wait_ge(v_step, vn.next())
            V.tensor_tensor(lastt[:, :], lastt_i[:, :], stepno[:, :], ALU.add).then_inc(v_step, 1)
            dve.wait_ge(v_step, vn.next())
            for g in range(SG):
                last = V.tensor_scalar(diag[:, g * P:(g + 1) * P], ident[:, :], lastt[:, g:g + 1], None, ALU.mult)
            last.then_inc(diag_ready, 1)
            for g in range(0, SG, 4):
                n = min(4, SG - g) * P
                dve.wait_ge(bcast_ready, g // 4 + 1)
                last = V.tensor_copy(ulast[:, g * P:g * P + n], psum[4 + g // 4][:, 0:n])
            last.then_inc(v_step, 1)
            dve.wait_ge(v_step, vn.next())
            for g in range(SG):
                V.tensor_scalar(junk[:, :], ulast[:, :], stepno[:, g:g + 1], 0.0, ALU.is_lt, ALU.add,
                                accum_out=istep[:, g:g + 1]).then_inc(v_step, 1)
                dve.wait_ge(v_step, vn.next())
            V.tensor_copy(istep_i[:, :], istep[:, :]).then_inc(walk_ready, 1)
            V.tensor_tensor(tstep[:, :], stepno[:, :], istep[:, :], ALU.subtract).then_inc(v_step, 1)
            dve.wait_ge(v_step, vn.next())
            V.tensor_scalar(tstep[:, :], tstep[:, :], float(NT), None, ALU.min).then_inc(v_step, 1)
            dve.wait_ge(v_step, vn.next())
            V.tensor_scalar(tneg[:, :], tstep[:, :], -float(P), None, ALU.mult).then_inc(v_step, 1)
            dve.wait_ge(v_step, vn.next())
            dve.wait_ge(weights_in, 16 * 5)
            V.tensor_reduce(hsum[0:1, 0:1], hw[0:1, 0, :], AX_X, ALU.max).then_inc(v_step, 1)
            dve.wait_ge(v_step, vn.next())
            V.tensor_scalar(hw[0:1, 1, :], hw[0:1, 0, :], hsum[0:1, 0:1], None, ALU.subtract).then_inc(prep_read, 1)
            dve.wait_ge(prep_exp, 1)
            V.tensor_reduce(hsum[0:1, 1:2], hw[0:1, 2, :], AX_X, ALU.add).then_inc(v_step, 1)
            dve.wait_ge(v_step, vn.next())
            V.reciprocal(hsum[0:1, 2:3], hsum[0:1, 1:2]).then_inc(v_step, 1)
            dve.wait_ge(v_step, vn.next())
            V.tensor_scalar(hw[0:1, 1, :], hw[0:1, 2, :], hsum[0:1, 2:3], None, ALU.mult).then_inc(prep_read, 1)
            dve.wait_ge(prep_ps, 1)
            V.tensor_copy(gs[:, :, :].rearrange("p c d -> p (c d)"), psum[4][:, :]).then_inc(prep_read, 1)
            V.tensor_tensor(wur[:, :, :, :].rearrange("p c k r -> p k c r"), ur[:, :, :, :].rearrange("p c k r -> p k c r"),
                            spread(spread(psum[5][:, 0:K].rearrange("p (k a b) -> p k a b", a=1, b=1), 2, DC), 3, R), ALU.mult).then_inc(prep_read, 1)
            dve.wait_ge(tiles_gathered, 32 * SG)
            for g in range(SG):
                last = V.tensor_scalar(dloc[:, g, :], dst_step[:, g, :], tneg[:, g:g + 1], None, ALU.add)
            last.then_inc(v_step, 1)
            dve.wait_ge(v_step, vn.next())
            V.memset(lastcol[:, 0:1], 0.0)
            V.tensor_copy(lastcol[:, 1:SG + 1], dloc[:, :, P - 1]).then_inc(dloc_ready, 1)
            V.tensor_copy(srcf[:, :, :], src_step[:, :, :]).then_inc(dloc_ready, 1)
            dve.wait_ge(dloc_ready, 2)
            V.tensor_scalar(okrow[:, :, :], dloc[:, :, :], 0.0, None, ALU.is_ge).then_inc(v_step, 1)
            dve.wait_ge(v_step, vn.next())
            V.scalar_tensor_tensor(okrow[:, :, :], dloc[:, :, :], float(P - 1), okrow[:, :, :], ALU.is_le, ALU.mult).then_inc(v_step, 1)
            dve.wait_ge(v_step, vn.next())
            dve.wait_ge(prep_ps, 2)
            V.tensor_tensor(mz[:, :, :].rearrange("p c d -> p (c d)"), dm[:, :, :].rearrange("p c d -> p (c d)"), psum[6][:, :], ALU.subtract).then_inc(v_step, 1)
            dve.wait_ge(v_step, vn.next())
            V.tensor_scalar(mz[:, :, :], mz[:, :, :], 0.5 * ETA, None, ALU.mult).then_inc(v_step, 1)
            dve.wait_ge(v_step, vn.next())
            for c in range(DC):
                blk = mz[:, c, c * P:(c + 1) * P]
                last = V.scalar_tensor_tensor(blk, ident[:, :], 0.5, blk, ALU.mult, ALU.add)
            last.then_inc(prep_read, 1)
            wv = wx[:, :, 0:HO].rearrange("p c (h o) -> p c h o", h=H)
            for n in range(2):
                V.tensor_tensor(wtmp[:, :, :].rearrange("p c (h o) -> p c h o", h=H), wv,
                                spread(psum[7][:, n * HO:(n + 1) * HO].rearrange("p (a h o) -> p a h o", a=1, h=H), 1, DC),
                                ALU.mult).then_inc(v_step, 1)
                dve.wait_ge(v_step, vn.next())
                V.tensor_reduce(wx[:, :, HO + n * H:HO + (n + 1) * H], wtmp[:, :, :].rearrange("p c (h o) -> p c h o", h=H),
                                AX_X, ALU.add).then_inc(v_step, 1)
                dve.wait_ge(v_step, vn.next())
            dve.wait_ge(prep_ps, 3)
            V.tensor_copy(w3[:, :], psum[4][0:KR, 0:D]).then_inc(prep_read, 1)
            dve.wait_ge(plast_ready, 1)
            V.tensor_copy(plast[:, :], psum[7][:, 0:SG]).then_inc(tab_read, 1)
            dve.wait_ge(tab_read, 1)
            V.tensor_tensor(cont[:, :, 1:P], dloc[:, :, 1:P], dloc[:, :, 0:P - 1], ALU.is_equal)
            V.tensor_tensor(cont[:, :, 0], dloc[:, :, 0], plast[:, :], ALU.is_equal).then_inc(v_step, 1)
            dve.wait_ge(v_step, vn.next())
            V.tensor_tensor(cont[:, :, :], cont[:, :, :], okrow[:, :, :], ALU.mult).then_inc(v_step, 1)
            dve.wait_ge(v_step, vn.next())
            V.tensor_scalar(cont[:, :, :], cont[:, :, :], 1.0, -NEG, ALU.subtract, ALU.mult).then_inc(reset_ready, 1)
            for n, table in enumerate((dslot, sslot, trow)):
                dve.wait_ge(tab_ps, n + 1)
                w = 1 if table is trow else P
                for g in range(0, SG, 4):
                    m = min(4, SG - g) * P
                    last = V.tensor_copy(table[0:w, g * P:g * P + m], psum[4 + g // 4][0:w, 0:m])
                last.then_inc(tab_read, 1)
                if table is sslot:
                    dve.wait_ge(tab_read, 3)
                    for b in range(2):
                        V.tensor_copy(sidx[:, b, :], sslot[:, b * B:(b + 1) * B]).then_inc(idx_ready, 1)
            dve.wait_ge(tab_read, 4)
            V.memset(keeprow[0:1, 0:1], 0.0)
            V.tensor_tensor(keeprow[0:1, 1:S], trow[0:1, 1:S], trow[0:1, 0:S - 1], ALU.is_equal).then_inc(keeprow_ready, 1)
            dve.wait_ge(iotas, 3)
            V.tensor_copy(spare, arow)
            V.tensor_copy(arowf, trow).then_inc(v_step, 1)
            stays = keeprow.rearrange("a (b j) -> a b j", j=B)
            here = arowf.rearrange("a (b j) -> a b j", j=B)[:, :, 0:B - 1]
            other = spare.rearrange("a (b j) -> a b j", j=B)[:, :, 0:B - 1]
            dve.wait_ge(v_step, vn.next())
            V.tensor_tensor(other, other, here, ALU.subtract).then_inc(v_step, 1)
            dve.wait_ge(v_step, vn.next())
            V.tensor_tensor(other, other, stays[:, :, 1:B], ALU.mult).then_inc(v_step, 1)
            dve.wait_ge(v_step, vn.next())
            V.tensor_tensor(here, here, other, ALU.add).then_inc(v_step, 1)
            dve.wait_ge(v_step, vn.next())
            V.tensor_copy(arow, arowf).then_inc(tab_read, 1)
            for n in range(0, S, 512):
                m = min(512, S - n)
                dve.wait_ge(bcast_ready, 5 + n // 512)
                last = V.tensor_copy(keep[:, n:n + m], psum[4 + n // 512][:, 0:m])
            last.then_inc(tab_read, 1)
            V.tensor_copy(okrow[:, 0, :], dst_sb[:, 0, :])
            V.tensor_copy(okrow[:, 1, :], src_sb[:, 0, :]).then_inc(tab_read, 1)
            dve.wait_ge(tab_ps, 4)
            V.tensor_copy(dst1[:, :], psum[4][:, 0:P])
            V.tensor_copy(src1[:, :], psum[4][:, P:2 * P]).then_inc(tab_read, 1)

            dve.wait_ge(tab_read, 8)
            dve.wait_ge(resets_out, 16)
            dve.wait_ge(prep_read, 6)

            V.memset(sums[:, :, 0], 0.0)
            dve.wait_ge(xt_ps, NT)
            V.memset(keepf[:, :, 0], 0.0).then_inc(v_step, 1)
            dve.wait_ge(v_step, vn.next())
            dve.wait_ge(z_out, 16 * NG7)
            V.memset(resets[:, :, P:P + 1], 0.0).then_inc(v_step, 1)
            dve.wait_ge(v_step, vn.next())
            for s in range(2):
                for half in range(2):
                    ts = slice(half * NT // 2, (half + 1) * NT // 2)
                    dve.wait_ge(z_parts, 2 * s + half + 1)
                    to = zf[:, ts, :] if s == 0 else z3[:, ts, ZP - 1, :]
                    V.tensor_tensor(to, zf[:, ts, :], z3[:, ts, s, :], ALU.subtract).then_inc(z_rest, 1)

            def copy_indices(b, h):
                V.tensor_copy(didx[:, h, :], dslot[:, bass.ds(b * B, B)]).then_inc(v_step, 1)
                dve.wait_ge(v_step, vn.next())

            def make_onehot(b, h, g, reused):
                if reused and g == 0:
                    dve.wait_ge(sums_ps, (b - 1) * (B // Q))
                for j in range(g * G, (g + 1) * G):
                    last = V.tensor_scalar(onehot[:, h, j, :], iota_b[:, :], didx[:, h, j:j + 1], None, ALU.is_equal)
                last.then_inc(onehot_ready, 1)

            def head_products(b, h, g, uses):
                dve.wait_ge(zd_ready, NG * b + g + 1)
                dve.wait_ge(gathered[h][g], 16 * G * uses)
                V.tensor_tensor(prod[:, :, :], zs[:, h, g * G:(g + 1) * G, 0:KR],
                                zd_ps[g % 2][:, :].rearrange("p (j c) -> p j c", j=G), ALU.mult).then_inc(zd_used, 1)
                dve.wait_ge(zd_used, NG * b + g + 1)
                last = V.tensor_reduce(logits[:, h, g * G * K:(g + 1) * G * K], prod[:, :, :].rearrange("p j (k r) -> p (j k) r", r=R),
                                       AX_X, ALU.add)
                if g == NG - 1:
                    last.then_inc(logits_ready, 1)
                else:
                    last.then_inc(v_step, 1)
                    dve.wait_ge(v_step, vn.next())

            def copy_next_indices(b, h):
                V.tensor_copy(sidx[:, h, :], sslot[:, bass.ds(b * B, B)]).then_inc(idx_ready, 1)

            def by_head(row, k):
                return row.rearrange("a (j k) -> a j k", k=K)[:, :, k]

            def scan_steps(b, first, last=False):
                dve.wait_ge(keep_ready, b + 1)
                for c0, c1, r in ((0, KR, R), (KR, AW, 1)):
                    k1 = keepf[:, c0:c1, 1].rearrange("p (k r) -> p k r", r=r)
                    f = fac[:, :].rearrange("p (k a) -> p k a", a=1)
                    scaled = V.scalar_tensor_tensor(k1, spread(f, 2, r) if r > 1 else f, 1.0, k1, ALU.add, ALU.mult)
                scaled.then_inc(v_step, 1)
                dve.wait_ge(v_step, vn.next())
                dve.wait_ge(sums_copied, (b + 1) * (B // Q))
                if not first:
                    dve.wait_ge(state_stored, B * b)
                V.tensor_tensor_scan(state.rearrange("p c j -> p (c j)"), keepf.rearrange("p c j -> p (c j)"),
                                     sums.rearrange("p c j -> p (c j)"), 0.0, ALU.mult, ALU.add).then_inc(scan_done, 1)
                if not last:
                    dve.wait_ge(scan_done, b + 1)
                    V.tensor_copy(sums[:, :, 0], state[:, :, B]).then_inc(v_step, 1)
                    dve.wait_ge(v_step, vn.next())

            def period(b, h, uses, reused=True, more_idx=True, more=True):
                first = type(b) is int and b == 0
                rs = resets[:, h, :]
                rs_rev = rs[:, P:0:-1]

                def next_onehot(g):
                    if more:
                        make_onehot(b + 1, 1 - h, g, reused)
                for g in range(NG):
                    head_products(b, h, g, uses)
                if more_idx:
                    copy_next_indices(b + 2, h)
                dve.wait_ge(resets_in[h], 16 * uses)
                V.tensor_reduce(inmin[:, :], rs[:, 1:P], AX_X, ALU.min)
                dve.wait_ge(lt_ready, b + 1)
                V.tensor_tensor_scan(fwd0, rs[:, 0:P], mid_ps[:, 0:P], NEG, ALU.add, ALU.max).then_inc(ends_ready, 1)
                if more:
                    copy_indices(b + 1, 1 - h)
                next_onehot(0)
                dve.wait_ge(ends_row, b + 1)
                V.tensor_copy(rows[0:1, :, :].rearrange("a n q -> a (n q)"), row_ps[0:1, 0:3 * P])
                V.tensor_copy(carry[0:1, 0:K], carry[0:1, P:P + K]).then_inc(v_step, 1)
                dve.wait_ge(v_step, vn.next())
                V.tensor_tensor(rmin[0:1, :], rows[0:1, 1, :], rows[0:1, 2, :], ALU.min)
                V.tensor_tensor(rnext[0:1, 0:P - K], rows[0:1, 1, 0:P - K], rows[0:1, 2, K:P], ALU.add).then_inc(v_step, 1)
                dve.wait_ge(v_step, vn.next())
                for k in range(K):
                    last = V.tensor_tensor_scan(by_head(carry[0:1, K:P + K], k), by_head(rmin[0:1, :], k), by_head(rows[0:1, 0, :], k),
                                                carry[0:1, k:k + 1], ALU.add, ALU.max)
                last.then_inc(carry_ready, 1)
                next_onehot(1)
                dve.wait_ge(carry_col, b + 1)
                V.tensor_copy(ccol[:, :], row_ps[:, 384:385]).then_inc(v_step, 1)
                dve.wait_ge(v_step, vn.next())
                V.tensor_tensor_scan(fwd, rs[:, 0:P], mid_ps[:, 0:P], ccol[:, :], ALU.add, ALU.max).then_inc(v_step, 1)
                dve.wait_ge(v_step, vn.next())
                V.tensor_tensor_scan(rev0[:, ::-1], rs_rev, fwd[:, ::-1], NEG, ALU.add, ALU.max).then_inc(heads_ready, 1)
                next_onehot(2)
                dve.wait_ge(heads_row, b + 1)
                for k in range(K):
                    last = V.tensor_tensor_scan(by_head(back[0:1, :], k)[:, ::-1], by_head(rnext[0:1, :], k)[:, ::-1],
                                                by_head(row_ps[0:1, 0:P], k)[:, ::-1], NEG, ALU.add, ALU.max)
                last.then_inc(v_step, 1)
                dve.wait_ge(v_step, vn.next())
                V.tensor_tensor(backx[0:1, 0:P - K], back[0:1, K:P], rows[0:1, 2, K:P], ALU.add).then_inc(back_ready, 1)
                V.tensor_tensor(ratio[0:1, 0, :], carry[0:1, 0:K], rows[0:1, 2, 0:K], ALU.add).then_inc(v_step, 1)
                next_onehot(3)
                dve.wait_ge(v_step, vn.next())
                V.tensor_tensor(ratio[0:1, 0, :], ratio[0:1, 0, :], back[0:1, 0:K], ALU.subtract)
                dve.wait_ge(back_col, b + 1)
                V.tensor_copy(dcol[:, :], row_ps[:, 385:386]).then_inc(v_step, 1)
                dve.wait_ge(v_step, vn.next())
                V.tensor_tensor_scan(rev[:, ::-1], rs_rev, fwd[:, ::-1], dcol[:, :], ALU.add, ALU.max).then_inc(v_step, 1)
                dve.wait_ge(v_step, vn.next())
                V.tensor_tensor(xexp, mid_ps[:, 0:P], rev, ALU.subtract).then_inc(x_ready, 1)
                if not first:
                    scan_steps(b - 1, type(b) is int and b == 1)
                dve.wait_ge(et_ready, b + 1)
                V.tensor_copy(zs[:, h, :, KR:AW], mid_ps[:, 0:P].rearrange("p (j k) -> p j k", k=K)).then_inc(weights_read, 1)
                dve.wait_ge(weights_read, b + 1)
                for g in range(NG):
                    z = zs[:, h, g * G:(g + 1) * G, 0:KR].rearrange("p j (k r) -> p j k r", r=R)
                    w = spread(zs[:, h, g * G:(g + 1) * G, KR:AW].rearrange("p j (k a) -> p j k a", a=1), 3, R)
                    V.tensor_tensor(z, z, w, ALU.mult).then_inc(weighted, 1)
                dve.wait_ge(scale_ready, b + 1)
                V.tensor_scalar(fac[:, :], row_ps[:, 386:386 + K], 1.0, first_col[:, h:h + 1], ALU.subtract, ALU.mult).then_inc(v_step, 1)
                dve.wait_ge(v_step, vn.next())
                for s, rounded, left in ((0, hi_ready, rest_ready), (1, mid_ready, parts_ready)):
                    for g in range(NG):
                        js = slice(g * G, (g + 1) * G)
                        dve.wait_ge(rounded, NG * b + g + 1)
                        V.tensor_tensor(zs[:, h, js, :] if s == 0 else wparts[:, js, ZP - 1, :], zs[:, h, js, :], wparts[:, js, s, :],
                                        ALU.subtract).then_inc(left, 1)

            copy_indices(0, 0)
            for g in range(NG):
                make_onehot(0, 0, g, False)
            period(0, 0, 1, reused=False)
            period(1, 1, 1)
            with nc.vector.Fori(1, NB // 2 - 1) as i:
                vn.loop(i - 1, 2 * PERIOD_STEPS)
                for h in range(2):
                    period(2 * i + h, h, i + 1)
                vn.end(NB // 2 - 2)
            period(NB - 2, 0, NB // 2, more_idx=False)
            period(NB - 1, 1, NB // 2, more_idx=False, more=False)
            scan_steps(NB - 1, False, last=True)

            dve.wait_ge(state_stored, S)

            def sums_reciprocal(g, h):
                V.tensor_scalar(rec[:, h, :, :], acc[:, bass.ds(g * T7, T7), KR:AW], 1e-16, None, ALU.add).then_inc(v_step, 1)
                dve.wait_ge(v_step, vn.next())
                V.reciprocal(rec[:, h, :, :], rec[:, h, :, :]).then_inc(rec_ready, 1)

            def inverse_variance(h, ready):
                V.tensor_scalar(rstd[:, h, :, 2], mv[:, h, :, 1], EPS, None, ALU.add).then_inc(v_step, 1)
                dve.wait_ge(v_step, vn.next())
                V.reciprocal(rstd[:, h, :, 2], rstd[:, h, :, 2]).then_inc(ready, 1)

            def norm_bias(h, g, rooted, ready):
                dve.wait_ge(rooted, g + 1)
                V.scalar_tensor_tensor(rstd[:, h, :, 1], mv[:, h, :, 0], -1.0, rstd[:, h, :, 0], ALU.mult, ALU.mult).then_inc(ready, 1)

            def dense_steps(j, h):
                for k in range(T7 + 3):
                    if k < T7:
                        n = j * T7 + k
                        dve.wait_ge(y_ps, n + 1)
                        V.scalar_tensor_tensor(xTb[:, h, k, :], psum[2 + (h + k) % 2][:, 0:D], -ETA * LAM, xTb[:, h, k, :],
                                               ALU.add, ALU.add).then_inc(y_summed, 1)
                    if 1 <= k <= T7:
                        n = j * T7 + k - 1
                        dve.wait_ge(y_summed, n + 1)
                        V.scalar_tensor_tensor(x1[:, bass.ds(n, 1), :].rearrange("p a d -> p (a d)"), xTb[:, h, k - 1, :], 0.0,
                                               xin[:, h, k - 1, :], ALU.max, ALU.add).then_inc(y_added, 1)
                    if 2 <= k <= T7 + 1:
                        n = j * T7 + k - 2
                        dve.wait_ge(y_added, n + 1)
                        V.nop(nofuse=True)
                        V.bn_stats(stats[:, k - 2, :], x1[:, bass.ds(n, 1), :].rearrange("p a d -> p (a d)")).then_inc(stats_ready, 1)
                    if k >= 3:
                        n = j * T7 + k - 3
                        dve.wait_ge(stats_ready, n + 1)
                        V.nop(nofuse=True)
                        last = V.bn_aggr(mv[:, h, k - 3, :], stats[:, k - 3, :])
                last.then_inc(v_step, 1)
                dve.wait_ge(v_step, vn.next())
                inverse_variance(h, var_ready)

            def copy_sums(j, h):
                for q in range(2):
                    dve.wait_ge(aT_ps, 2 * j + q + 1)
                    n = 4 if q == 0 else T7 - 4
                    V.tensor_copy(aT[h][:, q * 4 * P:(q * 4 + n) * P], psum[q][0:KR, 0:n * P]).then_inc(aT_ready, 1)

            def stage(j, h, more, two_parts=False, next_sums=True):
                dve.wait_ge(xmz_in[h], 16 * ((j - h) // 2 + 1) if type(j) is int else X2_IN)
                dve.wait_ge(x2_in[h], 16 * ((j - h) // 2 + 1) + (16 if two_parts else 0) if type(j) is int else X2_IN)
                dense_steps(j, h)
                if next_sums:
                    copy_sums(j + 1, 1 - h)
                norm_bias(h, j, rstd_ready, nb_ready)
                if more:
                    dve.wait_ge(agn_ready, j + 1)
                    sums_reciprocal(j + 2, h)

            for g in range(2):
                sums_reciprocal(g, g)
            copy_sums(0, 0)
            stage(0, 0, True)
            stage(1, 1, True)
            with nc.vector.Fori(1, NG7 // 2 - 1) as i:
                X2_IN = 16 * (i + 1)
                vn.loop(i - 1, 2 * 3)
                for h in range(2):
                    stage(2 * i + h, h, True)
                vn.end(NG7 // 2 - 2)
            stage(NG7 - 2, 0, False)
            stage(NG7 - 1, 1, False, two_parts=True, next_sums=False)

            def attend_group(i, h, first=False):
                g = 2 * i + h
                z = lg[:, h, :, :]
                rowsg = xto[:, h, :, 0:HO].rearrange("p t (h o) -> p t h o", h=H)
                dve.wait_ge(al_in[h], 16 * T7 * (i + 1))
                dve.wait_ge(xg_in[h], 16 * T7 * (i + 1))
                V.tensor_tensor(z, algat[:, h, :, :], xto[:, h, :, HO:XW], ALU.add).then_inc(v_step, 1)
                dve.wait_ge(v_step, vn.next())
                V.scalar_tensor_tensor(z, z, 0.01, z, ALU.mult, ALU.max).then_inc(v_step, 1)
                dve.wait_ge(v_step, vn.next())
                V.tensor_reduce(lmax[:, :, 0:1], z, AX_X, ALU.max).then_inc(v_step, 1)
                dve.wait_ge(v_step, vn.next())
                V.tensor_tensor(z, z, spread(lmax[:, :, 0:1], 2, H), ALU.subtract).then_inc(lg_ready, 1)
                if not first:
                    norm_bias(1 - h, g - 1, rstd2_ready, nb2_ready)
                dve.wait_ge(lg_exp, g + 1)
                V.tensor_reduce(lmax[:, :, 0:1], z, AX_X, ALU.add).then_inc(v_step, 1)
                dve.wait_ge(v_step, vn.next())
                V.reciprocal(lmax[:, :, 1:2], lmax[:, :, 0:1]).then_inc(v_step, 1)
                dve.wait_ge(v_step, vn.next())
                V.tensor_tensor(z, z, spread(lmax[:, :, 1:2], 2, H), ALU.mult).then_inc(v_step, 1)
                dve.wait_ge(v_step, vn.next())
                V.tensor_tensor(rowsg, rowsg, spread(z.rearrange("p t (h a) -> p t h a", a=1), 3, O), ALU.mult).then_inc(v_step, 1)
                dve.wait_ge(v_step, vn.next())
                V.tensor_reduce(tmp[:, :, :], rowsg.rearrange("p t h o -> p t o h"), AX_X, ALU.add).then_inc(xg_used, 1)
                dve.wait_ge(xg_used, g + 1)
                y = x1[:, bass.ds(g * T7, T7), :]
                V.tensor_tensor(y.rearrange("p t (h o) -> p t h o", h=H), y.rearrange("p t (h o) -> p t h o", h=H),
                                spread(tmp[:, :, :].rearrange("p t (a o) -> p t a o", a=1), 2, H), ALU.add).then_inc(v_step, 1)
                dve.wait_ge(v_step, vn.next())
                V.nop(nofuse=True)
                for t in range(T7):
                    last = V.bn_stats(stats[:, t, :], x1[:, bass.ds(g * T7 + t, 1), :].rearrange("p a d -> p (a d)"))
                last.then_inc(v_step, 1)
                dve.wait_ge(v_step, vn.next())
                V.nop(nofuse=True)
                for t in range(T7):
                    last = V.bn_aggr(mv[:, h, t, :], stats[:, t, :])
                last.then_inc(v_step, 1)
                dve.wait_ge(v_step, vn.next())
                inverse_variance(h, var2_ready)

            dve.wait_ge(x1_kept, NT)
            for g in range(2):
                attend_group(0, g, g == 0)
            with nc.vector.Fori(1, NG7 // 2) as i:
                vn.loop(i - 1, 2 * 11)
                for h in range(2):
                    attend_group(i, h)
                vn.end(NG7 // 2 - 1)
            norm_bias(1, NG7 - 1, rstd2_ready, nb2_ready)

        @block.tensor
        def _(pe):
            T = nc.tensor

            def steps_of(b, g):
                _, tiles = nc.values_load_multi_w_load_instructions(
                    trow[0:1, bass.ds(b * B + g * G, G)], engines=[mybir.EngineType.PE], min_val=0, max_val=NT,
                    skip_runtime_bounds_check_because="the vector engine has clamped the node tile")
                return tiles

            pe.wait_ge(diag_ready, 1)
            for g in range(SG):
                last = T.matmul(psum[4 + g // 4][:, (g % 4) * P:(g % 4 + 1) * P], ones[:, :], diag[:, g * P:(g + 1) * P], start=True, stop=True)
                if g % 4 == 3 or g == SG - 1:
                    last.then_inc(bcast_ready, 1)

            def transpose_x(h, t, r):
                for c in range(DC):
                    last = T.transpose(psum[r][:, c * P:(c + 1) * P], xin[:, h, t, c * P:(c + 1) * P], ident[:, :])
                last.then_inc(xt_ps, 1)

            def project_half(g, h, q):
                t0, t1 = HALVES[q]
                if not (type(g) is int and g == 0):
                    pe.wait_ge(zf_copied, 2 * g + q - 1)
                pe.wait_ge(xt_copied, T7 * g + t1)
                for c in range(DC):
                    last = T.matmul(psum[2 + q][0:KR, 0:(t1 - t0) * P], ur[:, c, :, :].rearrange("p k r -> p (k r)"),
                                    xTb[:, h, t0:t1, c * P:(c + 1) * P], start=(c == 0), stop=(c == DC - 1))
                last.then_inc(zT_ps, 1)

            def turn_half(g, q):
                t0, t1 = HALVES[q]
                pe.wait_ge(zT_copied, 2 * g + q + 1)
                T.nop(nofuse=True)
                for t in range(t0, t1):
                    last = T.transpose(psum[2 + q][:, (t - t0) * KR:(t - t0 + 1) * KR], zT[:, t * P:(t + 1) * P], ident[0:KR, 0:KR])
                last.then_inc(zf_ps, 1)

            def project(i, first, last_one, between=None):
                for h in range(2):
                    if h == 1 and between is not None:
                        between()
                    g = 2 * i + h
                    pe.wait_ge(x_in[h], 16 * (i + 1) + (16 if last_one and h == 1 else 0))
                    for t in range(T7):
                        if t >= 2 or not (first and h == 0):
                            pe.wait_ge(xt_copied, T7 * g + t - 1)
                        transpose_x(h, t, (h + t) % 2)
                        if not (first and h == 0):
                            if t == 1:
                                turn_half(g - 1, 0)
                            if t == 2:
                                project_half(g - 1, 1 - h, 1)
                            if t == 4:
                                turn_half(g - 1, 1)
                        if t == T7 - 1:
                            project_half(g, h, 0)

            pe.wait_ge(consts, 1)
            pe.wait_ge(u_in, 16 * DC)
            project(0, True, False)
            with nc.tensor.Fori(1, 3) as i:
                project(i, False, False)

            pe.wait_ge(weights_in, 16 * 5)
            pe.wait_ge(walk_ready, 1)
            T.matmul(psum[7][:, :], ones[0:1, :], attn[0:1, :], start=True, stop=True)
            for a in range(DC):
                for c in range(DC):
                    T.matmul(psum[4][:, a * D:(a + 1) * D], dm[:, c, a * P:(a + 1) * P], dm[:, c, :], start=(c == 0), stop=(c == DC - 1))
            pe.wait_ge(prep_read, 2)
            T.matmul(psum[5][:, 0:K], ones[0:1, :], hw[0:1, 1, :], start=True, stop=True).then_inc(prep_ps, 1)
            project(3, False, False)
            pe.wait_ge(prep_read, 3)
            for a in range(DC):
                for c in range(DC):
                    last = T.matmul(psum[6][:, a * D:(a + 1) * D], gs[:, c, a * P:(a + 1) * P], dm[:, c, :], start=(c == 0), stop=(c == DC - 1))
            last.then_inc(prep_ps, 1)
            def transpose_table(n, table):
                pe.wait_ge(tab_read, n + 1)
                for g in range(SG):
                    last = T.transpose(psum[4 + g // 4][:, (g % 4) * P:(g % 4 + 1) * P], table[:, g, :], ident[:, :])
                last.then_inc(tab_ps, 1)

            def fold_and_slots():
                pe.wait_ge(prep_read, 5)
                for c in range(DC):
                    last = T.matmul(psum[4][0:KR, 0:D], wur[:, c, :, :].rearrange("p k r -> p (k r)"), mz[:, c, :], start=(c == 0), stop=(c == DC - 1))
                last.then_inc(prep_ps, 1)
                pe.wait_ge(prep_read, 6)
                pe.wait_ge(dloc_ready, 2)
                T.matmul(psum[7][:, 0:SG], shift[:, :], lastcol[:, 1:SG + 1], start=True, stop=False)
                T.matmul(psum[7][:, 0:SG], corner[:, :], lastcol[:, 0:SG], start=False, stop=True).then_inc(plast_ready, 1)
                transpose_table(0, dloc)

            project(4, False, False)

            def tiles_by_step():
                pe.wait_ge(tab_read, 3)
                for g in range(SG):
                    last = T.matmul(psum[4 + g // 4][0:1, (g % 4) * P:(g % 4 + 1) * P], tstep[:, g:g + 1], ident[:, :], start=True, stop=True)
                last.then_inc(tab_ps, 1)

            project(5, False, False, fold_and_slots)
            transpose_table(1, srcf)
            project(6, False, True, tiles_by_step)
            turn_half(NG7 - 1, 0)
            project_half(NG7 - 1, 1, 1)
            turn_half(NG7 - 1, 1)

            pe.wait_ge(keeprow_ready, 1)
            for n in range(0, S, 512):
                m = min(512, S - n)
                T.matmul(psum[4 + n // 512][:, 0:m], ones[0:1, :], keeprow[0:1, n:n + m], start=True, stop=True).then_inc(bcast_ready, 1)
            pe.wait_ge(tab_read, 7)
            T.transpose(psum[4][:, 0:P], okrow[:, 0, :], ident[:, :])
            T.transpose(psum[4][:, P:2 * P], okrow[:, 1, :], ident[:, :]).then_inc(tab_ps, 1)


            def transpose_onehots(b, h, g):
                if g >= 2 or not (type(b) is int and b == 0):
                    pe.wait_ge(oneT_ready, NG * b + g - 1)
                pe.wait_ge(onehot_ready, NG * b + g + 1)
                for u in range(G):
                    last = T.transpose(tr_ps[g % 2][:, u * P:(u + 1) * P], onehot[:, h, g * G + u, :], ident_b[:, :])
                last.then_inc(oneT_ps, 1)

            def expand(b, g):
                tiles = steps_of(b, g)
                if g >= 2 or not (type(b) is int and b == 0):
                    pe.wait_ge(zd_used, NG * b + g - 1)
                pe.wait_ge(oneT_ready, NG * b + g + 1)
                for u in range(G):
                    for s in range(ZP):
                        last = T.matmul(zd_ps[g % 2][:, u * KR:(u + 1) * KR], onehotT[:, g * G + u, :],
                                        z3[:, bass.ds(tiles[u], 1), s, :].rearrange("p a c -> p (a c)"), start=(s == 0), stop=(s == ZP - 1))
                last.then_inc(zd_ready, 1)

            def add_up(b, h, q0, q1):
                for q in range(q0, q1):
                    if q >= 2 or not (type(b) is int and b == 0):
                        pe.wait_ge(sums_copied, (B // Q) * b + q - 1)
                    if q % 2 == 0:
                        pe.wait_ge(parts_ready, NG * b + q // 2 + 1)
                    for u in range(q * Q, (q + 1) * Q):
                        for s in range(ZP):
                            last = T.matmul(sum_ps[q % 2][:, (u % Q) * AW:(u % Q + 1) * AW], onehot[:, h, u, :], wparts[:, u, s, :],
                                            start=(s == 0), stop=(s == ZP - 1))
                    last.then_inc(sums_ps, 1)

            def period(b, h, more=True, dense=True):
                def next_transposes(g):
                    if more:
                        transpose_onehots(b + 1, 1 - h, g)

                def multiply_x(t):
                    for c in range(DC):
                        last = T.matmul(zd_ps[1][:, t * D:(t + 1) * D], dspace[:, 1, t, c * P:(c + 1) * P], mz[:, c, :],
                                        start=(c == 0), stop=(c == DC - 1))
                    if t == YT - 1:
                        last.then_inc(xmz_ps, 1)
                pe.wait_ge(logits_ready, b + 1)
                T.transpose(mid_ps[:, 0:P], logits[:, h, :], ident[:, :]).then_inc(lt_ready, 1)
                pe.wait_ge(ends_ready, b + 1)
                T.matmul(row_ps[0:1, 0:P], fwd0[:, P - 1:P], ident[:, :], start=True, stop=True)
                T.matmul(row_ps[0:1, P:2 * P], inmin[:, :], ident[:, :], start=True, stop=True)
                T.matmul(row_ps[0:1, 2 * P:3 * P], resets[:, h, 0:1], ident[:, :], start=True, stop=True).then_inc(ends_row, 1)
                next_transposes(0)
                if dense:
                    pe.wait_ge(xe_in, 16 * b)
                    T.nop(nofuse=True)
                    for t in range(YT):
                        for c in range(DC):
                            last = T.transpose(zd_ps[0][:, t * D + c * P:t * D + (c + 1) * P], dspace[:, 0, t, c * P:(c + 1) * P], ident[:, :])
                    last.then_inc(xe_ps, 1)
                pe.wait_ge(carry_ready, b + 1)
                T.matmul(row_ps[:, 384:385], carry[0:1, 0:P], ones[0:1, 0:1], start=True, stop=True).then_inc(carry_col, 1)
                next_transposes(1)
                pe.wait_ge(heads_ready, b + 1)
                T.matmul(row_ps[0:1, 0:P], rev0[:, 0:1], ident[:, :], start=True, stop=True).then_inc(heads_row, 1)
                next_transposes(2)
                pe.wait_ge(back_ready, b + 1)
                T.matmul(row_ps[:, 385:386], backx[0:1, :], ones[0:1, 0:1], start=True, stop=True).then_inc(back_col, 1)
                next_transposes(3)
                if dense:
                    pe.wait_ge(xe_copied, b)
                    multiply_x(0)
                pe.wait_ge(e_ready, b + 1)
                T.transpose(mid_ps[:, 0:P], eexp, ident[:, :]).then_inc(et_ready, 1)
                pe.wait_ge(ratio_ready, b + 1)
                T.matmul(row_ps[:, 386:386 + K], ones[0:1, :], ratio[0:1, 1, :], start=True, stop=True).then_inc(scale_ready, 1)
                if dense:
                    multiply_x(1)
                if more:
                    expand(b + 1, 0)
                    if dense:
                        pe.wait_ge(xmz_copied, b)
                    expand(b + 1, 1)
                add_up(b, h, 0, 2)
                if more:
                    expand(b + 1, 2)
                add_up(b, h, 2, 4)
                if more:
                    expand(b + 1, 3)
                add_up(b, h, 4, 8)

            for g in range(NG):
                transpose_onehots(0, 0, g)
            pe.wait_ge(z_rest, 4)
            for g in range(NG):
                expand(0, g)
            period(0, 0, dense=False)
            period(1, 1)
            with nc.tensor.Fori(1, NB // 2 - 1) as i:
                for h in range(2):
                    period(2 * i + h, h)
            period(NB - 2, 0, dense=False)
            period(NB - 1, 1, more=False, dense=False)

            def dense_tile(g, h, t, first):
                n = g * T7 + t
                r = (h + t) % 2
                if t >= 2 or not first:
                    pe.wait_ge(y_summed, n - 1)
                if t % 4 == 0:
                    pe.wait_ge(aT_ready, 2 * g + t // 4 + 1)
                T.matmul(psum[2 + r][:, 0:D], aT[h][:, t * P:(t + 1) * P], w3[:, :], start=True, stop=True).then_inc(y_ps, 1)

            def transpose_sums(j, h):
                pe.wait_ge(agn_ready, j + 1)
                if not (type(j) is int and j == 0):
                    pe.wait_ge(aT_ready, 2 * j)
                T.nop(nofuse=True)
                for t in range(T7):
                    last = T.transpose(psum[t // 4][0:KR, (t % 4) * P:(t % 4 + 1) * P], agn[:, h, t, :], ident[:, :])
                    if t in (3, T7 - 1):
                        last.then_inc(aT_ps, 1)

            def transpose_x1(h, t, r):
                for c in range(DC):
                    last = T.transpose(psum[4 + r][:, c * P:(c + 1) * P], xn[:, t % RING, c * P:(c + 1) * P], ident[:, :])
                last.then_inc(x1T_ps, 1)

            def table_tile(g, h, t, first):
                n = g * T7 + t
                r = (h + t) % 2
                if t == 0:
                    pe.wait_ge(x1_ready, n + 1)
                    transpose_x1(h, 0, r)
                if t + 1 < T7:
                    pe.wait_ge(x1_ready, n + 2)
                    transpose_x1(h, t + 1, 1 - r)
                if t >= 2 or not first:
                    pe.wait_ge(xt1_copied, n - 1)
                pe.wait_ge(x1T_ready, n + 1)
                for c in range(DC):
                    last = T.matmul(psum[6 + r][:, 0:WW], x1T[:, r, c * P:(c + 1) * P], wx[:, c, :], start=(c == 0), stop=(c == DC - 1))
                last.then_inc(xt1_ps, 1)

            def stage(j, h, dense, tables, next_sums=True):
                if dense:
                    for t in range(DENSE_FIRST):
                        dense_tile(j, h, t, not tables)
                for t in range(T7):
                    if tables:
                        table_tile(j - 1, 1 - h, t, type(j) is int and j == 1)
                    if dense:
                        for d in range(DENSE_FIRST * (t + 1), min(DENSE_FIRST * (t + 2), T7)):
                            dense_tile(j, h, d, not tables)
                    if dense and next_sums and t == T7 // 2:
                        transpose_sums(j + 1, 1 - h)

            transpose_sums(0, 0)
            stage(0, 0, True, False)
            stage(1, 1, True, True)
            with nc.tensor.Fori(1, NG7 // 2 - 1) as i:
                for h in range(2):
                    stage(2 * i + h, h, True, True)
            stage(NG7 - 2, 0, True, True)
            stage(NG7 - 1, 1, True, True, next_sums=False)
            stage(NG7, 0, False, True)

        @block.scalar
        def _(act):
            A = nc.scalar

            def copy_zT(g, q):
                t0, t1 = HALVES[q]
                act.wait_ge(zT_ps, 2 * g + q + 1)
                if not (type(g) is int and g == 0):
                    act.wait_ge(zf_ps, 2 * g + q - 1)
                A.activation(zT[:, t0 * P:t1 * P], psum[2 + q][0:KR, 0:(t1 - t0) * P], ACT.Copy).then_inc(zT_copied, 1)

            def copy_z(g, q):
                t0, t1 = HALVES[q]
                act.wait_ge(zf_ps, 2 * g + q + 1)
                A.activation(zf[:, bass.ds(g * T7 + t0, t1 - t0), :].rearrange("p t c -> p (t c)"), psum[2 + q][:, 0:(t1 - t0) * KR],
                             ACT.Copy).then_inc(zf_copied, 1)

            def project(i, first):
                for h in range(2):
                    g = 2 * i + h
                    for t in range(T7):
                        act.wait_ge(xt_ps, T7 * g + t + 1)
                        A.activation(xTb[:, h, t, :], psum[(h + t) % 2][:, 0:D], ACT.Copy).then_inc(xt_copied, 1)
                        if not (first and h == 0):
                            if t == 1:
                                copy_z(g - 1, 0)
                            if t == 2:
                                copy_zT(g - 1, 1)
                            if t == 4:
                                copy_z(g - 1, 1)
                        if t == T7 - 1:
                            copy_zT(g, 0)
            project(0, True)
            with nc.scalar.Fori(1, 3) as i:
                project(i, False)
            act.wait_ge(prep_read, 1)
            A.activation(hw[0:1, 2, :], hw[0:1, 1, :], ACT.Exp).then_inc(prep_exp, 1)
            with nc.scalar.Fori(3, NG7 // 2) as i:
                project(i, False)
            copy_z(NG7 - 1, 0)
            copy_zT(NG7 - 1, 1)
            copy_z(NG7 - 1, 1)

            for s in range(2):
                for half in range(2):
                    ts = slice(half * NT // 2, (half + 1) * NT // 2)
                    if s == 1:
                        act.wait_ge(z_rest, half + 1)
                    else:
                        act.wait_ge(zf_copied, 2 * NG7)
                    A.activation(z3[:, ts, s, :], zf[:, ts, :], ACT.Copy).then_inc(z_parts, 1)

            def store_states(b, g):
                _, tiles = nc.values_load_multi_w_load_instructions(
                    arow[0:1, bass.ds(b * B + g * G, G)], engines=[mybir.EngineType.Activation], min_val=0, max_val=NT + NSPARE,
                    skip_runtime_bounds_check_because="the vector engine has clamped the node tile")
                if g == 0:
                    act.wait_ge(scan_done, b + 1)
                    if not (type(b) is int and b == 0):
                        act.wait_ge(state_stored, B * b)
                for u in range(g * G, (g + 1) * G):
                    if u >= NSPARE:
                        act.wait_ge(state_stored, B * b + u - NSPARE + 1)
                    A.activation(acc[:, bass.ds(tiles[u % G], 1), :].rearrange("p a c -> p (a c)"), state[:, :, 1 + u], ACT.Copy
                                 ).then_inc(state_stored, 1)

            def copy_onehots(b, h, g):
                if not (type(b) is int and b == 0):
                    act.wait_ge(zd_ready, NG * (b - 1) + g + 1)
                act.wait_ge(oneT_ps, NG * b + g + 1)
                if g == 0:
                    A.activation(first_col[:, h:h + 1], tr_ps[0][:, 0:1], ACT.Copy)
                A.activation(onehotT[:, g * G:(g + 1) * G, :].rearrange("p j e -> p (j e)"), tr_ps[g % 2][:, :], ACT.Copy).then_inc(oneT_ready, 1)

            def copy_keeps(b):
                A.activation(keepf[:, :, 1:B + 1], spread(keep[:, bass.ds(b * B, B)].rearrange("p (a j) -> p a j", a=1), 1, AW),
                             ACT.Copy).then_inc(keep_ready, 1)

            def copy_sums(b, first, last):
                if last:
                    act.wait_ge(scan_done, b)
                    copy_keeps(b)
                if not first:
                    act.wait_ge(scan_done, b)
                for q in range(B // Q):
                    act.wait_ge(sums_ps, (B // Q) * b + q + 1)
                    A.activation(sums[:, :, 1 + q * Q:1 + (q + 1) * Q].rearrange("p c j -> p j c"),
                                 sum_ps[q % 2][:, 0:Q * AW].rearrange("p (j c) -> p j c", c=AW), ACT.Copy).then_inc(sums_copied, 1)
                if not last:
                    copy_keeps(b)

            def period(b, h, more=True, dense=True):
                first = type(b) is int and b == 0
                states = not (type(b) is int and b < 2)
                if more:
                    copy_onehots(b + 1, 1 - h, 0)
                if dense:
                    act.wait_ge(xe_ps, b)
                    A.activation(dspace[:, 1, :, :].rearrange("p t d -> p (t d)"), zd_ps[0][:, :], ACT.Copy).then_inc(xe_copied, 1)
                if states:
                    store_states(b - 2, 2)
                if more:
                    copy_onehots(b + 1, 1 - h, 1)
                if states:
                    store_states(b - 2, 3)
                if more:
                    copy_onehots(b + 1, 1 - h, 2)
                act.wait_ge(x_ready, b + 1)
                A.activation(eexp, xexp, ACT.Exp, scale=float(R) ** -0.5).then_inc(e_ready, 1)
                A.activation(ratio[0:1, 1, :], ratio[0:1, 0, :], ACT.Exp, scale=float(R) ** -0.5).then_inc(ratio_ready, 1)
                if more:
                    copy_onehots(b + 1, 1 - h, 3)
                if dense:
                    act.wait_ge(xmz_ps, b)
                    if not (type(b) is int and b == 1):
                        act.wait_ge(xmz_out, 16 * (b - 1))
                    A.activation(xmz, zd_ps[1][:, :], ACT.Copy).then_inc(xmz_copied, 1)
                if not first:
                    act.wait_ge(sums_ps, (B // Q) * b)
                for s, made, rounded in ((0, weighted, hi_ready), (1, rest_ready, mid_ready)):
                    for g in range(NG):
                        js = slice(g * G, (g + 1) * G)
                        act.wait_ge(made, NG * b + g + 1)
                        A.activation(wparts[:, js, s, :], zs[:, h, js, :], ACT.Copy).then_inc(rounded, 1)
                copy_sums(b, first, not more)
                if not first and more:
                    store_states(b - 1, 0)
                    store_states(b - 1, 1)

            act.wait_ge(tab_read, 8)
            for g in range(NG):
                copy_onehots(0, 0, g)
            period(0, 0, dense=False)
            period(1, 1)
            with nc.scalar.Fori(1, NB // 2 - 1) as i:
                for h in range(2):
                    period(2 * i + h, h)
            period(NB - 2, 0, dense=False)
            period(NB - 1, 1, more=False, dense=False)
            for g in range(NG):
                store_states(NB - 1, g)

            def root(g, h, variance, ready):
                act.wait_ge(variance, g + 1)
                A.activation(rstd[:, h, :, 0], rstd[:, h, :, 2], ACT.Sqrt).then_inc(ready, 1)

            def norm_tile(g, h, t):
                n = g * T7 + t
                before = n - RING if t >= RING else n - T7 if t == T7 // 2 else n - (T7 - RING)
                if not (type(g) is int and g == 0 and t < RING):
                    act.wait_ge(x1_kept, before + 1)
                    act.wait_ge(x1T_ps, before + 1)
                A.activation(xn[:, t % RING, :], x1[:, bass.ds(n, 1), :].rearrange("p a d -> p (a d)"), ACT.Identity,
                             bias=rstd[:, h, t, 1:2], scale=rstd[:, h, t, 0:1]).then_inc(x1_ready, 1)

            def stage(g, h, reuse, more=True):
                act.wait_ge(nb_ready, g + 1)
                if reuse is not None:
                    act.wait_ge(table_out[h], 32 * reuse)
                for k in range(T7 + 2):
                    if k < T7:
                        norm_tile(g, h, k)
                    if 1 <= k <= T7:
                        t = k - 1
                        act.wait_ge(x1T_ps, g * T7 + t + 1)
                        if t >= 2 or not (type(g) is int and g == 0):
                            act.wait_ge(xt1_ps, g * T7 + t - 1)
                        A.activation(x1T[:, (h + t) % 2, :], psum[4 + (h + t) % 2][:, 0:D], ACT.Copy).then_inc(x1T_ready, 1)
                    if k >= 2:
                        t = k - 2
                        act.wait_ge(xt1_ps, g * T7 + t + 1)
                        A.activation(xto[:, h, t, :], psum[6 + (h + t) % 2][:, 0:WW], ACT.Copy).then_inc(xt1_copied, 1)
                    if k == T7 - 1 and more:
                        root(g + 1, 1 - h, var_ready, rstd_ready)

            root(0, 0, var_ready, rstd_ready)
            for g in range(4):
                stage(g, g % 2, 1 if g >= 2 else None)
            with nc.scalar.Fori(2, NG7 // 2 - 1) as i:
                for h in range(2):
                    stage(2 * i + h, h, i)
            stage(NG7 - 2, 0, NG7 // 2 - 1)
            stage(NG7 - 1, 1, NG7 // 2 - 1, more=False)

            def exp_logits(g, h):
                act.wait_ge(lg_ready, g + 1)
                A.activation(lg[:, h, :, :], lg[:, h, :, :], ACT.Exp).then_inc(lg_exp, 1)

            def finish_group(g, h):
                act.wait_ge(nb2_ready, g + 1)
                for t in range(T7):
                    y = x1[:, bass.ds(g * T7 + t, 1), :].rearrange("p a d -> p (a d)")
                    last = A.activation(y, y, ACT.Identity, bias=rstd[:, h, t, 1:2], scale=rstd[:, h, t, 0:1])
                last.then_inc(out_ready, 1)

            def next_group(g, h):
                root(g - 1, 1 - h, var2_ready, rstd2_ready)
                exp_logits(g, h)
                finish_group(g - 1, 1 - h)

            exp_logits(0, 0)
            next_group(1, 1)
            with nc.scalar.Fori(1, NG7 // 2) as i:
                for h in range(2):
                    next_group(2 * i + h, h)
            root(NG7 - 1, 1, var2_ready, rstd2_ready)
            finish_group(NG7 - 1, 1)


_INS = ["x", "src", "dst", "L0_gnn_U", "L0_gnn_Dmat", "L0_gnn_head_w", "L1_gnn_weight", "L1_gnn_attn_l", "L1_gnn_attn_r"]


def kernel(**inputs):
    import concourse.bacc as bacc
    from concourse.bass_utils import run_bass_kernel_spmd

    nc = bacc.Bacc("TRN2", target_bir_lowering=False, num_devices=1)
    arrays, args = {}, []
    for name in _INS:
        a = np.ascontiguousarray(inputs[name])
        arrays[f"in_{name}"] = a
        args.append(nc.dram_tensor(f"in_{name}", a.shape, mybir.dt.from_np(a.dtype), kind="ExternalInput").ap())
    out = nc.dram_tensor("out_0", (N, D), F32, kind="ExternalOutput").ap()
    program(nc, *args, out)
    r = run_bass_kernel_spmd(nc, [arrays], core_ids=[0])
    return r.results[0]["out_0"]
```
